# Optimizing a Trainium2 kernel written in Bass

```python
import numpy as np
import jax
import jax.numpy as jnp

def _softmax(x, axis=-1):
    return jax.nn.softmax(x, axis=axis)
def _gelu(x):
    return jax.nn.gelu(x, approximate=True)
def _silu(x):
    return jax.nn.silu(x)
def _sigmoid(x):
    return jax.nn.sigmoid(x)
def _layernorm(x, axis=-1, eps=1e-5):
    m = jnp.mean(x, axis=axis, keepdims=True)
    v = jnp.var(x, axis=axis, keepdims=True)
    return (x - m) / jnp.sqrt(v + eps)
def _scatter_add(tgt, idx, src, axis=0):
    return tgt.at[idx].add(src)
def _segment_sum(src, seg, n):
    return jax.ops.segment_sum(src, seg, n)

kernel_name = 'mk_conv_attn_hybrid_d2_conv_nhwc128_0202dc'

def setup_inputs(seed: int = 0):
    np.random.seed(seed)
    _w = jnp.asarray
    def _rec_inputs():
        import jax
        import jax.numpy as jnp
        _gk = jax.random.key(seed)
        x = 7.22e-05 + 1 * jax.random.normal(jax.random.fold_in(_gk, 1), (16, 64, 64, 128), jnp.float32)
        return x
    x = _rec_inputs()
    def _L0_conv_setup():
        import jax, jax.numpy as jnp
        import numpy as np
        B, D0, D1, F, U = (16, 64, 64, 128, 128)
        key = jax.random.key(seed)
        ks = jax.random.split(key, 11)
        std = 0.05
        x = jax.random.normal(ks[0], (B, D0, D1, F), jnp.float32)

        def gen(k):
            kw, ku = jax.random.split(k)
            w = jax.random.normal(kw, (F, U), jnp.float32) * std
            u = jax.random.normal(ku, (U, U), jnp.float32) * std
            b = jnp.zeros((U,), jnp.float32)
            return (w, u, b)
        wf0, uf0, bf0 = gen(ks[1])
        wf1, uf1, bf1 = gen(ks[2])
        wi, ui, bi = gen(ks[3])
        wo, uo, bo = gen(ks[4])
        wc, uc, bc = gen(ks[5])
        return dict(x=x, wf0=wf0, uf0=uf0, bf0=bf0, wf1=wf1, uf1=uf1, bf1=bf1, wi=wi, ui=ui, bi=bi, wo=wo, uo=uo, bo=bo, wc=wc, uc=uc, bc=bc)
    _L0_conv_all = _L0_conv_setup()
    _L0_conv_in = {k: v for k, v in _L0_conv_all.items() if k in ('wf0', 'uf0', 'bf0', 'wf1', 'uf1', 'bf1', 'wi', 'ui', 'bi', 'wo', 'uo', 'bo', 'wc', 'uc', 'bc', )}
    del _L0_conv_all

    def _L1_attn_setup():
        import jax, jax.numpy as jnp
        import numpy as np
        HEADS = 8
        DIM = 128
        DIM_HEAD = 16
        LANDMARKS = 64
        PINV_ITERS = 6
        KS = 33
        LN_EPS = 1e-05

        def moore_penrose_pinv(x, iters=PINV_ITERS):
            abs_x = jnp.abs(x)
            col = abs_x.sum(axis=-1).max()
            row = abs_x.sum(axis=-2).max()
            z = jnp.swapaxes(x, -1, -2) / (col * row)
            I = jnp.eye(x.shape[-1], dtype=x.dtype)
            for _ in range(iters):
                xz = x @ z
                z = 0.25 * z @ (13.0 * I - xz @ (15.0 * I - xz @ (7.0 * I - xz)))
            return z
        key = jax.random.key(seed)
        ks = jax.random.split(key, 4)
        b, n, d = (8, 8192, DIM)
        x = jax.random.normal(ks[0], (b, n, d), dtype=jnp.float32)
        gamma = jnp.ones((d,), jnp.float32)
        beta = jnp.zeros((d,), jnp.float32)
        w_qkv = jax.random.normal(ks[1], (d, 3 * HEADS * DIM_HEAD), jnp.float32) * d ** (-0.5)
        w_out = jax.random.normal(ks[2], (HEADS * DIM_HEAD, d), jnp.float32) * (HEADS * DIM_HEAD) ** (-0.5)
        b_out = jnp.zeros((d,), jnp.float32)
        conv_w = jax.random.normal(ks[3], (HEADS, 1, KS, 1), jnp.float32) * KS ** (-0.5)
        return {'x': x, 'gamma': gamma, 'beta': beta, 'w_qkv': w_qkv, 'w_out': w_out, 'b_out': b_out, 'conv_w': conv_w}
    _L1_attn_all = _L1_attn_setup()
    _L1_attn_in = {k: v for k, v in _L1_attn_all.items() if k in ('gamma', 'beta', 'w_qkv', 'w_out', 'b_out', 'conv_w', )}
    del _L1_attn_all

    def _L1_ffn_setup():
        import jax, jax.numpy as jnp
        import numpy as np
        BN_EPS = 1e-05
        key = jax.random.key(seed)
        k1, k2, k3 = jax.random.split(key, 3)
        B, T, I, H = (64, 2048, 128, 128)
        x = jax.random.normal(k1, (B, T, I), dtype=jnp.float32)
        W = jax.random.normal(k2, (H, I), dtype=jnp.float32) * (1.0 / np.sqrt(I))
        V = jnp.linalg.qr(jax.random.normal(k3, (H, H), dtype=jnp.float32))[0]
        gamma = jnp.ones((H,), dtype=jnp.float32)
        beta = jnp.zeros((H,), dtype=jnp.float32)
        return {'x': x, 'W': W, 'V': V, 'gamma': gamma, 'beta': beta}
    _L1_ffn_all = _L1_ffn_setup()
    _L1_ffn_in = {k: v for k, v in _L1_ffn_all.items() if k in ('W', 'V', 'gamma', 'beta', )}
    del _L1_ffn_all

    return {
        "x": x,
        "L0_conv_wf0": _L0_conv_in["wf0"],
        "L0_conv_uf0": _L0_conv_in["uf0"],
        "L0_conv_bf0": _L0_conv_in["bf0"],
        "L0_conv_wf1": _L0_conv_in["wf1"],
        "L0_conv_uf1": _L0_conv_in["uf1"],
        "L0_conv_bf1": _L0_conv_in["bf1"],
        "L0_conv_wi": _L0_conv_in["wi"],
        "L0_conv_ui": _L0_conv_in["ui"],
        "L0_conv_bi": _L0_conv_in["bi"],
        "L0_conv_wo": _L0_conv_in["wo"],
        "L0_conv_uo": _L0_conv_in["uo"],
        "L0_conv_bo": _L0_conv_in["bo"],
        "L0_conv_wc": _L0_conv_in["wc"],
        "L0_conv_uc": _L0_conv_in["uc"],
        "L0_conv_bc": _L0_conv_in["bc"],
        "L1_attn_gamma": _L1_attn_in["gamma"],
        "L1_attn_beta": _L1_attn_in["beta"],
        "L1_attn_w_qkv": _L1_attn_in["w_qkv"],
        "L1_attn_w_out": _L1_attn_in["w_out"],
        "L1_attn_b_out": _L1_attn_in["b_out"],
        "L1_attn_conv_w": _L1_attn_in["conv_w"],
        "L1_ffn_W": _L1_ffn_in["W"],
        "L1_ffn_V": _L1_ffn_in["V"],
        "L1_ffn_gamma": _L1_ffn_in["gamma"],
        "L1_ffn_beta": _L1_ffn_in["beta"],
    }

def reference(x, L0_conv_wf0, L0_conv_uf0, L0_conv_bf0, L0_conv_wf1, L0_conv_uf1, L0_conv_bf1, L0_conv_wi, L0_conv_ui, L0_conv_bi, L0_conv_wo, L0_conv_uo, L0_conv_bo, L0_conv_wc, L0_conv_uc, L0_conv_bc, L1_attn_gamma, L1_attn_beta, L1_attn_w_qkv, L1_attn_w_out, L1_attn_b_out, L1_attn_conv_w, L1_ffn_W, L1_ffn_V, L1_ffn_gamma, L1_ffn_beta):
    import jax
    import jax.numpy as jnp
    def _L0_conv_ref(x, wf0, uf0, bf0, wf1, uf1, bf1, wi, ui, bi, wo, uo, bo, wc, uc, bc):
        import jax, jax.numpy as jnp
        import numpy as np
        B, D0, D1, F, U = (16, 64, 64, 128, 128)
        b, d0, d1, _ = x.shape
        u_dim = uf0.shape[0]

        def proj(w, bias):
            return jnp.einsum('bijf,fu->ijbu', x, w) + bias
        xf0, xf1, xi, xo, xc = (proj(wf0, bf0), proj(wf1, bf1), proj(wi, bi), proj(wo, bo), proj(wc, bc))

        def col_step(carry, cols):
            h_l, c_l = carry
            pf0, pf1, pi, po, pc, h_u, c_u = cols
            f0 = jax.nn.sigmoid(pf0 + h_u @ uf0)
            f1 = jax.nn.sigmoid(pf1 + h_l @ uf1)
            hsum = h_u + h_l
            it = jax.nn.sigmoid(pi + hsum @ ui)
            ot = jax.nn.sigmoid(po + hsum @ uo)
            cp = jnp.tanh(pc + hsum @ uc)
            c = f0 * c_u + f1 * c_l + it * cp
            h = ot * jnp.tanh(c)
            return ((h, c), (h, c))

        def row_step(carry, xs):
            h_up, c_up = carry
            rf0, rf1, ri, ro, rc = xs
            init = (jnp.zeros((b, u_dim), x.dtype), jnp.zeros((b, u_dim), x.dtype))
            _, (h_row, c_row) = jax.lax.scan(col_step, init, (rf0, rf1, ri, ro, rc, h_up, c_up))
            return ((h_row, c_row), h_row)
        init = (jnp.zeros((d1, b, u_dim), x.dtype), jnp.zeros((d1, b, u_dim), x.dtype))
        _, h_all = jax.lax.scan(row_step, init, (xf0, xf1, xi, xo, xc))
        return jnp.transpose(h_all, (2, 0, 1, 3))

    def _L1_attn_ref(x, gamma, beta, w_qkv, w_out, b_out, conv_w):
        import jax, jax.numpy as jnp
        import numpy as np
        HEADS = 8
        DIM = 128
        DIM_HEAD = 16
        LANDMARKS = 64
        PINV_ITERS = 6
        KS = 33
        LN_EPS = 1e-05

        def moore_penrose_pinv(x, iters=PINV_ITERS):
            abs_x = jnp.abs(x)
            col = abs_x.sum(axis=-1).max()
            row = abs_x.sum(axis=-2).max()
            z = jnp.swapaxes(x, -1, -2) / (col * row)
            I = jnp.eye(x.shape[-1], dtype=x.dtype)
            for _ in range(iters):
                xz = x @ z
                z = 0.25 * z @ (13.0 * I - xz @ (15.0 * I - xz @ (7.0 * I - xz)))
            return z
        b, n, d = x.shape
        h, m, dh = (HEADS, LANDMARKS, DIM_HEAD)
        mu = x.mean(-1, keepdims=True)
        var = ((x - mu) ** 2).mean(-1, keepdims=True)
        xn = (x - mu) * jax.lax.rsqrt(var + LN_EPS) * gamma + beta
        qkv = xn @ w_qkv
        q, k, v = jnp.split(qkv, 3, axis=-1)
        to_heads = lambda t: t.reshape(b, n, h, dh).transpose(0, 2, 1, 3)
        q, k, v = (to_heads(q), to_heads(k), to_heads(v))
        q = q * dh ** (-0.5)
        l = n // m
        q_l = q.reshape(b, h, m, l, dh).mean(axis=3)
        k_l = k.reshape(b, h, m, l, dh).mean(axis=3)
        sim1 = jnp.einsum('bhid,bhjd->bhij', q, k_l)
        sim2 = jnp.einsum('bhid,bhjd->bhij', q_l, k_l)
        sim3 = jnp.einsum('bhid,bhjd->bhij', q_l, k)
        attn1 = jax.nn.softmax(sim1, axis=-1)
        attn2 = jax.nn.softmax(sim2, axis=-1)
        attn3 = jax.nn.softmax(sim3, axis=-1)
        attn2_inv = moore_penrose_pinv(attn2)
        out = attn1 @ attn2_inv @ (attn3 @ v)
        res = jax.lax.conv_general_dilated(v, conv_w, window_strides=(1, 1), padding=((KS // 2, KS // 2), (0, 0)), dimension_numbers=('NCHW', 'OIHW', 'NCHW'), feature_group_count=h)
        out = out + res
        out = out.transpose(0, 2, 1, 3).reshape(b, n, h * dh)
        out = out @ w_out + b_out
        return x + out

    def _L1_ffn_ref(x, W, V, gamma, beta):
        import jax, jax.numpy as jnp
        import numpy as np
        BN_EPS = 1e-05
        B, T, H = (x.shape[0], x.shape[1], W.shape[0])
        Wx = jnp.einsum('bti,hi->bth', x, W)
        flat = Wx.reshape(B * T, H)
        mean = jnp.mean(flat, axis=0)
        var = jnp.var(flat, axis=0)
        Wx = ((flat - mean) * jax.lax.rsqrt(var + BN_EPS) * gamma + beta).reshape(B, T, H)
        Vt = V.T

        def step(yt, wx_t):
            yt = jax.nn.sigmoid(wx_t + yt @ Vt)
            return (yt, yt)
        y0 = jnp.zeros((B, H), dtype=Wx.dtype)
        _, ys = jax.lax.scan(step, y0, jnp.swapaxes(Wx, 0, 1))
        return jnp.swapaxes(ys, 0, 1)

    def _gn(v, G=32, eps=1e-5):
        B_, H_, W_, C_ = v.shape
        g = v.reshape(B_, H_, W_, G, C_ // G)
        m = jnp.mean(g, axis=(1, 2, 4), keepdims=True)
        s = jnp.var(g, axis=(1, 2, 4), keepdims=True)
        return ((g - m) / jnp.sqrt(s + eps)).reshape(v.shape)

    def _ln_c(v, eps=1e-6):
        m = jnp.mean(v, axis=-1, keepdims=True)
        s = jnp.var(v, axis=-1, keepdims=True)
        return (v - m) / jnp.sqrt(s + eps)

    def _ln_t(v, eps=1e-5):
        m = jnp.mean(v, axis=-1, keepdims=True)
        s = jnp.var(v, axis=-1, keepdims=True)
        return (v - m) / jnp.sqrt(s + eps)

    def _to_tokens(v):
        B_, H_, W_, C_ = v.shape
        return v.reshape(B_, H_ * W_, C_)
    def _from_tokens(t, like):
        return t.reshape(like.shape)

    x = x + _L0_conv_ref(_gn(x), L0_conv_wf0, L0_conv_uf0, L0_conv_bf0, L0_conv_wf1, L0_conv_uf1, L0_conv_bf1, L0_conv_wi, L0_conv_ui, L0_conv_bi, L0_conv_wo, L0_conv_uo, L0_conv_bo, L0_conv_wc, L0_conv_uc, L0_conv_bc)
    t = _to_tokens(x)
    t = t + _L1_attn_ref(_ln_t(t), L1_attn_gamma, L1_attn_beta, L1_attn_w_qkv, L1_attn_w_out, L1_attn_b_out, L1_attn_conv_w)
    t = t + _L1_ffn_ref(_ln_t(t), L1_ffn_W, L1_ffn_V, L1_ffn_gamma, L1_ffn_beta)
    x = _from_tokens(t, x)
    return x


_drawn_inputs = setup_inputs


def setup_inputs(seed=0):
    import zlib

    import numpy as np

    out = dict(_drawn_inputs(seed))
    spreads = {'L0_conv_bf0': (0.0, 0.1),
     'L0_conv_bf1': (0.0, 0.1),
     'L0_conv_bi': (0.0, 0.1),
     'L0_conv_bo': (0.0, 0.1),
     'L0_conv_bc': (0.0, 0.1),
     'L1_attn_gamma': (1.0, 0.2),
     'L1_attn_beta': (0.0, 0.1),
     'L1_attn_b_out': (0.0, 0.1),
     'L1_ffn_gamma': (1.0, 0.6),
     'L1_ffn_beta': (0.0, 0.8)}
    factors = {}
    for name, (base, spread) in spreads.items():
        noise = np.random.default_rng([zlib.crc32(name.encode()), seed]).standard_normal(out[name].shape)
        drawn = base * np.exp(spread * noise) if base else spread * noise
        out[name] = jnp.asarray(drawn.astype(out[name].dtype))
    for name, factor in factors.items():
        out[name] = (out[name] * factor).astype(out[name].dtype)
    return out
```

```python
from contextlib import ExitStack

import concourse.bass as bass
from concourse import mybir

F32 = mybir.dt.float32
BF16 = mybir.dt.bfloat16
ALU = mybir.AluOpType
ACT = mybir.ActivationFunctionType
AX = mybir.AxisListType

P = 128
B = 16
G = 64
C = 128
TOK = G * G
NT = TOK // P
SETS = 2
LANES = B // SETS
CHAINS = 2
LPC = LANES // CHAINS
PERIOD = G + 1
WIN = 8
STEPS = 192
SLOT = G + 1
GN_GROUP = 4
EPS = 1e-5


class Memory:

    def __init__(self, nc, ctx):
        self.nc, self.ctx = nc, ctx

    def sb(self, name, shape, dt=F32):
        return self.ctx.enter_context(self.nc.sbuf_tensor(name, shape, dt))

    def ps(self, name, shape, dt=F32):
        return self.ctx.enter_context(self.nc.psum_tensor(name, shape, dt))

    def sem(self, name):
        return self.ctx.enter_context(self.nc.semaphore(name))


def strided(start, dims):
    return bass.AP(tensor=start.tensor, offset=start.offset, ap=[start.ap[0], *dims])


def make_identity(pool, ident, sem):
    pool.memset(ident[:, :], 0.0).then_inc(sem, 1)
    pool.wait_ge(sem, 1)
    pool.affine_select(out=ident[:, :], in_=ident[:, :], compare_op=ALU.not_equal, fill=1.0,
                       base=0, pattern=[[-1, P]], channel_multiplier=1).then_inc(sem, 1)


def group_norm_phase(nc, sems, x, skew):
    with ExitStack() as ctx:
        m = Memory(nc, ctx)
        xin = [m.sb(f"gn_x{s}", [P, NT, C]) for s in range(SETS)]
        D = [m.sb(f"gn_skew{q}", [P, STEPS * G]) for q in range(2)]
        ident = m.sb("gn_ident", [P, P])
        avg = m.sb("gn_avg", [P, P])
        stats = m.sb("gn_stats", [P, 8, 6])
        mv = m.sb("gn_mv", [P, 2])
        gmean = m.sb("gn_gmean", [P, 1])
        dev = m.sb("gn_dev", [P, 1])
        spread = m.sb("gn_spread", [P, 1])
        veps = m.sb("gn_veps", [P, 1])
        rstd = m.sb("gn_rstd", [P, 1])
        minus_half = m.sb("gn_minus_half", [P, 1])
        shift = m.sb("gn_shift", [P, 1])
        turned = [m.ps(f"gn_turned{k}", [P, 4, P]) for k in range(4)]
        group = m.ps("gn_group", [P, 512])

        s_const = sems.sem("gn_const")
        s_avg = sems.sem("gn_avg")
        s_clear = sems.sem("gn_clear")
        s_load = [sems.sem(f"gn_load{s}") for s in range(SETS)]
        s_turned = sems.sem("gn_turned")
        s_copied = sems.sem("gn_copied")
        s_vec = sems.sem("gn_vec")
        s_group = sems.sem("gn_group")
        s_rstd = sems.sem("gn_rstd")
        s_store = [sems.sem(f"gn_store{q}") for q in range(2)]
        VS = 9 + 6

        def chunk(q, s, k):
            return strided(D[q][:, (PERIOD * s + 4 * k) * G:(PERIOD * s + 4 * k) * G + 1],
                           [[G, 4], [G + 1, G], [G * NT, 2]])

        def image(q, s):
            return strided(D[q][:, PERIOD * s * G:PERIOD * s * G + 1], [[G + 1, G], [G, G]])

        block = ctx.enter_context(nc.Block())

        @block.sync
        def _(sp):
            def load(q, s, it):
                sp.dma_start(xin[s][:, :, :], x[8 * s + 2 * it + q].rearrange("(p n) c -> p n c", n=NT)
                             ).then_inc(s_load[s], 16)

            with sp.Fori(0, LANES // 2) as it:
                for q in range(2):
                    for s in range(SETS):
                        sp.wait_ge(s_turned, 32 * it + 16 * q + 8 * s + 8)
                        load(q, s, it)

        @block.gpsimd
        def _(pool):
            make_identity(pool, ident, s_const)
            pool.memset(avg[:, :], 1.0 / GN_GROUP).then_inc(s_avg, 1)
            pool.wait_ge(s_avg, 1)
            v = avg[:, :].rearrange("p (g k) -> p g k", k=GN_GROUP)
            pool.affine_select(out=v, in_=v, compare_op=ALU.is_ge, fill=0.0, base=0,
                               pattern=[[-GN_GROUP, P // GN_GROUP], [0, GN_GROUP]],
                               channel_multiplier=1).then_inc(s_avg, 1)
            pool.wait_ge(s_avg, 2)
            pool.affine_select(out=v, in_=v, compare_op=ALU.is_ge, fill=0.0, base=GN_GROUP - 1,
                               pattern=[[GN_GROUP, P // GN_GROUP], [0, GN_GROUP]],
                               channel_multiplier=-1).then_inc(s_avg, 1)
            for q in range(2):
                pool.memset(D[q][:, :], 0.0).then_inc(s_clear, 1)
            pool.wait_ge(s_clear, 2)
            for q in range(2):
                pool.dma_start(skew[q, 0:1, 0:1], D[q][0:1, 0:1]).then_inc(s_store[q], 16)
            pool.memset(minus_half[:, :], -0.5).then_inc(s_avg, 1)
            pool.wait_ge(s_avg, 4)
            with pool.Fori(0, LANES // 2) as it:
                for q in range(2):
                    for s in range(SETS):
                        k = 4 * it + 2 * q + s
                        pool.wait_ge(s_vec, VS * k + 13)
                        pool.tensor_tensor(rstd[:, :], veps[:, :], minus_half[:, :], ALU.pow).then_inc(s_rstd, 1)
                    pool.wait_ge(s_vec, VS * (4 * it + 2 * q + 2))
                    pool.dma_start(skew[2 * it + q], D[q][:, :]).then_inc(s_store[q], 16)
            for q in range(2):
                pool.wait_ge(s_store[q], 16 * (LANES // 2 + 1))

        @block.tensor
        def _(pe):
            pe.sem_inc(s_turned, 16)
            pe.wait_ge(s_const, 2)
            pe.wait_ge(s_avg, 3)
            with pe.Fori(0, LANES // 2) as it:
                for q in range(2):
                    for s in range(SETS):
                        k = 4 * it + 2 * q + s
                        pe.wait_ge(s_load[s], 16 * (2 * it + q + 1))
                        for g in range(8):
                            pe.wait_ge(s_copied, 8 * k + g + 1)
                            for n in range(4):
                                last = nc.tensor.transpose(turned[g % 4][:, n, :], xin[s][:, 4 * g + n, :], ident[:, :])
                            last.then_inc(s_turned, 1)
                        pe.wait_ge(s_vec, VS * k + 9)
                        nc.tensor.matmul(group[:, 0:1], avg[:, :], mv[:, 0:1], start=True, stop=True).then_inc(s_group, 1)
                        pe.wait_ge(s_vec, VS * k + 12)
                        nc.tensor.matmul(group[:, 0:1], avg[:, :], spread[:, :], start=True, stop=True).then_inc(s_group, 1)

        @block.scalar
        def _(act):
            act.sem_inc(s_copied, 4)
            act.wait_ge(s_clear, 2)
            with act.Fori(0, LANES // 2) as it:
                for q in range(2):
                    act.wait_ge(s_store[q], 16 * it + 16)
                    for s in range(SETS):
                        k = 4 * it + 2 * q + s
                        for g in range(8):
                            act.wait_ge(s_turned, 16 + 8 * k + g + 1)
                            nc.scalar.copy(chunk(q, s, g), turned[g % 4][:, :, :].rearrange("c n (i h) -> c n i h", h=2)).then_inc(s_copied, 1)

        @block.vector
        def _(dve):
            with dve.Fori(0, LANES // 2) as it:
                for q in range(2):
                    for s in range(SETS):
                        k = 4 * it + 2 * q + s
                        for g in range(8):
                            dve.wait_ge(s_copied, 4 + 8 * k + g + 1)
                            nc.vector.bn_stats(stats[:, g, :], strided(chunk(q, s, g)[:, 0:1, 0:1, 0:1], [[G, 4], [G + 1, G], [G * NT, 2]])).then_inc(s_vec, 1)
                        dve.drain()
                        nc.vector.bn_aggr(mv[:, :], stats[:, :, :]).then_inc(s_vec, 1)
                        dve.wait_ge(s_group, 2 * k + 1)
                        nc.vector.tensor_copy(gmean[:, :], group[:, 0:1]).then_inc(s_vec, 1)
                        dve.wait_ge(s_vec, VS * k + 10)
                        nc.vector.tensor_tensor(dev[:, :], mv[:, 0:1], gmean[:, :], ALU.subtract).then_inc(s_vec, 1)
                        dve.wait_ge(s_vec, VS * k + 11)
                        nc.vector.scalar_tensor_tensor(out=spread[:, :], in0=dev[:, :], scalar=dev[:, 0:1], in1=mv[:, 1:2],
                                                       op0=ALU.mult, op1=ALU.add).then_inc(s_vec, 1)
                        dve.wait_ge(s_group, 2 * k + 2)
                        nc.vector.tensor_scalar(veps[:, :], group[:, 0:1], EPS, None, ALU.add).then_inc(s_vec, 1)
                        dve.wait_ge(s_rstd, k + 1)
                        nc.vector.scalar_tensor_tensor(out=shift[:, :], in0=gmean[:, :], scalar=-1.0, in1=rstd[:, :],
                                                       op0=ALU.mult, op1=ALU.mult).then_inc(s_vec, 1)
                        dve.wait_ge(s_vec, VS * k + 14)
                        nc.vector.tensor_scalar(image(q, s), image(q, s), rstd[:, 0:1], shift[:, 0:1],
                                                ALU.mult, ALU.add).then_inc(s_vec, 1)


PAIRS = STEPS // (2 * WIN)


def rows_of(pair):
    first = max(0, (pair * 2 * WIN - PERIOD * (SETS - 1) - G + 1) // (2 * WIN) * (2 * WIN))
    last = min(G, (pair + 1) * 2 * WIN)
    return first, last


def cleared_row(t):
    if t < G - 1:
        return t + 1
    if PERIOD <= t + 1 < PERIOD + G:
        return t - G
    return None


def lstm_phase(nc, sems, skew, hidden, weights, biases):
    W = ["wf0", "wf1", "wc", "wi", "wo"]
    U = ["uf0", "uf1", "uc", "ui", "uo"]
    BI = ["bf0", "bf1", "bc", "bi", "bo"]
    with ExitStack() as ctx:
        m = Memory(nc, ctx)
        w = {n: m.sb("l_" + n, [C, C]) for n in W + U}
        bias = {n: m.sb("l_" + n, [C, 1]) for n in BI}
        xw = [[m.sb(f"l_x{c}{q}", [C, LPC, WIN, G]) for q in range(2)] for c in range(CHAINS)]
        hw = [[m.sb(f"l_h{c}{q}", [C, LPC, WIN, SLOT]) for q in range(2)] for c in range(CHAINS)]
        hsum = [m.sb(f"l_hsum{c}", [C, LPC, G]) for c in range(CHAINS)]
        cell = [m.sb(f"l_cell{c}", [C, LPC, SLOT]) for c in range(CHAINS)]
        gate = [m.sb(f"l_gate{c}", [C, 5, LPC, G]) for c in range(CHAINS)]
        keep_up = [m.sb(f"l_up{c}", [C, LPC, G]) for c in range(CHAINS)]
        keep_left = [m.sb(f"l_left{c}", [C, LPC, G]) for c in range(CHAINS)]
        fresh = [m.sb(f"l_fresh{c}", [C, LPC, G]) for c in range(CHAINS)]
        tanhc = [m.sb(f"l_tanhc{c}", [C, LPC, G]) for c in range(CHAINS)]
        zero = m.sb("l_zero", [C, LPC])
        pf = [m.ps(f"l_pf{c}", [C, 2, LPC, G]) for c in range(CHAINS)]
        pc = [m.ps(f"l_pc{c}", [C, 2, LPC, G]) for c in range(CHAINS)]
        pio = [m.ps(f"l_pio{c}", [C, 2, LPC, G]) for c in range(CHAINS)]
        banks = [[pf[c][:, 0], pf[c][:, 1], pc[c][:, 0], pio[c][:, 0], pio[c][:, 1]] for c in range(CHAINS)]

        s_w = sems.sem("l_weights")
        s_init = sems.sem("l_init")
        s_x = [[sems.sem(f"l_x{c}{q}") for q in range(2)] for c in range(CHAINS)]
        s_st = [[sems.sem(f"l_store{c}{q}") for q in range(2)] for c in range(CHAINS)]
        s_xdone = [sems.sem(f"l_xdone{c}") for c in range(CHAINS)]
        s_gates = [sems.sem(f"l_gates{c}") for c in range(CHAINS)]
        s_act = [sems.sem(f"l_act{c}") for c in range(CHAINS)]
        s_cell = [sems.sem(f"l_cell{c}") for c in range(CHAINS)]
        VC = 9

        block = ctx.enter_context(nc.Block())

        def sizes(pair):
            r0, r1 = rows_of(pair)
            return slice(r0, r1), slice(r0 + 1, r1 + 1)

        def runs():
            looped = [p for p in range(PAIRS) if rows_of(p) == (0, G)
                      and all(cleared_row(t) == t - G for t in range(2 * WIN * p, 2 * WIN * (p + 1)))]
            lo, hi = looped[0], looped[-1] + 1
            return lo, hi

        LO, HI = runs()

        def each_pair(eng, body):
            for p in range(LO):
                body(p, p)
            with eng.Fori(LO, HI) as p:
                body(p, LO)
            for p in range(HI, PAIRS):
                body(p, p)

        @block.sync
        def _(sp):
            for n in W + U:
                sp.dma_start(w[n][:, :], weights[n]).then_inc(s_w, 16)
            for n in BI:
                sp.dma_start(bias[n][:, :], biases[n].rearrange("(p a) -> p a", a=1)).then_inc(s_w, 16)

            def body(p, like):
                for q in range(2):
                    for c in range(CHAINS):
                        sp.wait_ge(s_xdone[c], 2 * p + q + 1)
                        sp.dma_start(xw[c][q][:, :, :, :].rearrange("c l t g -> c l (t g)"),
                                     skew[c * LPC:(c + 1) * LPC, :, bass.ds((2 * p + q) * WIN * G, WIN * G)]
                                     .rearrange("l c g -> c l g")).then_inc(s_x[c][q], 16)
            each_pair(sp, body)

        @block.gpsimd
        def _(pool):
            for c in range(CHAINS):
                for q in range(2):
                    pool.memset(hw[c][q][:, :, :, :], 0.0).then_inc(s_init, 1)
                pool.memset(cell[c][:, :, :], 0.0).then_inc(s_init, 1)
                pool.memset(hsum[c][:, :, :], 0.0).then_inc(s_init, 1)
            pool.memset(zero[:, :], 0.0).then_inc(s_init, 1)
            pool.wait_ge(s_init, 4 * CHAINS + 1)
            for c in range(CHAINS):
                for q in range(2):
                    pool.dma_start(hidden[c * LPC, 0:1, q * WIN * SLOT:q * WIN * SLOT + 1],
                                   hw[c][q][0:1, 0, 0, 0:1]).then_inc(s_st[c][q], 16)

            def body(p, like):
                for q in range(2):
                    for c in range(CHAINS):
                        pool.wait_ge(s_cell[c], VC * ((2 * p + q + 1) * WIN))
                        pool.dma_start(hidden[c * LPC:(c + 1) * LPC, :, bass.ds((2 * p + q) * WIN * SLOT, WIN * SLOT)]
                                       .rearrange("l c g -> c l g"),
                                       hw[c][q][:, :, :, :].rearrange("c l t g -> c l (t g)")).then_inc(s_st[c][q], 16)
            each_pair(pool, body)
            for c in range(CHAINS):
                for q in range(2):
                    pool.wait_ge(s_st[c][q], 16 * (PAIRS + 1))

        @block.tensor
        def _(pe):
            for c in range(CHAINS):
                pe.sem_inc(s_xdone[c], 2)
            pe.wait_ge(s_w, 16 * 15)
            pe.wait_ge(s_init, 4 * CHAINS + 1)

            def body(p, like):
                rows, slots = sizes(like)
                for u in range(2 * WIN):
                    q, k = u // WIN, u % WIN
                    t = 2 * WIN * p + u
                    for c in range(CHAINS):
                        if k == 0:
                            pe.wait_ge(s_x[c][q], 16 * p + 16)
                        first = like == 0 and u == 0
                        xs = xw[c][q][:, :, k, rows]
                        for g in range(5):
                            if not first and g in (0, 2, 3):
                                pe.wait_ge(s_act[c], 6 * t - 6 + (2, 0, 3, 5)[g] if g != 3 else 6 * t - 6 + 5)
                            mm = nc.tensor.matmul(banks[c][g][:, :, rows], w[W[g]][:, :], xs,
                                                  start=g in (0, 2, 3), stop=False, skip_group_check=True)
                        if k == WIN - 1:
                            mm.then_inc(s_xdone[c], 1)
                        hprev = hw[c][(q if k else 1 - q)][:, :, (k - 1) % WIN, :]
                        up, left = hprev[:, :, rows], hprev[:, :, slots]
                        if not first:
                            pe.wait_ge(s_cell[c], VC * t - 1)
                        nc.tensor.matmul(banks[c][0][:, :, rows], w[U[0]][:, :], up, start=False, stop=True, skip_group_check=True)
                        nc.tensor.matmul(banks[c][1][:, :, rows], w[U[1]][:, :], left, start=False, stop=True,
                                         skip_group_check=True).then_inc(s_gates[c], 1)
                        if not first:
                            pe.wait_ge(s_cell[c], VC * t)
                        for g in (2, 3, 4):
                            mm = nc.tensor.matmul(banks[c][g][:, :, rows], w[U[g]][:, :], hsum[c][:, :, rows],
                                                  start=False, stop=True, skip_group_check=True)
                            if g != 3:
                                mm.then_inc(s_gates[c], 1)
            each_pair(pe, body)

        @block.scalar
        def _(act):
            act.wait_ge(s_w, 16 * 15)

            def body(p, like):
                rows, slots = sizes(like)
                for u in range(2 * WIN):
                    t = 2 * WIN * p + u
                    for c in range(CHAINS):
                        for g in range(5):
                            if g in (0, 2, 3):
                                act.wait_ge(s_gates[c], 3 * t + (1, 0, 2, 3)[g])
                            if g == 0 and not (like == 0 and u == 0):
                                act.wait_ge(s_cell[c], VC * t - 3)
                            nc.scalar.activation(gate[c][:, g, :, rows], banks[c][g][:, :, rows],
                                                 ACT.Tanh if g == 2 else ACT.Sigmoid, bias=bias[BI[g]][:, 0:1]).then_inc(s_act[c], 1)
                        act.wait_ge(s_cell[c], VC * t + 5)
                        nc.scalar.activation(tanhc[c][:, :, rows], cell[c][:, :, slots], ACT.Tanh).then_inc(s_act[c], 1)
            each_pair(act, body)

        @block.vector
        def _(dve):
            dve.wait_ge(s_init, 4 * CHAINS + 1)

            def body(p, like):
                rows, slots = sizes(like)
                for u in range(2 * WIN):
                    q, k = u // WIN, u % WIN
                    t = 2 * WIN * p + u
                    for c in range(CHAINS):
                        g = gate[c]
                        n = VC * t
                        up, left, mix, th = keep_up[c][:, :, rows], keep_left[c][:, :, rows], fresh[c][:, :, rows], tanhc[c][:, :, rows]
                        dve.wait_ge(s_act[c], 6 * t + 1)
                        if not (like == 0 and u == 0):
                            dve.wait_ge(s_cell[c], n)
                        nc.vector.tensor_tensor(up, g[:, 0, :, rows], cell[c][:, :, rows], ALU.mult).then_inc(s_cell[c], 1)
                        dve.wait_ge(s_act[c], 6 * t + 2)
                        nc.vector.tensor_tensor(left, g[:, 1, :, rows], cell[c][:, :, slots], ALU.mult).then_inc(s_cell[c], 1)
                        dve.wait_ge(s_cell[c], n + 2)
                        nc.vector.tensor_tensor(up, up, left, ALU.add).then_inc(s_cell[c], 1)
                        dve.wait_ge(s_act[c], 6 * t + 4)
                        nc.vector.tensor_tensor(mix, g[:, 3, :, rows], g[:, 2, :, rows], ALU.mult).then_inc(s_cell[c], 1)
                        dve.wait_ge(s_cell[c], n + 4)
                        nc.vector.tensor_tensor(cell[c][:, :, slots], up, mix, ALU.add).then_inc(s_cell[c], 1)
                        dve.wait_ge(s_act[c], 6 * t + 6)
                        if k == 0:
                            dve.wait_ge(s_st[c][q], 16 * p + 16)
                        h = hw[c][q][:, :, k, :]
                        nc.vector.tensor_tensor(h[:, :, slots], g[:, 4, :, rows], th, ALU.mult).then_inc(s_cell[c], 1)
                        dve.wait_ge(s_cell[c], n + 6)
                        if LO <= like < HI:
                            row = 2 * WIN * p + u - G + 1
                            hz, cz = h[:, :, bass.ds(row, 1)], cell[c][:, :, bass.ds(row, 1)]
                        elif cleared_row(2 * WIN * like + u) is not None and cleared_row(2 * WIN * like + u) < G:
                            row = cleared_row(2 * WIN * like + u) + 1
                            hz, cz = h[:, :, row:row + 1], cell[c][:, :, row:row + 1]
                        else:
                            hz, cz = h[:, :, 0:1], cell[c][:, :, 0:1]
                        z = zero[:, :].rearrange("p (l a) -> p l a", a=1)
                        nc.vector.tensor_copy(cz, z).then_inc(s_cell[c], 1)
                        nc.vector.tensor_copy(hz, z).then_inc(s_cell[c], 1)
                        nr, ns = sizes(like + 1) if (u == 2 * WIN - 1 and not LO <= like < HI - 0 and like + 1 < PAIRS) else (rows, slots)
                        dve.wait_ge(s_cell[c], n + 8)
                        nc.vector.tensor_tensor(hsum[c][:, :, nr], h[:, :, nr], h[:, :, ns], ALU.add).then_inc(s_cell[c], 1)
            each_pair(dve, body)


HEADS, DH, LM = 8, 16, 64
SEG = TOK // LM
PAIRS_H = HEADS // 2
GT = 4
NG = NT // GT
LSTM_RUN = (2 * G - 1) * SLOT
RMAX = bass.bass_isa.ReduceOp.max


class Resident:

    def __init__(self, m):
        self.attn2 = m.sb("r_attn2", [P, B, PAIRS_H, LM])
        self.k_lm = m.sb("r_k_lm", [C, B, LM])
        self.ctx = m.sb("r_ctx", [P, B, PAIRS_H, DH])
        self.ident = m.sb("r_ident", [P, P])
        self.head_mask = m.sb("r_head_mask", [C, HEADS, LM])


def fill_masks(pool, R, sem):
    make_identity(pool, R.ident, sem)
    mask = R.head_mask[:, :, :]
    pool.memset(mask, 1.0).then_inc(sem, 1)
    pool.wait_ge(sem, 3)
    pool.affine_select(out=mask, in_=mask, compare_op=ALU.is_ge, fill=0.0, base=0,
                       pattern=[[-DH, HEADS], [0, LM]], channel_multiplier=1).then_inc(sem, 1)
    pool.wait_ge(sem, 4)
    pool.affine_select(out=mask, in_=mask, compare_op=ALU.is_ge, fill=0.0, base=DH - 1,
                       pattern=[[DH, HEADS], [0, LM]], channel_multiplier=-1).then_inc(sem, 1)


def landmark_phase(nc, sems, R, x, hidden, wqkv, gamma, beta, b_out, xnt, base, vals):
    with ExitStack() as ctx:
        m = Memory(nc, ctx)
        hid = m.sb("a_hid", [C, LSTM_RUN])
        hrow = [m.sb(f"a_hrow{k}", [C, GT * P]) for k in range(2)]
        xin = m.sb("a_xin", [P, NT, C])
        t = m.sb("a_t", [P, NT, C])
        xn = [m.sb(f"a_xn{k}", [P, GT, C]) for k in range(2)]
        xnT = m.sb("a_xnT", [C, TOK])
        kT = m.sb("a_kT", [C, TOK])
        kT_lp = m.sb("a_kT_lp", [C, TOK], BF16)
        v = m.sb("a_v", [P, NT, C])
        w = m.sb("a_w", [C, 3 * C])
        gam = m.sb("a_gamma", [C, 1])
        bet = m.sb("a_beta", [C, 1])
        bout = m.sb("a_bout", [P, C])
        st = m.sb("a_st", [P, NT, 6])
        half = m.sb("a_half", [P, NT])
        stat = {n: m.sb("a_" + n, [P, NT]) for n in
                ("msum", "mdif", "m2", "msq", "m2s", "var", "vare", "r1", "r1sq", "v2", "v2e", "r2", "r", "sh", "rb", "shb")}
        xm = m.sb("a_xm", [C, LM])
        ql = m.sb("a_ql", [C, LM])
        kl = m.sb("a_kl", [C, LM])
        qbd = m.sb("a_qbd", [C, HEADS * LM])
        qbd_lp = m.sb("a_qbd_lp", [C, HEADS * LM], BF16)
        mx2 = m.sb("a_mx2", [P, PAIRS_H])
        sum2 = m.sb("a_sum2", [P, PAIRS_H])
        rec2 = m.sb("a_rec2", [P, PAIRS_H])
        e2 = m.sb("a_e2", [P, PAIRS_H, LM])
        e2x = m.sb("a_e2x", [P, PAIRS_H, LM])
        m3p = m.sb("a_m3p", [P, PAIRS_H, NG])
        m3 = m.sb("a_m3", [P, PAIRS_H])
        neg4 = m.sb("a_neg4", [PAIRS_H, PAIRS_H, P])
        m3row = m.sb("a_m3row", [PAIRS_H, PAIRS_H, P], BF16)
        ones4 = m.sb("a_ones4", [PAIRS_H, P], BF16)
        ones = m.sb("a_ones", [P, 1])
        p3 = [m.sb(f"a_p3{k}", [P, HEADS * LM]) for k in range(4)]
        acc = m.sb("a_acc", [P, HEADS * LM])
        pvs = m.sb("a_pvs", [C, P])
        den = m.sb("a_den", [P, PAIRS_H])
        turn = [m.ps(f"a_turn{k}", [P, GT, P]) for k in range(2)]
        S = [m.ps(f"a_s{k}", [P, 512]) for k in range(4)]
        pv = m.ps("a_pv", [C, 512])
        misc = m.ps("a_misc", [P, 512])

        s_w = sems.sem("a_w")
        s_const = sems.sem("a_const")
        s_ones = sems.sem("a_ones")
        s_hid = sems.sem("a_hid")
        s_xin = sems.sem("a_xin")
        s_hc = sems.sem("a_hc")
        s_ht = sems.sem("a_ht")
        s_add = sems.sem("a_add")
        s_ln = sems.sem("a_ln")
        s_pow = sems.sem("a_pow")
        s_xn = sems.sem("a_xn")
        s_sc = sems.sem("a_sc")
        s_base = sems.sem("a_base")
        s_xt = sems.sem("a_xt")
        s_xnT = sems.sem("a_xnT")
        s_stx = sems.sem("a_store_xnt")
        s_stb = sems.sem("a_store_base")
        s_stv = sems.sem("a_store_v")
        s_lm = sems.sem("a_lm")
        s_mm = sems.sem("a_mm")
        s_e2 = sems.sem("a_e2")
        s_s = sems.sem("a_s")
        s_sa = sems.sem("a_sa")
        s_kl = sems.sem("a_kl")
        s_mx = sems.sem("a_mx")
        s_pv = sems.sem("a_pv")
        s_acc = sems.sem("a_acc")
        LN = NG + 14
        K0, V0, L0, S0 = 0, NG, 2 * NG, 2 * NG + PAIRS_H * NG
        SU = S0 + NT
        NORMED = 20

        def lm(b, k):
            return 1 + 17 * b + k

        def mm(b, k):
            return 1 + 5 * b + k

        def sa(b, k):
            return 4 + (2 * NG + NT) * b + k

        def pv_done(b, n):
            return 4 + NT * b + n + 1

        def acc_done(b, n):
            return 4 + (NT - 1) * b + max(n, 1)

        block = ctx.enter_context(nc.Block())

        @block.sync
        def _(sp):
            sp.dma_start(w[:, :], wqkv).then_inc(s_w, 16)
            sp.dma_start(gam[:, :], gamma.rearrange("(p a) -> p a", a=1)).then_inc(s_w, 16)
            sp.dma_start(bet[:, :], beta.rearrange("(p a) -> p a", a=1)).then_inc(s_w, 16)
            sp.dma_start(bout[:, :], b_out.rearrange("(a c) -> a c", a=1).broadcast_to([P, C])).then_inc(s_w, 16)

            def load(a):
                sp.dma_start(hid[:, :], hidden[a % LANES, :, bass.ds((a // LANES) * (PERIOD * SLOT), LSTM_RUN)]
                             ).then_inc(s_hid, 16)
                for g in range(NG):
                    sp.dma_start(xin[:, GT * g:GT * g + GT, :], x[a, 512 * g:512 * g + 512, :].rearrange("(n p) c -> p n c", p=P)
                                 ).then_inc(s_xin, 16)

            def image(b, more):
                sp.wait_ge(s_xnT, 2 + NG * (b + 1))
                sp.dma_start(xnt[b], xnT[:, :]).then_inc(s_stx, 16)
                sp.wait_ge(s_base, NG * (b + 1))
                sp.dma_start(base[b].rearrange("(n p) c -> p n c", p=P), t[:, :, :]).then_inc(s_stb, 16)
                if more:
                    sp.wait_ge(s_hc, NG * (b + 1))
                    sp.wait_ge(s_add, NG * (b + 1))
                    load(b + 1)
                sp.wait_ge(s_sa, sa(b, 2 * NG))
                sp.dma_start(vals[b].rearrange("(n p) c -> p n c", p=P), v[:, :, :]).then_inc(s_stv, 16)
            load(0)
            with sp.Fori(0, B - 1) as b:
                image(b, True)
            image(B - 1, False)
            sp.wait_ge(s_stx, 16 * B)
            sp.wait_ge(s_stb, 16 * B)
            sp.wait_ge(s_stv, 16 * B)

        @block.gpsimd
        def _(pool):
            fill_masks(pool, R, s_const)
            pool.memset(half[:, :], -0.5).then_inc(s_const, 1)
            pool.memset(ones4[:, :], 1.0).then_inc(s_ones, 1)
            pool.memset(ones[:, :], 1.0).then_inc(s_ones, 1)
            pool.memset(neg4[:, :, :], 0.0).then_inc(s_ones, 1)
            pool.wait_ge(s_ones, 3)
            pool.affine_select(out=neg4[:, :, :], in_=neg4[:, :, :], compare_op=ALU.not_equal, fill=-1.0, base=0,
                               pattern=[[-1, PAIRS_H], [0, P]], channel_multiplier=1).then_inc(s_ones, 1)
            pool.sem_inc(s_acc, 4)
            pool.wait_ge(s_const, 6)
            pool.wait_ge(s_w, 64)

            def powers(a):
                pool.wait_ge(s_ln, LN * a + NG + 7)
                pool.tensor_tensor(stat["r1"][:, :], stat["vare"][:, :], half[:, :], ALU.pow).then_inc(s_pow, 1)
                pool.wait_ge(s_ln, LN * a + NG + 10)
                pool.tensor_tensor(stat["r2"][:, :], stat["v2e"][:, :], half[:, :], ALU.pow).then_inc(s_pow, 1)

            def add_bias(a, g):
                pool.wait_ge(s_sc, NG * a + g + 1)
                tg = t[:, GT * g:GT * g + GT, :]
                pool.tensor_tensor(tg, tg, bout[:, :].unsqueeze(1).broadcast_to([P, GT, C]), ALU.add).then_inc(s_base, 1)

            def image(b, more):
                for n in range(NT):
                    if n == 1:
                        pool.wait_ge(s_mm, mm(b, 0))
                        pool.wait_ge(s_sa, sa(b, 2 * NG + 2))
                        pool.tensor_tensor(acc[:, :], p3[0][:, :], p3[1][:, :], ALU.add).then_inc(s_acc, 1)
                    elif n:
                        pool.wait_ge(s_sa, sa(b, 2 * NG + n + 1))
                        pool.wait_ge(s_acc, acc_done(b, n - 1))
                        pool.tensor_tensor(acc[:, :], acc[:, :], p3[n % 4][:, :], ALU.add).then_inc(s_acc, 1)
                    if more and n == 18:
                        powers(b + 1)
                    if more and 0 <= n - NORMED - 2 < NG:
                        add_bias(b + 1, n - NORMED - 2)
            powers(0)
            for g in range(NG):
                add_bias(0, g)
            with pool.Fori(0, B - 1) as b:
                image(b, True)
            image(B - 1, False)

        @block.tensor
        def _(pe):
            pe.sem_inc(s_mm, 1)
            pe.sem_inc(s_pv, 4)
            pe.wait_ge(s_const, 6)
            pe.wait_ge(s_ones, 4)
            pe.wait_ge(s_w, 64)

            def turn_hidden(a, g):
                pe.wait_ge(s_hc, NG * a + g + 1)
                if g < 2:
                    pe.wait_ge(s_xnT, NG * a + g + 1)
                else:
                    pe.wait_ge(s_add, NG * a + g - 1)
                for k in range(GT):
                    mt = nc.tensor.transpose(turn[g % 2][:, k, :], hrow[g % 2][:, P * k:P * k + P], R.ident[:, :])
                mt.then_inc(s_ht, 1)

            def turn_normed(a, g):
                if g < 2:
                    pe.wait_ge(s_add, NG * a + g + 7)
                else:
                    pe.wait_ge(s_xnT, 2 + NG * a + g - 1)
                pe.wait_ge(s_xn, NG * a + g + 1)
                for k in range(GT):
                    mt = nc.tensor.transpose(turn[g % 2][:, k, :], xn[g % 2][:, k, :], R.ident[:, :])
                mt.then_inc(s_xt, 1)

            def image(b, more):
                pe.wait_ge(s_lm, lm(b, 1))
                nc.tensor.matmul(misc[:, 0:LM], w[:, 0:C], xm[:, :], start=True, stop=True)
                nc.tensor.matmul(misc[:, LM:2 * LM], w[:, C:2 * C], xm[:, :], start=True, stop=True).then_inc(s_mm, 1)
                for g in range(NG):
                    pe.wait_ge(s_sa, sa(b, g - 3))
                    nc.tensor.matmul(S[(K0 + g) % 4][:, :], w[:, C:2 * C], xnT[:, 512 * g:512 * g + 512],
                                     start=True, stop=True).then_inc(s_s, 1)
                pe.wait_ge(s_lm, lm(b, 5))
                for g in range(PAIRS_H):
                    mt = nc.tensor.matmul(misc[:, P + LM * g:P + LM * g + LM], qbd[:, P * g:P * g + P], kl[:, :],
                                          start=True, stop=True)
                mt.then_inc(s_mm, 1)
                for g in range(NG):
                    pe.wait_ge(s_sa, sa(b, NG + g - 3))
                    for k in range(GT):
                        n = GT * g + k
                        mt = nc.tensor.matmul(S[(V0 + g) % 4][:, P * k:P * k + P], xnT[:, P * n:P * n + P], w[:, 2 * C:3 * C],
                                              start=True, stop=True)
                    mt.then_inc(s_s, 1)
                pe.wait_ge(s_lm, lm(b, 6))
                for j in range(PAIRS_H * NG):
                    c, g = j // PAIRS_H, j % PAIRS_H
                    if g == 0:
                        pe.wait_ge(s_kl, NG * b + c + 1)
                    if j < 4:
                        pe.wait_ge(s_sa, sa(b, NG + 4 + j + 1))
                    else:
                        pe.wait_ge(s_mx, PAIRS_H * NG * b + j - 3)
                    nc.tensor.matmul(S[(L0 + j) % 4][:, :], qbd_lp[:, P * g:P * g + P], kT_lp[:, 512 * c:512 * c + 512],
                                     start=True, stop=True).then_inc(s_s, 1)
                pe.wait_ge(s_lm, lm(b, 9))
                nc.tensor.transpose(misc[0:PAIRS_H, 384:512], m3[:, :], R.ident[:, :]).then_inc(s_mm, 1)

                def weigh(n):
                    pe.wait_ge(s_sa, sa(b, 2 * NG + n + 1))
                    if n == 0:
                        pe.wait_ge(s_lm, lm(b, 0))
                    for g in range(PAIRS_H):
                        mt = nc.tensor.matmul(pv[32 * g:32 * g + 32, 0:P], v[:, n, 32 * g:32 * g + 32],
                                              p3[n % 4][:, P * g:P * g + P], start=n == 0, stop=n == NT - 1)
                    mt.then_inc(s_pv, 1)

                for n in range(NT):
                    if n == 0:
                        pe.wait_ge(s_lm, lm(b, 10))
                    if n < 4:
                        pe.wait_ge(s_mx, PAIRS_H * NG * b + 28 + n + 1)
                    else:
                        pe.wait_ge(s_sa, sa(b, 2 * NG + n - 3))
                    bank = S[(S0 + n) % 4]
                    nc.tensor.matmul(bank[:, :], kT[:, P * n:P * n + P], qbd[:, :], start=True, stop=False)
                    nc.tensor.matmul(bank[:, :], ones4[:, :], m3row[:, :, :].rearrange("p g c -> p (g c)"),
                                     start=False, stop=True).then_inc(s_s, 1)
                    if n >= 2:
                        weigh(n - 2)
                    if more and n % 2 == 0 and 0 <= n // 2 - 1 < NG:
                        turn_hidden(b + 1, n // 2 - 1)
                    if more and 0 <= n - NORMED < NG:
                        turn_normed(b + 1, n - NORMED)
                weigh(NT - 2)
                weigh(NT - 1)
                pe.wait_ge(s_acc, acc_done(b, NT - 1))
                for g in range(PAIRS_H):
                    mt = nc.tensor.matmul(misc[:, g:g + 1], acc[:, P * g:P * g + P], ones[:, :], start=True, stop=True)
                mt.then_inc(s_mm, 1)
                pe.wait_ge(s_lm, lm(b, 14))
                nc.tensor.transpose(misc[:, P:2 * P], pvs[:, :], R.ident[:, :]).then_inc(s_mm, 1)

            for turn_group in (turn_hidden, turn_normed):
                for g in range(NG):
                    turn_group(0, g)
            with pe.Fori(0, B - 1) as b:
                image(b, True)
            image(B - 1, False)

        @block.scalar
        def _(act):
            act.sem_inc(s_xnT, 2)
            act.sem_inc(s_sa, 4)
            act.wait_ge(s_w, 64)

            def unskew(a, g):
                if g == 0:
                    act.wait_ge(s_hid, 16 * a + 16)
                if g >= 2 or not isinstance(a, int):
                    act.wait_ge(s_ht, NG * a + g - 1)
                rows = GT * P // G
                start = (SLOT + 1) * rows * g + 1
                nc.scalar.activation(hrow[g % 2][:, :].rearrange("c (i j) -> c i j", j=G),
                                     strided(hid[:, start:start + 1], [[SLOT + 1, rows], [SLOT, G]]),
                                     ACT.Identity).then_inc(s_hc, 1)

            def norm_group(a, g):
                act.wait_ge(s_xn, NG * a + g + 1)
                for k in range(GT):
                    n = GT * g + k
                    ma = nc.scalar.activation(t[:, n, :], t[:, n, :], ACT.Identity, bias=stat["shb"][:, n:n + 1],
                                              scale=stat["rb"][:, n:n + 1])
                ma.then_inc(s_sc, 1)
                act.wait_ge(s_xt, NG * a + g + 1)
                if g == 0 and not isinstance(a, int):
                    act.wait_ge(s_stx, 16 * a)
                nc.scalar.activation(xnT[:, 512 * g:512 * g + 512], turn[g % 2][:, :, :].rearrange("c k t -> c (k t)"), ACT.Identity,
                                     bias=bet[:, 0:1], scale=gam[:, 0:1]).then_inc(s_xnT, 1)

            def image(b, more):
                for g in range(NG):
                    act.wait_ge(s_s, SU * b + K0 + g + 1)
                    nc.scalar.activation(kT[:, 512 * g:512 * g + 512], S[(K0 + g) % 4][:, :], ACT.Identity).then_inc(s_sa, 1)
                for g in range(NG):
                    act.wait_ge(s_s, SU * b + V0 + g + 1)
                    nc.scalar.activation(v[:, GT * g:GT * g + GT, :].rearrange("p k c -> p (k c)"), S[(V0 + g) % 4][:, :],
                                         ACT.Identity).then_inc(s_sa, 1)
                act.wait_ge(s_lm, lm(b, 8))
                nc.scalar.activation(e2x[:, :, :], e2[:, :, :], ACT.Exp).then_inc(s_e2, 1)
                for n in range(NT):
                    act.wait_ge(s_s, SU * b + S0 + n + 1)
                    act.wait_ge(s_pv, pv_done(b, n - 4))
                    act.wait_ge(s_acc, (acc_done(b, n - 4) if n >= 4 else 4 + (NT - 1) * b - 3 + n))
                    nc.scalar.activation(p3[n % 4][:, :], S[(S0 + n) % 4][:, :], ACT.Exp).then_inc(s_sa, 1)
                    if more and n % 2 == 0 and n // 2 < NG:
                        unskew(b + 1, n // 2)
                    if more and 0 <= n - NORMED - 1 < NG:
                        norm_group(b + 1, n - NORMED - 1)
                if more:
                    act.wait_ge(s_stv, 16 * (b + 1))
            for g in range(NG):
                unskew(0, g)
            for g in range(NG):
                norm_group(0, g)
            with act.Fori(0, B - 1) as b:
                image(b, True)
            image(B - 1, False)

        @block.vector
        def _(dve):
            dve.sem_inc(s_lm, 1)
            dve.wait_ge(s_const, 6)
            dve.wait_ge(s_ones, 4)
            dve.wait_ge(s_w, 64)

            def add_group(a, g):
                if g == 0:
                    dve.wait_ge(s_xin, 16 * NG * (a + 1))
                    if not isinstance(a, int):
                        dve.wait_ge(s_stb, 16 * a)
                dve.wait_ge(s_ht, NG * a + g + 1)
                nc.vector.tensor_tensor(t[:, GT * g:GT * g + GT, :], turn[g % 2][:, :, :], xin[:, GT * g:GT * g + GT, :],
                                        ALU.add).then_inc(s_add, 1)
                dve.wait_ge(s_add, NG * a + g + 1)
                for n in range(GT * g, GT * g + GT):
                    ms = nc.vector.bn_stats(st[:, n, :], t[:, n, :])
                ms.then_inc(s_ln, 1)

            def statistics(a):
                T = {n: s[:, :] for n, s in stat.items()}
                me, qe, mo, qo = st[:, :, 1], st[:, :, 2], st[:, :, 4], st[:, :, 5]
                at = LN * a + NG
                steps = 0

                def step(ins):
                    nonlocal steps
                    steps += 1
                    ins.then_inc(s_ln, 1)
                    dve.wait_ge(s_ln, at + steps)

                dve.wait_ge(s_ln, at)
                step(nc.vector.tensor_tensor(T["msum"], me, mo, ALU.add))
                step(nc.vector.tensor_tensor(T["mdif"], me, mo, ALU.subtract))
                step(nc.vector.tensor_tensor(T["m2"], qe, qo, ALU.add))
                step(nc.vector.tensor_tensor(T["msq"], T["mdif"], T["mdif"], ALU.mult))
                step(nc.vector.tensor_scalar(T["m2s"], T["m2"], 1.0 / C, None, ALU.mult))
                step(nc.vector.scalar_tensor_tensor(out=T["var"], in0=T["msq"], scalar=0.25, in1=T["m2s"], op0=ALU.mult, op1=ALU.add))
                step(nc.vector.tensor_scalar(T["vare"], T["var"], EPS, None, ALU.add))
                dve.wait_ge(s_pow, 2 * a + 1)
                step(nc.vector.tensor_tensor(T["r1sq"], T["r1"], T["r1"], ALU.mult))
                step(nc.vector.tensor_tensor(T["v2"], T["var"], T["r1sq"], ALU.mult))
                step(nc.vector.tensor_scalar(T["v2e"], T["v2"], EPS, None, ALU.add))
                step(nc.vector.tensor_scalar(T["rb"], T["r1"], 1.0, None, ALU.add))
                step(nc.vector.scalar_tensor_tensor(out=T["shb"], in0=T["msum"], scalar=-0.5, in1=T["r1"], op0=ALU.mult, op1=ALU.mult))
                dve.wait_ge(s_pow, 2 * a + 2)
                step(nc.vector.tensor_tensor(T["r"], T["r1"], T["r2"], ALU.mult))
                step(nc.vector.scalar_tensor_tensor(out=T["sh"], in0=T["msum"], scalar=-0.5, in1=T["r"], op0=ALU.mult, op1=ALU.mult))
                assert steps == LN - NG

            def norm_group(a, g):
                if g >= 2:
                    dve.wait_ge(s_xt, NG * a + g - 1)
                for k in range(GT):
                    n = GT * g + k
                    mn = nc.vector.tensor_scalar(xn[g % 2][:, k, :], t[:, n, :], stat["r"][:, n:n + 1], stat["sh"][:, n:n + 1],
                                                 ALU.mult, ALU.add)
                mn.then_inc(s_xn, 1)

            def norms(a):
                for g in range(NG):
                    add_group(a, g)
                statistics(a)
                for g in range(NG):
                    norm_group(a, g)

            def image(b, more):
                steps = 0

                def step(ins):
                    nonlocal steps
                    steps += 1
                    ins.then_inc(s_lm, 1)
                    return steps

                dve.wait_ge(s_xnT, 2 + NG * (b + 1))
                step(nc.vector.tensor_reduce(xm[:, :], xnT[:, :].rearrange("c (l k) -> c l k", k=SEG), AX.X, ALU.add))
                dve.wait_ge(s_mm, mm(b, 1))
                step(nc.vector.tensor_scalar(ql[:, :], misc[:, 0:LM], DH ** -0.5 / SEG, None, ALU.mult))
                step(nc.vector.tensor_scalar(kl[:, :], misc[:, LM:2 * LM], 1.0 / SEG, None, ALU.mult))
                dve.wait_ge(s_lm, lm(b, 3))
                step(nc.vector.tensor_scalar(R.k_lm[:, bass.ds(b, 1), :], kl[:, :].unsqueeze(1), 1.0, None, ALU.mult))
                step(nc.vector.tensor_tensor(qbd[:, :].rearrange("c (h l) -> c h l", l=LM), R.head_mask[:, :, :],
                                             ql[:, :].unsqueeze(1).broadcast_to([C, HEADS, LM]), ALU.mult))
                dve.wait_ge(s_lm, lm(b, 5))
                step(nc.vector.tensor_copy(qbd_lp[:, :], qbd[:, :]))
                for g in range(NG):
                    dve.wait_ge(s_sa, sa(b, g + 1))
                    nc.vector.tensor_copy(kT_lp[:, 512 * g:512 * g + 512], kT[:, 512 * g:512 * g + 512]).then_inc(s_kl, 1)
                scores = misc[:, P:P + PAIRS_H * LM].rearrange("p (g l) -> p g l", l=LM)
                dve.wait_ge(s_mm, mm(b, 2))
                step(nc.vector.tensor_reduce(mx2[:, :], scores, AX.X, ALU.max))
                dve.wait_ge(s_lm, lm(b, 7))
                step(nc.vector.tensor_tensor(e2[:, :, :], scores, mx2[:, :].unsqueeze(2).broadcast_to([P, PAIRS_H, LM]), ALU.subtract))
                for j in range(PAIRS_H * NG):
                    c, g = j // PAIRS_H, j % PAIRS_H
                    dve.wait_ge(s_s, SU * b + L0 + j + 1)
                    nc.vector.tensor_reduce(m3p[:, g, c:c + 1], S[(L0 + j) % 4][:, :], AX.X, ALU.max).then_inc(s_mx, 1)
                dve.wait_ge(s_mx, PAIRS_H * NG * (b + 1))
                step(nc.vector.tensor_reduce(m3[:, :], m3p[:, :, :], AX.X, ALU.max))
                dve.wait_ge(s_mm, mm(b, 3))
                step(nc.vector.tensor_tensor(m3row[:, :, :], misc[0:PAIRS_H, 384:512].unsqueeze(1).broadcast_to([PAIRS_H, PAIRS_H, P]),
                                             neg4[:, :, :], ALU.mult))
                dve.wait_ge(s_e2, b + 1)
                step(nc.vector.tensor_reduce(sum2[:, :], e2x[:, :, :], AX.X, ALU.add))
                dve.wait_ge(s_lm, lm(b, 11))
                step(nc.vector.reciprocal(rec2[:, :], sum2[:, :]))
                dve.wait_ge(s_lm, lm(b, 12))
                step(nc.vector.tensor_tensor(R.attn2[:, bass.ds(b, 1), :, :].rearrange("p a g l -> p (a g) l"), e2x[:, :, :],
                                             rec2[:, :].unsqueeze(2).broadcast_to([P, PAIRS_H, LM]), ALU.mult))
                if more:
                    norms(b + 1)
                dve.wait_ge(s_pv, pv_done(b, NT - 1))
                step(nc.vector.tensor_copy(pvs[:, :], pv[:, 0:P]))
                dve.wait_ge(s_mm, mm(b, 5))
                step(nc.vector.reciprocal(den[:, :], misc[:, 0:PAIRS_H]))
                dve.wait_ge(s_lm, lm(b, 15))
                for h in range(2):
                    rows = slice(LM * h, LM * h + LM)
                    src = misc[rows, P:2 * P].rearrange("p (g h d) -> p g h d", g=PAIRS_H, h=2)[:, :, h, :]
                    step(nc.vector.tensor_tensor(R.ctx[rows, bass.ds(b, 1), :, :].rearrange("p a g d -> p (a g) d"), src,
                                                 den[rows, :].unsqueeze(2).broadcast_to([LM, PAIRS_H, DH]), ALU.mult))
                assert steps == 17

            norms(0)
            with dve.Fori(0, B - 1) as b:
                image(b, True)
            image(B - 1, False)


PINV_ITERS = 6
NP = B * PAIRS_H
PCH = 8
NCH = NP // PCH


def pinv_phase(nc, sems, R):
    with ExitStack() as ctx:
        m = Memory(nc, ctx)
        xT = m.sb("i_xT", [P, NP, LM])
        pz = m.sb("i_pz", [P, NP, 2, LM])
        tm = m.sb("i_tm", [P, NP, LM])
        eye = {k: m.sb(f"i_eye{n}", [P, LM]) for n, k in enumerate((1.0, 7.0, 15.0, 3.25))}
        halves = m.sb("i_halves", [P, P])
        rsum = m.sb("i_rsum", [P, NP])
        cmax = m.sb("i_cmax", [P, NCH])
        top = m.sb("i_top", [P, 2])
        tops = m.sb("i_tops", [P, 2])
        prod = m.sb("i_prod", [P, 1])
        inv = m.sb("i_inv", [P, 1])
        bank = [m.ps(f"i_bank{k}", [P, PCH, LM]) for k in range(4)]
        wide = [[m.ps(f"i_wide{k}{h}", [P, PCH // 2, 2, LM]) for h in range(2)] for k in range(2)]

        s_const = sems.sem("i_const")
        s_norm = sems.sem("i_norm")
        s_col = sems.sem("i_col")
        s_all = sems.sem("i_all")
        s_x = sems.sem("i_x")
        s_xc = sems.sem("i_xc")
        s_q = sems.sem("i_q")
        s_t = sems.sem("i_t")
        s_pz = sems.sem("i_pz")
        s_new = sems.sem("i_new")
        s_pass = sems.sem("i_pass")
        s_z = sems.sem("i_z")

        block = ctx.enter_context(nc.Block())

        def flat(ap):
            return ap.rearrange("p a l -> p (a l)")

        x = R.attn2[:, :, :, :].rearrange("p b g l -> p (b g) l")
        c3 = R.ctx[:, :, :, :].rearrange("p b g d -> p (b g) d")
        chunk = [slice(PCH * c, PCH * c + PCH) for c in range(NCH)]
        HEAD = [slice(0, LM), slice(LM, 2 * LM)]

        @block.gpsimd
        def _(pool):
            pool.memset(halves[:, :], 0.0).then_inc(s_const, 1)
            pool.wait_ge(s_const, 1)
            for h in HEAD:
                pool.memset(halves[h, h], 1.0).then_inc(s_const, 1)
            pool.wait_ge(s_norm, 7)
            pool.partition_all_reduce(tops[:, :], top[:, :], P, RMAX).then_inc(s_all, 1)

        @block.tensor
        def _(pe):
            pe.wait_ge(s_const, 3)
            for c in range(NCH):
                if c >= 4:
                    pe.wait_ge(s_col, c - 3)
                nc.tensor.matmul(flat(bank[c % 4][:, :, :]), halves[:, :], flat(x[:, chunk[c], :]), start=True, stop=True).then_inc(s_x, 1)
            pe.wait_ge(s_norm, 4)
            for c in range(NCH):
                if c < 4:
                    pe.wait_ge(s_col, NCH + c - 3)
                else:
                    pe.wait_ge(s_xc, c - 3)
                for j in range(PCH):
                    for h in HEAD:
                        mt = nc.tensor.matmul(bank[c % 4][h, j, :], x[h, PCH * c + j, :], eye[1.0][h, :], start=True, stop=True)
                mt.then_inc(s_x, 1)
            for c in range(NCH):
                pe.wait_ge(s_xc, NCH + c - 3)
                pe.wait_ge(s_xc, c + 1)
                for j in range(PCH):
                    for h in HEAD:
                        xt = xT[h, PCH * c + j, :]
                        mt = nc.tensor.matmul(bank[c % 4][h, j, :], xt, xt, start=True, stop=True)
                mt.then_inc(s_x, 1)

            def iteration(k):
                for stage in range(2):
                    for c in range(NCH):
                        at = 3 * NCH * k + NCH * stage
                        pe.wait_ge(s_t, at + NCH + c - 3 if c >= 4 else at + c + 1 + 4 * stage)
                        pe.sem_inc(s_pass, 1)
                        for j in range(PCH):
                            for h in HEAD:
                                n = PCH * c + j
                                mt = nc.tensor.matmul(bank[c % 4][h, j, :], pz[h, n, 0, :], tm[h, n, :], start=True, stop=True)
                        mt.then_inc(s_q, 1)
                for c in range(NCH):
                    pe.wait_ge(s_t, 3 * NCH * k + 2 * NCH + c + 1)
                    pe.sem_inc(s_pass, 1)
                    pe.wait_ge(s_new, NCH * (k + 1) + c + 1)
                    pe.sem_inc(s_pass, 1)
                    for j in range(PCH):
                        for h in HEAD:
                            n = PCH * c + j
                            out = wide[c % 2][j // 4][h, j % 4, :, :].rearrange("p a l -> p (a l)")
                            mt = nc.tensor.matmul(out, tm[h, n, :], pz[h, n, :, :].rearrange("p a l -> p (a l)"),
                                                  start=True, stop=True)
                    mt.then_inc(s_pz, 1)
            pe.wait_ge(s_xc, 2 * NCH)
            with pe.Fori(0, PINV_ITERS) as k:
                iteration(k)
            pe.wait_ge(s_new, 2 + NCH * (PINV_ITERS + 1))
            for n in range(NP):
                for h in HEAD:
                    out = bank[n // 32][h, n % 32 // 4, DH * (n % 4):DH * (n % 4) + DH]
                    mt = nc.tensor.matmul(out, pz[h, n, 1, :], c3[h, n, :], start=True, stop=True)
            mt.then_inc(s_z, 1)

        @block.scalar
        def _(act):
            act.sem_inc(s_new, 2)
            for c in range(NCH):
                act.wait_ge(s_x, NCH + c + 1)
                nc.scalar.activation(xT[:, chunk[c], :], bank[c % 4][:, :, :], ACT.Identity).then_inc(s_xc, 1)
            act.wait_ge(s_norm, 9)
            for c in range(NCH):
                act.wait_ge(s_x, 2 * NCH + c + 1)
                nc.scalar.activation(pz[:, chunk[c], 0, :], bank[c % 4][:, :, :], ACT.Identity, scale=inv[:, 0:1]).then_inc(s_xc, 1)
                nc.scalar.activation(pz[:, chunk[c], 1, :], x[:, chunk[c], :], ACT.Identity, scale=inv[:, 0:1]).then_inc(s_new, 1)

            with act.Fori(0, PINV_ITERS) as k:
                for c in range(NCH):
                    act.wait_ge(s_pz, NCH * k + c + 1)
                    for h in range(2):
                        lo = PCH * c + 4 * h
                        mc = nc.scalar.activation(pz[:, lo:lo + 4, :, :], wide[c % 2][h][:, :, :, :], ACT.Identity)
                    mc.then_inc(s_new, 1)

        @block.vector
        def _(dve):
            steps = 0

            def step(ins):
                nonlocal steps
                steps += 1
                ins.then_inc(s_norm, 1)
                dve.wait_ge(s_norm, steps)
            step(nc.vector.tensor_tensor(eye[1.0][:, :], R.ident[:, 0:LM], R.ident[:, LM:2 * LM], ALU.add))
            for k in (7.0, 15.0, 3.25):
                step(nc.vector.tensor_scalar(eye[k][:, :], eye[1.0][:, :], k, None, ALU.mult))
            step(nc.vector.tensor_reduce(rsum[:, :], x, AX.X, ALU.add))
            step(nc.vector.tensor_reduce(top[:, 0:1], rsum[:, :], AX.X, ALU.max))
            for c in range(NCH):
                dve.wait_ge(s_x, c + 1)
                nc.vector.tensor_reduce(cmax[:, c:c + 1], flat(bank[c % 4][:, :, :]), AX.X, ALU.max).then_inc(s_col, 1)
            dve.wait_ge(s_col, NCH)
            step(nc.vector.tensor_reduce(top[:, 1:2], cmax[:, :], AX.X, ALU.max))
            dve.wait_ge(s_all, 1)
            step(nc.vector.tensor_tensor(prod[:, :], tops[:, 0:1], tops[:, 1:2], ALU.mult))
            step(nc.vector.reciprocal(inv[:, :], prod[:, :]))

            def both(k):
                return eye[k][:, :].unsqueeze(1).broadcast_to([P, PCH, LM])

            with dve.Fori(0, PINV_ITERS) as k:
                for c in range(NCH):
                    dve.wait_ge(s_new, 2 + NCH * k + c + 1)
                    nc.vector.tensor_tensor(tm[:, chunk[c], :], both(7.0), pz[:, chunk[c], 0, :], ALU.subtract).then_inc(s_t, 1)
                for c in range(NCH):
                    dve.wait_ge(s_q, 2 * NCH * k + c + 1)
                    nc.vector.tensor_tensor(tm[:, chunk[c], :], both(15.0), bank[c % 4][:, :, :], ALU.subtract).then_inc(s_t, 1)
                for c in range(NCH):
                    dve.wait_ge(s_q, 2 * NCH * k + NCH + c + 1)
                    nc.vector.scalar_tensor_tensor(out=tm[:, chunk[c], :], in0=bank[c % 4][:, :, :], scalar=-0.25,
                                                   in1=both(3.25), op0=ALU.mult, op1=ALU.add).then_inc(s_t, 1)
            dve.wait_ge(s_z, 1)
            for q in range(2):
                nc.vector.tensor_copy(c3[:, 32 * q:32 * q + 32, :].rearrange("p n d -> p (n d)"),
                                      flat(bank[q][:, :, :])).then_inc(s_z, 1)


TAPS = 33
EDGE = 32
BAND = P + 2 * EDGE


def output_phase(nc, sems, R, xnt, base, vals, band, taps, wqkv, w_out, ffn_wT, t2, wx, wx_stats):
    with ExitStack() as ctx:
        m = Memory(nc, ctx)
        w = m.sb("o_wq", [C, C])
        wT = m.sb("o_wqT", [C, C])
        wo = m.sb("o_wo", [C, C])
        fw = m.sb("o_fw", [C, C])
        bands = m.sb("o_bands", [P, HEADS, BAND])
        v = m.sb("o_v", [P, NT, C])
        res = m.sb("o_res", [P, NT, C])
        xnT = [m.sb(f"o_xnT{k}", [C, 512]) for k in range(4)]
        bs = [m.sb(f"o_base{k}", [P, GT, C]) for k in range(4)]
        kbd = m.sb("o_kbd", [C, HEADS * LM])
        wk = m.sb("o_wk", [C, HEADS * LM])
        wk_lp = m.sb("o_wk_lp", [C, HEADS * LM], BF16)
        zb = m.sb("o_zb", [P, PAIRS_H, 2 * DH])
        onesb = m.sb("o_onesb", [P, 2 * DH])
        ind = m.sb("o_ind", [HEADS, HEADS, LM], BF16)
        xn_lp = m.sb("o_xn_lp", [C, 512], BF16)
        m1 = m.sb("o_m1", [P, GT, HEADS])
        negm = [m.sb(f"o_negm{k}", [HEADS, 512], BF16) for k in range(2)]
        p1 = [m.sb(f"o_p1{k}", [P, 512]) for k in range(4)]
        rden = m.sb("o_rden", [C, 512])
        att = m.sb("o_att", [C, 512])
        oT = m.sb("o_oT", [C, 512])
        t2s = [m.sb(f"o_t2{k}", [P, GT, C]) for k in range(2)]
        z = m.sb("o_z", [P, GT, C])
        zT = m.sb("o_zT", [C, 512])
        wxs = [m.sb(f"o_wx{k}", [C, 512]) for k in range(2)]
        st = m.sb("o_st", [P, GT, 6])
        fst = m.sb("o_fst", [C, NG, 6])
        half = m.sb("o_half", [P, GT])
        eps = m.sb("o_eps", [P, GT])
        mv = m.sb("o_mv", [P, GT, 2])
        vare = m.sb("o_vare", [P, GT])
        r = m.sb("o_r", [P, GT])
        bank_q = m.ps("o_bank_q", [C, 512])
        bank_l = [m.ps(f"o_bank_l{k}", [P, 512]) for k in range(2)]
        bank_s = [m.ps(f"o_bank_s{k}", [P, 512]) for k in range(2)]
        bank_pv = m.ps("o_bank_pv", [C, 512])
        bank_den = m.ps("o_bank_den", [C, 512])
        bank_m = m.ps("o_bank_m", [P, GT, P])

        names = """w const ones v conv convc setup turnw copyw wkm wk xr lp max mt neg s1 exp pv ct rec add wo res
                   z bn pow zt ztc wxm wxc fst stats""".split()
        s = {n: sems.sem("o_" + n) for n in names}
        credit = dict(convc=0, neg=1, max=2, exp=4, pv=4, rec=2, wo=1, s1=8, lp=1, mt=1, zt=1, wxm=1, fst=2,
                      ct=1, ztc=1, wxc=2, add=1, bn=1)
        s_band = sems.sem("o_band")
        s_xl = [sems.sem(f"o_xl{k}") for k in range(4)]
        s_bl = [sems.sem(f"o_bl{k}") for k in range(4)]
        s_t2 = [sems.sem(f"o_t2st{k}") for k in range(2)]
        s_wx = [sems.sem(f"o_wxst{k}") for k in range(2)]
        SETUP = 4

        def nth(b, c):
            return NG * b + c + 1

        def start_counts(eng, *names):
            for n in names:
                eng.sem_inc(s[n], credit[n])

        def wait(eng, name, count):
            eng.wait_ge(s[name], credit.get(name, 0) + count)

        block = ctx.enter_context(nc.Block())

        @block.sync
        def _(sp):
            for q in range(2):
                sp.sem_inc(s_t2[q], 16)
                sp.sem_inc(s_wx[q], 16)
            for dst, src in ((w[:, :], wqkv[:, 0:C]), (wo[:, :], w_out), (fw[:, :], ffn_wT)):
                sp.dma_start(dst, src).then_inc(s["w"], 16)
            sp.wait_ge(s["const"], 1)
            sp.dma_start(band.rearrange("h p c -> p h c"), bands[:, :, :]).then_inc(s_band, 16)
            sp.wait_ge(s_band, 16)
            for h in range(HEADS):
                diagonals = bass.AP(tensor=band.tensor, offset=band.offset + h * P * BAND + EDGE - TAPS // 2,
                                    ap=[[BAND + 1, P], [1, TAPS]])
                sp.dma_start(diagonals, taps[h:h + 1, :].broadcast_to([P, TAPS])).then_inc(s_band, 16)
            sp.wait_ge(s_band, 16 * (HEADS + 1))
            sp.dma_start(bands[:, :, :], band.rearrange("h p c -> p h c")).then_inc(s_band, 16)

            def load_v(b):
                for g in range(NG):
                    sp.dma_start(v[:, GT * g:GT * g + GT, :], vals[b, 512 * g:512 * g + 512, :].rearrange("(n p) c -> p n c", p=P)
                                 ).then_inc(s["v"], 16)

            def load_chunk(b, c):
                sp.dma_start(xnT[c % 4][:, :], xnt[b, :, 512 * c:512 * c + 512]).then_inc(s_xl[c % 4], 16)
                sp.dma_start(bs[c % 4][:, :, :], base[b, 512 * c:512 * c + 512, :].rearrange("(n p) c -> p n c", p=P)
                             ).then_inc(s_bl[c % 4], 16)

            def stores(b, c):
                sp.wait_ge(s["res"], nth(b, c))
                sp.dma_start(t2[b, 512 * c:512 * c + 512, :].rearrange("(n p) c -> p n c", p=P), t2s[c % 2][:, :, :]
                             ).then_inc(s_t2[c % 2], 16)
                wait(sp, "wxc", nth(b, c))
                sp.dma_start(wx[b, :, 512 * c:512 * c + 512], wxs[c % 2][:, :]).then_inc(s_wx[c % 2], 16)

            def image(b, more):
                for c in range(NG):
                    if c == 1 and more:
                        sp.wait_ge(s["conv"], HEADS * (b + 1))
                        load_v(b + 1)
                    stores(b, c)
                    if c < NG - 4:
                        load_chunk(b, c + 4)
                    elif more:
                        load_chunk(b + 1, c - 4)
            load_v(0)
            for c in range(4):
                load_chunk(0, c)
            with sp.Fori(0, B - 1) as b:
                image(b, True)
            image(B - 1, False)
            for q in range(2):
                sp.wait_ge(s_t2[q], 16 * (1 + B * NG // 2))
                sp.wait_ge(s_wx[q], 16 * (1 + B * NG // 2))

        @block.gpsimd
        def _(pool):
            pool.memset(bands[:, :, :], 0.0).then_inc(s["const"], 1)
            pool.memset(zb[:, :, :], 0.0).then_inc(s["ones"], 1)
            pool.memset(onesb[:, :], 0.0).then_inc(s["ones"], 1)
            pool.memset(half[:, :], -0.5).then_inc(s["ones"], 1)
            pool.memset(eps[:, :], EPS).then_inc(s["ones"], 1)
            pool.memset(ind[:, :, :], 0.0).then_inc(s["ones"], 1)
            pool.wait_ge(s["ones"], 5)
            for h in range(2):
                pool.memset(onesb[LM * h:LM * h + LM, DH * h:DH * h + DH], 1.0).then_inc(s["ones"], 1)
            pool.affine_select(out=ind[:, :, :], in_=ind[:, :, :], compare_op=ALU.not_equal, fill=1.0, base=0,
                               pattern=[[-1, HEADS], [0, LM]], channel_multiplier=1).then_inc(s["ones"], 1)

            def image(b):
                for c in range(NG):
                    wait(pool, "bn", nth(b, c))
                    pool.tensor_tensor(vare[:, :], mv[:, :, 1], eps[:, :], ALU.add).then_inc(s["pow"], 1)
                    pool.wait_ge(s["pow"], 2 * nth(b, c) - 1)
                    pool.tensor_tensor(r[:, :], vare[:, :], half[:, :], ALU.pow).then_inc(s["pow"], 1)
            with pool.Fori(0, B) as b:
                image(b)

        @block.tensor
        def _(pe):
            start_counts(pe, "pv", "wo", "s1", "lp", "mt", "zt", "wxm", "ct")
            pe.wait_ge(s["w"], 48)
            pe.wait_ge(s["ones"], 8)
            pe.wait_ge(s_band, 16 * (HEADS + 2))
            nc.tensor.transpose(bank_q[:, 0:C], w[:, :], R.ident[:, :]).then_inc(s["turnw"], 1)
            pe.wait_ge(s["copyw"], 1)

            def weights(b):
                pe.wait_ge(s["setup"], SETUP * b + 1)
                wait(pe, "wxc", NG * b - 1)
                nc.tensor.matmul(bank_q[:, :], wT[:, :], kbd[:, :], start=True, stop=True).then_inc(s["wkm"], 1)

            def convolve(b, first):
                pe.wait_ge(s["v"], 16 * NG * (b + 1))
                for h in range(HEADS):
                    ch = slice(DH * h, DH * h + DH)
                    out = bank_l[h % 2]
                    if h < 2:
                        wait(pe, ("neg", "max")[h], (NG * b, NT * b)[h])
                    else:
                        wait(pe, "convc", HEADS * b + h - 1)
                    nc.tensor.matmul(out[:, :], bands[:, h, EDGE:EDGE + P], v[:, :, ch], start=True, stop=False,
                                     skip_group_check=True)
                    nc.tensor.matmul(out[P - EDGE:P, 0:(NT - 1) * DH], bands[:, h, 0:EDGE], v[:, 1:NT, ch],
                                     start=False, stop=False, skip_group_check=True)
                    nc.tensor.matmul(out[0:EDGE, DH:NT * DH], bands[:, h, EDGE + P:BAND], v[:, 0:NT - 1, ch],
                                     start=False, stop=True, skip_group_check=True).then_inc(s["conv"], 1)
                    if h == 1 and not first:
                        project(b, -1)
                    if h == 2:
                        weights(b)
                    if h == 5 and not first:
                        turn_normed(b, -1)
                if not first:
                    ffn(b, -1)

            def row_maxima(b, c, k):
                if k == 0:
                    wait(pe, "xr", nth(b, c))
                    wait(pe, "neg", nth(b, c) - 1)
                wait(pe, "max", GT * (NG * b + c) + k - 1)
                nc.tensor.matmul(bank_l[k % 2][:, :], xn_lp[:, P * k:P * k + P], wk_lp[:, :], start=True, stop=True
                                 ).then_inc(s["lp"], 1)

            def turn_maxima(b, c):
                wait(pe, "max", GT * nth(b, c))
                for k in range(GT):
                    mt = nc.tensor.transpose(bank_l[0][0:HEADS, P * k:P * k + P], m1[:, k, :], R.ident[:, :])
                mt.then_inc(s["mt"], 1)

            def attend(b, c):
                wait(pe, "neg", nth(b, c))
                for g in range(PAIRS_H + 1):
                    i = PAIRS_H * (NG * b + c) + g
                    if g < PAIRS_H:
                        wait(pe, "exp", i - 1)
                        nc.tensor.matmul(bank_s[g % 2][:, :], wk[:, P * g:P * g + P], xnT[c % 4][:, :], start=True, stop=False)
                        nc.tensor.matmul(bank_s[g % 2][:, :], ind[:, 2 * g:2 * g + 2, :].rearrange("h a l -> h (a l)"),
                                         negm[c % 2][:, :], start=False, stop=True).then_inc(s["s1"], 1)
                    if g == 1 and c:
                        project(b, c - 1)
                    if g:
                        h = g - 1
                        wait(pe, "exp", i)
                        if h == 0:
                            wait(pe, "rec", 2 * (NG * b + c))
                        rows = slice(2 * DH * h, 2 * DH * h + 2 * DH)
                        nc.tensor.matmul(bank_pv[rows, :], zb[:, h, :], p1[h][:, :], start=True, stop=True)
                        nc.tensor.matmul(bank_den[rows, :], onesb[:, :], p1[h][:, :], start=True, stop=True).then_inc(s["pv"], 1)
                    if c + 1 < NG and g >= 2:
                        row_maxima(b, c + 1, g - 2)
                if c + 1 < NG:
                    row_maxima(b, c + 1, GT - 1)

            def turn_normed(b, c):
                wait(pe, "z", nth(b, c))
                for k in range(GT):
                    mt = nc.tensor.transpose(bank_m[:, k, :], z[:, k, :], R.ident[:, :])
                mt.then_inc(s["zt"], 1)

            def turn_convolved(b, c):
                wait(pe, "convc", HEADS * (b + 1))
                wait(pe, "ztc", NG * b + c)
                for k in range(GT):
                    mt = nc.tensor.transpose(bank_m[:, k, :], res[:, GT * c + k, :], R.ident[:, :])
                mt.then_inc(s["ct"], 1)

            def project(b, c):
                wait(pe, "add", nth(b, c))
                for k in range(GT):
                    mt = nc.tensor.matmul(bank_m[:, k, :], oT[:, P * k:P * k + P], wo[:, :], start=True, stop=True)
                mt.then_inc(s["wo"], 1)

            def ffn(b, c):
                wait(pe, "ztc", nth(b, c))
                if c == -1:
                    pe.wait_ge(s["wk"], b + 1)
                else:
                    wait(pe, "wxc", nth(b, c) - 1)
                nc.tensor.matmul(bank_q[:, :], fw[:, :], zT[:, :], start=True, stop=True).then_inc(s["wxm"], 1)

            def image(b, first):
                convolve(b, first)
                pe.wait_ge(s["setup"], SETUP * (b + 1))
                wait(pe, "convc", HEADS * (b + 1))
                for k in range(GT):
                    row_maxima(b, 0, k)
                turn_maxima(b, 0)
                for c in range(NG):
                    attend(b, c)
                    if c:
                        turn_normed(b, c - 1)
                    turn_convolved(b, c)
                    if c + 1 < NG:
                        turn_maxima(b, c + 1)
                    if c:
                        ffn(b, c - 1)
            image(0, True)
            with pe.Fori(1, B) as b:
                image(b, False)
            project(B - 1, NG - 1)
            turn_normed(B - 1, NG - 1)
            ffn(B - 1, NG - 1)

        @block.scalar
        def _(act):
            start_counts(act, "neg", "exp", "ztc", "wxc")

            act.wait_ge(s["turnw"], 1)
            nc.scalar.activation(wT[:, :], bank_q[:, 0:C], ACT.Copy).then_inc(s["copyw"], 1)

            def negate(b, c):
                wait(act, "mt", nth(b, c))
                nc.scalar.activation(negm[c % 2][:, :], bank_l[0][0:HEADS, :], ACT.Copy, scale=-1.0).then_inc(s["neg"], 1)

            def copy_normed(b, c):
                wait(act, "zt", nth(b, c))
                wait(act, "wxm", nth(b, c) - 1)
                nc.scalar.activation(zT[:, :], bank_m[:, :, :].rearrange("c k t -> c (k t)"), ACT.Copy).then_inc(s["ztc"], 1)

            def copy_wx(b, c):
                q = c % 2
                wait(act, "wxm", nth(b, c))
                wait(act, "fst", nth(b, c) - 2)
                act.wait_ge(s_wx[q], 16 + 16 * (NG // 2 * b + c // 2))
                nc.scalar.activation(wxs[q][:, :], bank_q[:, :], ACT.Copy).then_inc(s["wxc"], 1)

            def image(b, first):
                wait(act, "ct", NG * b)
                for h in range(HEADS):
                    wait(act, "conv", HEADS * b + h + 1)
                    nc.scalar.activation(res[:, :, DH * h:DH * h + DH], bank_l[h % 2][:, :].rearrange("p (n d) -> p n d", d=DH),
                                         ACT.Copy).then_inc(s["convc"], 1)
                    if h == 2:
                        act.wait_ge(s["wkm"], b + 1)
                        nc.scalar.activation(wk[:, :], bank_q[:, :], ACT.Copy, scale=DH ** -0.5).then_inc(s["wk"], 1)
                    if h == 5 and not first:
                        copy_normed(b, -1)
                if not first:
                    copy_wx(b, -1)
                negate(b, 0)
                for c in range(NG):
                    for g in range(PAIRS_H):
                        i = PAIRS_H * (NG * b + c) + g
                        wait(act, "s1", i + 1)
                        wait(act, "pv", i - 3)
                        nc.scalar.activation(p1[g][:, :], bank_s[g % 2][:, :], ACT.Exp).then_inc(s["exp"], 1)
                    if c:
                        copy_normed(b, c - 1)
                    if c + 1 < NG:
                        negate(b, c + 1)
                    if c:
                        copy_wx(b, c - 1)
            image(0, True)
            with act.Fori(1, B) as b:
                image(b, False)
            copy_normed(B - 1, NG - 1)
            copy_wx(B - 1, NG - 1)

        @block.vector
        def _(dve):
            start_counts(dve, "max", "rec", "fst", "add", "bn")
            dve.wait_ge(s["ones"], 8)

            def set_up(b, first):
                wait(dve, "pv", NT * b)
                nc.vector.tensor_tensor(kbd[:, :].rearrange("c (h l) -> c h l", l=LM), R.head_mask[:, :, :],
                                        R.k_lm[:, bass.ds(b, 1), :].broadcast_to([C, HEADS, LM]), ALU.mult).then_inc(s["setup"], 1)
                for h in range(2):
                    rows = slice(LM * h, LM * h + LM)
                    nc.vector.tensor_scalar(zb[rows, :, DH * h:DH * h + DH], R.ctx[rows, bass.ds(b, 1), :, :].rearrange("p a g d -> p (a g) d"),
                                            1.0, None, ALU.mult).then_inc(s["setup"], 1)
                if not first:
                    residual(b, -1)
                dve.wait_ge(s["wk"], b + 1)
                nc.vector.tensor_copy(wk_lp[:, :], wk[:, :]).then_inc(s["setup"], 1)

            def round_tokens(b, c):
                dve.wait_ge(s_xl[c % 4], 16 * (2 * b + c // 4 + 1))
                wait(dve, "lp", GT * (NG * b + c))
                nc.vector.tensor_copy(xn_lp[:, :], xnT[c % 4][:, :]).then_inc(s["xr"], 1)

            def maxima(b, c, tiles):
                wait(dve, "mt", NG * b + c)
                for k in tiles:
                    wait(dve, "lp", GT * (NG * b + c) + k + 1)
                    nc.vector.tensor_reduce(m1[:, k, :], bank_l[k % 2][:, :].rearrange("p (h l) -> p h l", l=LM), AX.X, ALU.max
                                            ).then_inc(s["max"], 1)

            def residual(b, c):
                out = t2s[c % 2]
                wait(dve, "wo", nth(b, c))
                dve.wait_ge(s_bl[c % 4], 16 * (2 * b + c // 4 + 1))
                dve.wait_ge(s_t2[c % 2], 16 + 16 * (NG // 2 * b + c // 2))
                nc.vector.tensor_tensor(out[:, :, :], bank_m[:, :, :], bs[c % 4][:, :, :], ALU.add).then_inc(s["res"], 1)
                wait(dve, "res", nth(b, c))
                for k in range(GT):
                    nc.vector.bn_stats(st[:, k, :], out[:, k, :])
                dve.drain()
                for k in range(GT):
                    ms = nc.vector.bn_aggr(mv[:, k, :], st[:, k:k + 1, :])
                ms.then_inc(s["bn"], 1)

            def norm(b, c):
                out = t2s[c % 2]
                wait(dve, "bn", nth(b, c))
                wait(dve, "pow", 2 * nth(b, c))
                wait(dve, "zt", nth(b, c) - 1)
                for k in range(GT):
                    mz = nc.vector.tensor_scalar(z[:, k, :], out[:, k, :], mv[:, k, 0:1], r[:, k:k + 1], ALU.subtract, ALU.mult)
                mz.then_inc(s["z"], 1)

            def statistics(b, c):
                wait(dve, "wxc", nth(b, c))
                nc.vector.bn_stats(fst[:, c % NG, :], wxs[c % 2][:, :]).then_inc(s["fst"], 1)
                if c % NG == NG - 1:
                    wait(dve, "fst", nth(b, c))
                    at = b - 1 if c < 0 else b
                    nc.vector.tensor_scalar(wx_stats[:, bass.ds(at, 1), :], fst[:, :, :].rearrange("c k s -> c (k s)").unsqueeze(1),
                                            1.0, None, ALU.mult).then_inc(s["stats"], 1)

            def image(b, first):
                set_up(b, first)
                round_tokens(b, 0)
                if not first:
                    norm(b, -1)
                    statistics(b, -1)
                maxima(b, 0, range(GT))
                for c in range(NG):
                    if c + 1 < NG:
                        round_tokens(b, c + 1)
                    if c:
                        residual(b, c - 1)
                    if c + 1 < NG:
                        maxima(b, c + 1, range(2))
                    if c:
                        norm(b, c - 1)
                    if c + 1 < NG:
                        maxima(b, c + 1, range(2, GT))
                    wait(dve, "pv", PAIRS_H * nth(b, c))
                    nc.vector.reciprocal(rden[:, :], bank_den[:, :]).then_inc(s["rec"], 1)
                    wait(dve, "rec", 2 * (NG * b + c) + 1)
                    wait(dve, "add", nth(b, c) - 1)
                    nc.vector.tensor_tensor(att[:, :], bank_pv[:, :], rden[:, :], ALU.mult).then_inc(s["rec"], 1)
                    wait(dve, "rec", 2 * nth(b, c))
                    wait(dve, "ct", nth(b, c))
                    wait(dve, "wo", nth(b, c) - 1)
                    nc.vector.tensor_tensor(oT[:, :], att[:, :], bank_m[:, :, :].rearrange("c k t -> c (k t)"), ALU.add
                                            ).then_inc(s["add"], 1)
                    if c:
                        if c == 1 and not first:
                            dve.wait_ge(s["stats"], b)
                        statistics(b, c - 1)
            image(0, True)
            with dve.Fori(1, B) as b:
                image(b, False)
            residual(B - 1, NG - 1)
            norm(B - 1, NG - 1)
            statistics(B - 1, NG - 1)


RT = P
RC = 32
CHUNKS = RT // RC
BLOCKS = TOK // RT
PIECES = 4
PT = RC // PIECES
FILL = 256


def recurrence_phase(nc, sems, t2, wx, wx_stats, ffn_v_t, gamma, beta, out):
    with ExitStack() as ctx:
        m = Memory(nc, ctx)
        vT = m.sb("f_vT", [C, C])
        gam = m.sb("f_gamma", [C, 1])
        bet = m.sb("f_beta", [C, 1])
        ident = m.sb("f_ident", [P, P])
        mv = m.sb("f_mv", [C, 2])
        vare = m.sb("f_vare", [C, 1])
        half = m.sb("f_half", [C, 1])
        rstd = m.sb("f_rstd", [C, 1])
        scale = m.sb("f_scale", [C, 1])
        moved = m.sb("f_moved", [C, 1])
        shift = m.sb("f_shift", [C, 1])
        wxb = [m.sb(f"f_wx{q}", [C, B, RT]) for q in range(2)]
        t2b = [m.sb(f"f_t2{q}", [P, B, C]) for q in range(2)]
        y = [m.sb(f"f_y{q}", [C, RT, B]) for q in range(2)]
        sums = [m.sb(f"f_sum{q}", [P, B, C]) for q in range(2)]
        idle = m.sb("f_idle", [C, FILL], BF16)
        acc = [m.ps(f"f_acc{k}", [C, RC, B]) for k in range(2)]
        turned = [m.ps(f"f_turned{k}", [P, 4, C]) for k in range(2)]
        junk = m.ps("f_junk", [C, FILL])

        s_w = sems.sem("f_weights")
        s_const = sems.sem("f_const")
        s_bn = sems.sem("f_bn")
        s_rstd = sems.sem("f_rstd")
        s_wx = [sems.sem(f"f_wx{q}") for q in range(2)]
        s_t2 = [sems.sem(f"f_t2{q}") for q in range(2)]
        s_norm = sems.sem("f_norm")
        s_pre = sems.sem("f_pre")
        s_mm = sems.sem("f_mm")
        s_y = sems.sem("f_y")
        s_turn = sems.sem("f_turn")
        s_sum = sems.sem("f_sum")
        s_out = [sems.sem(f"f_out{q}") for q in range(2)]
        GR = B // 4
        TURN0, SUM0 = 2 * GR, 2

        block = ctx.enter_context(nc.Block())

        def each_pair(eng, body):
            for q in range(2):
                body(q, q, q == 0, False)
            with eng.Fori(1, BLOCKS // 2 - 1) as i:
                for q in range(2):
                    body(2 * i + q, q, False, False)
            for q in range(2):
                body(BLOCKS - 2 + q, q, False, q == 1)

        @block.sync
        def _(sp):
            for dst, src in ((vT[:, :], ffn_v_t), (gam[:, :], gamma.rearrange("(p a) -> p a", a=1)),
                             (bet[:, :], beta.rearrange("(p a) -> p a", a=1))):
                sp.dma_start(dst, src).then_inc(s_w, 16)
            for q in range(2):
                sp.sem_inc(s_out[q], 16 * GR)

            def load_wx(T, q):
                for g in range(GR):
                    sp.dma_start(wxb[q][:, 4 * g:4 * g + 4, :], wx[4 * g:4 * g + 4, :, bass.ds(T * RT, RT)].rearrange("b c t -> c b t")
                                 ).then_inc(s_wx[q], 16)

            def load_t2(T, q):
                for g in range(GR):
                    sp.dma_start(t2b[q][:, 4 * g:4 * g + 4, :], t2[4 * g:4 * g + 4, bass.ds(T * RT, RT), :].rearrange("b p c -> p b c")
                                 ).then_inc(s_t2[q], 16)

            def store(T, q):
                for g in range(GR):
                    sp.wait_ge(s_sum, SUM0 + GR * T + g + 1)
                    sp.dma_start(out[4 * g:4 * g + 4, bass.ds(T * RT, RT), :].rearrange("b p c -> p b c"), sums[q][:, 4 * g:4 * g + 4, :]
                                 ).then_inc(s_out[q], 16)

            def body(T, q, first, last):
                if not first:
                    store(T - 1, 1 - q)
                if not last:
                    load_t2(T + 1, 1 - q)
                if not isinstance(T, int) or T + 2 < BLOCKS:
                    sp.wait_ge(s_pre, CHUNKS * (T + 1))
                    load_wx(T + 2, q)
            load_wx(0, 0)
            load_wx(1, 1)
            load_t2(0, 0)
            each_pair(sp, body)
            store(BLOCKS - 1, 1)
            for q in range(2):
                sp.wait_ge(s_out[q], 16 * GR * (1 + BLOCKS // 2))

        @block.gpsimd
        def _(pool):
            make_identity(pool, ident, s_const)
            pool.memset(half[:, :], -0.5).then_inc(s_const, 1)
            pool.memset(idle[:, :], 0.0).then_inc(s_const, 1)
            pool.wait_ge(s_const, 4)
            pool.wait_ge(s_bn, 2)
            pool.tensor_tensor(rstd[:, :], vare[:, :], half[:, :], ALU.pow).then_inc(s_rstd, 1)

        @block.vector
        def _(dve):
            dve.sem_inc(s_sum, SUM0)
            nc.vector.memset(y[1][:, RT - 1, :], 0.0).then_inc(s_y, 1)
            nc.vector.bn_aggr(mv[:, :], wx_stats[:, :, :].rearrange("c b (k s) -> c (b k) s", s=6)).then_inc(s_bn, 1)
            dve.wait_ge(s_bn, 1)
            nc.vector.tensor_scalar(vare[:, :], mv[:, 1:2], EPS, None, ALU.add).then_inc(s_bn, 1)
            dve.wait_ge(s_w, 48)
            dve.wait_ge(s_rstd, 1)
            nc.vector.tensor_tensor(scale[:, :], rstd[:, :], gam[:, :], ALU.mult).then_inc(s_bn, 1)
            dve.wait_ge(s_bn, 3)
            nc.vector.tensor_tensor(moved[:, :], mv[:, 0:1], scale[:, :], ALU.mult).then_inc(s_bn, 1)
            dve.wait_ge(s_bn, 4)
            nc.vector.tensor_tensor(shift[:, :], bet[:, :], moved[:, :], ALU.subtract).then_inc(s_bn, 1)
            dve.wait_ge(s_bn, 5)

            def normalise(T, q):
                dve.wait_ge(s_wx[q], 16 * GR * (T // 2 + 1) if isinstance(T, int) else 8 * GR * (T - q) + 16 * GR)
                nc.vector.tensor_scalar(wxb[q][:, :, :], wxb[q][:, :, :], scale[:, 0:1], shift[:, 0:1], ALU.mult, ALU.add
                                        ).then_inc(s_norm, 1)

            def add(T, q):
                pair = 8 * GR * (T - q) + 16 * GR
                dve.wait_ge(s_t2[q], pair)
                dve.wait_ge(s_out[q], pair)
                for g in range(GR):
                    dve.wait_ge(s_turn, TURN0 + GR * T + g + 1)
                    at = slice(4 * g, 4 * g + 4)
                    nc.vector.tensor_tensor(sums[q][:, at, :], turned[g % 2][:, :, :], t2b[q][:, at, :], ALU.add).then_inc(s_sum, 1)

            def body(T, q, first, last):
                if not last:
                    normalise(T + 1, 1 - q)
                if not first:
                    add(T - 1, 1 - q)
            normalise(0, 0)
            each_pair(dve, body)
            add(BLOCKS - 1, 1)

        @block.tensor
        def _(pe):
            pe.sem_inc(s_turn, TURN0)
            pe.wait_ge(s_w, 48)
            pe.wait_ge(s_const, 4)

            def lay(T, q, k, piece):
                if piece == 0 and k == 0:
                    pe.wait_ge(s_norm, T + 1)
                at = slice(RC * k + PT * piece, RC * k + PT * piece + PT)
                mm = nc.tensor.matmul(acc[k % 2][:, PT * piece:PT * piece + PT, :], ident[:, :],
                                      wxb[q][:, :, at].rearrange("c b t -> c t b"), start=piece == 0, stop=False,
                                      skip_group_check=True)
                if piece == PIECES - 1:
                    mm.then_inc(s_pre, 1)

            def turn(T, q, b):
                g = b // 4
                if b % 4 == 0:
                    pe.wait_ge(s_sum, GR * T + g + 1)
                mt = nc.tensor.transpose(turned[g % 2][:, b % 4, :], y[q][:, :, b], ident[:, :])
                if b % 4 == 3:
                    mt.then_inc(s_turn, 1)

            def body(T, q, first, last):
                for u in range(RT):
                    k, t = u // RC, u % RC
                    pe.wait_ge(s_y, RT * T + u + 1)
                    before = y[q][:, u - 1, :] if u else y[1 - q][:, RT - 1, :]
                    for g in range(4):
                        rows = slice(32 * g, 32 * g + 32)
                        mm = nc.tensor.matmul(acc[k % 2][rows, t, :], vT[:, rows], before, start=False, stop=True,
                                              skip_group_check=True)
                    mm.then_inc(s_mm, 1)
                    work = 0
                    if t % 2 == 0 and t // 2 < PIECES and not (last and k == CHUNKS - 1):
                        work = 1
                        if k < CHUNKS - 1:
                            lay(T, q, k + 1, t // 2)
                        else:
                            lay(T + 1, 1 - q, 0, t // 2)
                    b = 4 * k + (t - 2 * PIECES) // 4
                    if not first and 2 * PIECES <= t < 2 * PIECES + 16 and t % 4 == 0:
                        work = 1
                        turn(T - 1, 1 - q, b)
                    for _ in range(3 - work):
                        nc.tensor.matmul(junk[:, :], idle[:, 0:P], idle[:, :], start=True, stop=True)

            for piece in range(PIECES):
                lay(0, 0, 0, piece)
            each_pair(pe, body)
            pe.wait_ge(s_y, TOK + 1)
            for b in range(B):
                turn(BLOCKS - 1, 1, b)

        @block.scalar
        def _(act):
            def body(T, q, first, last):
                act.wait_ge(s_turn, GR * T + GR)
                for u in range(RT):
                    act.wait_ge(s_mm, RT * T + u + 1)
                    nc.scalar.activation(y[q][:, u, :], acc[u // RC % 2][:, u % RC, :], ACT.Sigmoid).then_inc(s_y, 1)
            each_pair(act, body)


WEIGHTS = ["wf0", "uf0", "bf0", "wf1", "uf1", "bf1", "wi", "ui", "bi", "wo", "uo", "bo", "wc", "uc", "bc"]


def program(nc, args, out):
    def scratch(name, shape):
        return nc.dram_tensor(name, shape, F32, kind="Internal").ap()

    skew = scratch("skew", (LANES, C, STEPS * G))
    hidden = scratch("hidden", (LANES, C, STEPS * SLOT))
    xnt = scratch("xnt", (B, C, TOK))
    base = scratch("base", (B, TOK, C))
    vals = scratch("vals", (B, TOK, C))
    band = scratch("band", (HEADS, P, BAND))
    t2 = scratch("t2", (B, TOK, C))
    wx = scratch("wx", (B, C, TOK))
    lstm = {n: args["L0_conv_" + n] for n in WEIGHTS}
    attn = {n: args["L1_attn_" + n] for n in ("gamma", "beta", "w_qkv", "w_out", "b_out", "conv_w")}
    with ExitStack() as ctx:
        sems = Memory(nc, ctx)
        group_norm_phase(nc, sems, args["x"], skew)
        lstm_phase(nc, sems, skew, hidden, lstm, lstm)
        wx_stats = sems.sb("wx_stats", [C, B, NG * 6])
        with ExitStack() as attention:
            R = Resident(Memory(nc, attention))
            landmark_phase(nc, sems, R, args["x"], hidden, attn["w_qkv"], attn["gamma"], attn["beta"], attn["b_out"],
                           xnt, base, vals)
            pinv_phase(nc, sems, R)
            output_phase(nc, sems, R, xnt, base, vals, band, attn["conv_w"], attn["w_qkv"], attn["w_out"],
                         args["L1_ffn_W"], t2, wx, wx_stats)
        recurrence_phase(nc, sems, t2, wx, wx_stats, args["L1_ffn_V"], args["L1_ffn_gamma"], args["L1_ffn_beta"], out)


def kernel(**inputs):
    import numpy as np
    import concourse.bacc as bacc
    from concourse.bass_utils import run_bass_kernel_spmd

    nc = bacc.Bacc("TRN2", target_bir_lowering=False, num_devices=1)
    arrays, args = {}, {}
    for name, value in inputs.items():
        a = np.asarray(value)
        if name == "x":
            a = a.reshape(B, TOK, C)
        elif name == "L1_attn_conv_w":
            a = a[:, 0, ::-1, 0]
        elif name in ("L1_ffn_W", "L1_ffn_V"):
            a = a.T
        arrays[f"in_{name}"] = np.ascontiguousarray(a)
        args[name] = nc.dram_tensor(f"in_{name}", a.shape, mybir.dt.from_np(a.dtype), kind="ExternalInput").ap()
    out = nc.dram_tensor("out", (B, TOK, C), F32, kind="ExternalOutput").ap()
    program(nc, args, out)
    r = run_bass_kernel_spmd(nc, [arrays], core_ids=[0])
    return np.asarray(r.results[0]["out"]).reshape(B, G, G, C)
```

```python
from contextlib import ExitStack

import concourse.bass as bass
from concourse import mybir

F32 = mybir.dt.float32
BF16 = mybir.dt.bfloat16
ALU = mybir.AluOpType
ACT = mybir.ActivationFunctionType
AX = mybir.AxisListType

P = 128
B = 16
G = 64
C = 128
TOK = G * G
NT = TOK // P
SETS = 2
LANES = B // SETS
CHAINS = 2
LPC = LANES // CHAINS
PERIOD = G + 1
WIN = 8
STEPS = 192
SLOT = G + 1
GN_GROUP = 4
EPS = 1e-5


class Memory:

    def __init__(self, nc, ctx):
        self.nc, self.ctx = nc, ctx

    def sb(self, name, shape, dt=F32):
        return self.ctx.enter_context(self.nc.sbuf_tensor(name, shape, dt))

    def ps(self, name, shape, dt=F32):
        return self.ctx.enter_context(self.nc.psum_tensor(name, shape, dt))

    def sem(self, name):
        return self.ctx.enter_context(self.nc.semaphore(name))


def strided(start, dims):
    return bass.AP(tensor=start.tensor, offset=start.offset, ap=[start.ap[0], *dims])


def make_identity(pool, ident, sem):
    pool.memset(ident[:, :], 0.0).then_inc(sem, 1)
    pool.wait_ge(sem, 1)
    pool.affine_select(out=ident[:, :], in_=ident[:, :], compare_op=ALU.not_equal, fill=1.0,
                       base=0, pattern=[[-1, P]], channel_multiplier=1).then_inc(sem, 1)


def group_norm_phase(nc, sems, x, skew):
    with ExitStack() as ctx:
        m = Memory(nc, ctx)
        xin = [m.sb(f"gn_x{s}", [P, NT, C]) for s in range(SETS)]
        D = [m.sb(f"gn_skew{q}", [P, STEPS * G]) for q in range(2)]
        ident = m.sb("gn_ident", [P, P])
        avg = m.sb("gn_avg", [P, P])
        stats = m.sb("gn_stats", [P, 8, 6])
        mv = m.sb("gn_mv", [P, 2])
        gmean = m.sb("gn_gmean", [P, 1])
        dev = m.sb("gn_dev", [P, 1])
        spread = m.sb("gn_spread", [P, 1])
        veps = m.sb("gn_veps", [P, 1])
        rstd = m.sb("gn_rstd", [P, 1])
        minus_half = m.sb("gn_minus_half", [P, 1])
        shift = m.sb("gn_shift", [P, 1])
        turned = [m.ps(f"gn_turned{k}", [P, 4, P]) for k in range(4)]
        group = m.ps("gn_group", [P, 512])

        s_const = sems.sem("gn_const")
        s_avg = sems.sem("gn_avg")
        s_clear = sems.sem("gn_clear")
        s_load = [sems.sem(f"gn_load{s}") for s in range(SETS)]
        s_turned = sems.sem("gn_turned")
        s_copied = sems.sem("gn_copied")
        s_vec = sems.sem("gn_vec")
        s_group = sems.sem("gn_group")
        s_rstd = sems.sem("gn_rstd")
        s_store = [sems.sem(f"gn_store{q}") for q in range(2)]
        VS = 9 + 6

        def chunk(q, s, k):
            return strided(D[q][:, (PERIOD * s + 4 * k) * G:(PERIOD * s + 4 * k) * G + 1],
                           [[G, 4], [G + 1, G], [G * NT, 2]])

        def image(q, s):
            return strided(D[q][:, PERIOD * s * G:PERIOD * s * G + 1], [[G + 1, G], [G, G]])

        block = ctx.enter_context(nc.Block())

        @block.sync
        def _(sp):
            def load(q, s, it):
                sp.dma_start(xin[s][:, :, :], x[8 * s + 2 * it + q].rearrange("(p n) c -> p n c", n=NT)
                             ).then_inc(s_load[s], 16)

            with sp.Fori(0, LANES // 2) as it:
                for q in range(2):
                    for s in range(SETS):
                        sp.wait_ge(s_turned, 32 * it + 16 * q + 8 * s + 8)
                        load(q, s, it)

        @block.gpsimd
        def _(pool):
            make_identity(pool, ident, s_const)
            pool.memset(avg[:, :], 1.0 / GN_GROUP).then_inc(s_avg, 1)
            pool.wait_ge(s_avg, 1)
            v = avg[:, :].rearrange("p (g k) -> p g k", k=GN_GROUP)
            pool.affine_select(out=v, in_=v, compare_op=ALU.is_ge, fill=0.0, base=0,
                               pattern=[[-GN_GROUP, P // GN_GROUP], [0, GN_GROUP]],
                               channel_multiplier=1).then_inc(s_avg, 1)
            pool.wait_ge(s_avg, 2)
            pool.affine_select(out=v, in_=v, compare_op=ALU.is_ge, fill=0.0, base=GN_GROUP - 1,
                               pattern=[[GN_GROUP, P // GN_GROUP], [0, GN_GROUP]],
                               channel_multiplier=-1).then_inc(s_avg, 1)
            for q in range(2):
                pool.memset(D[q][:, :], 0.0).then_inc(s_clear, 1)
            pool.wait_ge(s_clear, 2)
            for q in range(2):
                pool.dma_start(skew[q, 0:1, 0:1], D[q][0:1, 0:1]).then_inc(s_store[q], 16)
            pool.memset(minus_half[:, :], -0.5).then_inc(s_avg, 1)
            pool.wait_ge(s_avg, 4)
            with pool.Fori(0, LANES // 2) as it:
                for q in range(2):
                    for s in range(SETS):
                        k = 4 * it + 2 * q + s
                        pool.wait_ge(s_vec, VS * k + 13)
                        pool.tensor_tensor(rstd[:, :], veps[:, :], minus_half[:, :], ALU.pow).then_inc(s_rstd, 1)
                    pool.wait_ge(s_vec, VS * (4 * it + 2 * q + 2))
                    pool.dma_start(skew[2 * it + q], D[q][:, :]).then_inc(s_store[q], 16)
            for q in range(2):
                pool.wait_ge(s_store[q], 16 * (LANES // 2 + 1))

        @block.tensor
        def _(pe):
            pe.sem_inc(s_turned, 16)
            pe.wait_ge(s_const, 2)
            pe.wait_ge(s_avg, 3)
            with pe.Fori(0, LANES // 2) as it:
                for q in range(2):
                    for s in range(SETS):
                        k = 4 * it + 2 * q + s
                        pe.wait_ge(s_load[s], 16 * (2 * it + q + 1))
                        for g in range(8):
                            pe.wait_ge(s_copied, 8 * k + g + 1)
                            for n in range(4):
                                last = nc.tensor.transpose(turned[g % 4][:, n, :], xin[s][:, 4 * g + n, :], ident[:, :])
                            last.then_inc(s_turned, 1)
                        pe.wait_ge(s_vec, VS * k + 9)
                        nc.tensor.matmul(group[:, 0:1], avg[:, :], mv[:, 0:1], start=True, stop=True).then_inc(s_group, 1)
                        pe.wait_ge(s_vec, VS * k + 12)
                        nc.tensor.matmul(group[:, 0:1], avg[:, :], spread[:, :], start=True, stop=True).then_inc(s_group, 1)

        @block.scalar
        def _(act):
            act.sem_inc(s_copied, 4)
            act.wait_ge(s_clear, 2)
            with act.Fori(0, LANES // 2) as it:
                for q in range(2):
                    act.wait_ge(s_store[q], 16 * it + 16)
                    for s in range(SETS):
                        k = 4 * it + 2 * q + s
                        for g in range(8):
                            act.wait_ge(s_turned, 16 + 8 * k + g + 1)
                            nc.scalar.copy(chunk(q, s, g), turned[g % 4][:, :, :].rearrange("c n (i h) -> c n i h", h=2)).then_inc(s_copied, 1)

        @block.vector
        def _(dve):
            with dve.Fori(0, LANES // 2) as it:
                for q in range(2):
                    for s in range(SETS):
                        k = 4 * it + 2 * q + s
                        for g in range(8):
                            dve.wait_ge(s_copied, 4 + 8 * k + g + 1)
                            nc.vector.bn_stats(stats[:, g, :], strided(chunk(q, s, g)[:, 0:1, 0:1, 0:1], [[G, 4], [G + 1, G], [G * NT, 2]])).then_inc(s_vec, 1)
                        dve.drain()
                        nc.vector.bn_aggr(mv[:, :], stats[:, :, :]).then_inc(s_vec, 1)
                        dve.wait_ge(s_group, 2 * k + 1)
                        nc.vector.tensor_copy(gmean[:, :], group[:, 0:1]).then_inc(s_vec, 1)
                        dve.wait_ge(s_vec, VS * k + 10)
                        nc.vector.tensor_tensor(dev[:, :], mv[:, 0:1], gmean[:, :], ALU.subtract).then_inc(s_vec, 1)
                        dve.wait_ge(s_vec, VS * k + 11)
                        nc.vector.scalar_tensor_tensor(out=spread[:, :], in0=dev[:, :], scalar=dev[:, 0:1], in1=mv[:, 1:2],
                                                       op0=ALU.mult, op1=ALU.add).then_inc(s_vec, 1)
                        dve.wait_ge(s_group, 2 * k + 2)
                        nc.vector.tensor_scalar(veps[:, :], group[:, 0:1], EPS, None, ALU.add).then_inc(s_vec, 1)
                        dve.wait_ge(s_rstd, k + 1)
                        nc.vector.scalar_tensor_tensor(out=shift[:, :], in0=gmean[:, :], scalar=-1.0, in1=rstd[:, :],
                                                       op0=ALU.mult, op1=ALU.mult).then_inc(s_vec, 1)
                        dve.wait_ge(s_vec, VS * k + 14)
                        nc.vector.tensor_scalar(image(q, s), image(q, s), rstd[:, 0:1], shift[:, 0:1],
                                                ALU.mult, ALU.add).then_inc(s_vec, 1)


PAIRS = STEPS // (2 * WIN)


def rows_of(pair):
    first = max(0, (pair * 2 * WIN - PERIOD * (SETS - 1) - G + 1) // (2 * WIN) * (2 * WIN))
    last = min(G, (pair + 1) * 2 * WIN)
    return first, last


def cleared_row(t):
    if t < G - 1:
        return t + 1
    if PERIOD <= t + 1 < PERIOD + G:
        return t - G
    return None


def lstm_phase(nc, sems, skew, hidden, weights, biases):
    W = ["wf0", "wf1", "wc", "wi", "wo"]
    U = ["uf0", "uf1", "uc", "ui", "uo"]
    BI = ["bf0", "bf1", "bc", "bi", "bo"]
    with ExitStack() as ctx:
        m = Memory(nc, ctx)
        w = {n: m.sb("l_" + n, [C, C]) for n in W + U}
        bias = {n: m.sb("l_" + n, [C, 1]) for n in BI}
        xw = [[m.sb(f"l_x{c}{q}", [C, LPC, WIN, G]) for q in range(2)] for c in range(CHAINS)]
        hw = [[m.sb(f"l_h{c}{q}", [C, LPC, WIN, SLOT]) for q in range(2)] for c in range(CHAINS)]
        hsum = [m.sb(f"l_hsum{c}", [C, LPC, G]) for c in range(CHAINS)]
        cell = [m.sb(f"l_cell{c}", [C, LPC, SLOT]) for c in range(CHAINS)]
        gate = [m.sb(f"l_gate{c}", [C, 5, LPC, G]) for c in range(CHAINS)]
        keep_up = [m.sb(f"l_up{c}", [C, LPC, G]) for c in range(CHAINS)]
        keep_left = [m.sb(f"l_left{c}", [C, LPC, G]) for c in range(CHAINS)]
        fresh = [m.sb(f"l_fresh{c}", [C, LPC, G]) for c in range(CHAINS)]
        tanhc = [m.sb(f"l_tanhc{c}", [C, LPC, G]) for c in range(CHAINS)]
        zero = m.sb("l_zero", [C, LPC])
        pf = [m.ps(f"l_pf{c}", [C, 2, LPC, G]) for c in range(CHAINS)]
        pc = [m.ps(f"l_pc{c}", [C, 2, LPC, G]) for c in range(CHAINS)]
        pio = [m.ps(f"l_pio{c}", [C, 2, LPC, G]) for c in range(CHAINS)]
        banks = [[pf[c][:, 0], pf[c][:, 1], pc[c][:, 0], pio[c][:, 0], pio[c][:, 1]] for c in range(CHAINS)]

        s_w = sems.sem("l_weights")
        s_init = sems.sem("l_init")
        s_x = [[sems.sem(f"l_x{c}{q}") for q in range(2)] for c in range(CHAINS)]
        s_st = [[sems.sem(f"l_store{c}{q}") for q in range(2)] for c in range(CHAINS)]
        s_xdone = [sems.sem(f"l_xdone{c}") for c in range(CHAINS)]
        s_gates = [sems.sem(f"l_gates{c}") for c in range(CHAINS)]
        s_act = [sems.sem(f"l_act{c}") for c in range(CHAINS)]
        s_cell = [sems.sem(f"l_cell{c}") for c in range(CHAINS)]
        VC = 9

        block = ctx.enter_context(nc.Block())

        def sizes(pair):
            r0, r1 = rows_of(pair)
            return slice(r0, r1), slice(r0 + 1, r1 + 1)

        def runs():
            looped = [p for p in range(PAIRS) if rows_of(p) == (0, G)
                      and all(cleared_row(t) == t - G for t in range(2 * WIN * p, 2 * WIN * (p + 1)))]
            lo, hi = looped[0], looped[-1] + 1
            return lo, hi

        LO, HI = runs()

        def each_pair(eng, body):
            for p in range(LO):
                body(p, p)
            with eng.Fori(LO, HI) as p:
                body(p, LO)
            for p in range(HI, PAIRS):
                body(p, p)

        @block.sync
        def _(sp):
            for n in W + U:
                sp.dma_start(w[n][:, :], weights[n]).then_inc(s_w, 16)
            for n in BI:
                sp.dma_start(bias[n][:, :], biases[n].rearrange("(p a) -> p a", a=1)).then_inc(s_w, 16)

            def body(p, like):
                for q in range(2):
                    for c in range(CHAINS):
                        sp.wait_ge(s_xdone[c], 2 * p + q + 1)
                        sp.dma_start(xw[c][q][:, :, :, :].rearrange("c l t g -> c l (t g)"),
                                     skew[c * LPC:(c + 1) * LPC, :, bass.ds((2 * p + q) * WIN * G, WIN * G)]
                                     .rearrange("l c g -> c l g")).then_inc(s_x[c][q], 16)
            each_pair(sp, body)

        @block.gpsimd
        def _(pool):
            for c in range(CHAINS):
                for q in range(2):
                    pool.memset(hw[c][q][:, :, :, :], 0.0).then_inc(s_init, 1)
                pool.memset(cell[c][:, :, :], 0.0).then_inc(s_init, 1)
                pool.memset(hsum[c][:, :, :], 0.0).then_inc(s_init, 1)
            pool.memset(zero[:, :], 0.0).then_inc(s_init, 1)
            pool.wait_ge(s_init, 4 * CHAINS + 1)
            for c in range(CHAINS):
                for q in range(2):
                    pool.dma_start(hidden[c * LPC, 0:1, q * WIN * SLOT:q * WIN * SLOT + 1],
                                   hw[c][q][0:1, 0, 0, 0:1]).then_inc(s_st[c][q], 16)

            def body(p, like):
                for q in range(2):
                    for c in range(CHAINS):
                        pool.wait_ge(s_cell[c], VC * ((2 * p + q + 1) * WIN))
                        pool.dma_start(hidden[c * LPC:(c + 1) * LPC, :, bass.ds((2 * p + q) * WIN * SLOT, WIN * SLOT)]
                                       .rearrange("l c g -> c l g"),
                                       hw[c][q][:, :, :, :].rearrange("c l t g -> c l (t g)")).then_inc(s_st[c][q], 16)
            each_pair(pool, body)
            for c in range(CHAINS):
                for q in range(2):
                    pool.wait_ge(s_st[c][q], 16 * (PAIRS + 1))

        @block.tensor
        def _(pe):
            for c in range(CHAINS):
                pe.sem_inc(s_xdone[c], 2)
            pe.wait_ge(s_w, 16 * 15)
            pe.wait_ge(s_init, 4 * CHAINS + 1)

            def body(p, like):
                rows, slots = sizes(like)
                for u in range(2 * WIN):
                    q, k = u // WIN, u % WIN
                    t = 2 * WIN * p + u
                    for c in range(CHAINS):
                        if k == 0:
                            pe.wait_ge(s_x[c][q], 16 * p + 16)
                        first = like == 0 and u == 0
                        xs = xw[c][q][:, :, k, rows]
                        for g in range(5):
                            if not first and g in (0, 2, 3):
                                pe.wait_ge(s_act[c], 6 * t - 6 + (2, 0, 3, 5)[g] if g != 3 else 6 * t - 6 + 5)
                            mm = nc.tensor.matmul(banks[c][g][:, :, rows], w[W[g]][:, :], xs,
                                                  start=g in (0, 2, 3), stop=False, skip_group_check=True)
                        if k == WIN - 1:
                            mm.then_inc(s_xdone[c], 1)
                        hprev = hw[c][(q if k else 1 - q)][:, :, (k - 1) % WIN, :]
                        up, left = hprev[:, :, rows], hprev[:, :, slots]
                        if not first:
                            pe.wait_ge(s_cell[c], VC * t - 1)
                        nc.tensor.matmul(banks[c][0][:, :, rows], w[U[0]][:, :], up, start=False, stop=True, skip_group_check=True)
                        nc.tensor.matmul(banks[c][1][:, :, rows], w[U[1]][:, :], left, start=False, stop=True,
                                         skip_group_check=True).then_inc(s_gates[c], 1)
                        if not first:
                            pe.wait_ge(s_cell[c], VC * t)
                        for g in (2, 3, 4):
                            mm = nc.tensor.matmul(banks[c][g][:, :, rows], w[U[g]][:, :], hsum[c][:, :, rows],
                                                  start=False, stop=True, skip_group_check=True)
                            if g != 3:
                                mm.then_inc(s_gates[c], 1)
            each_pair(pe, body)

        @block.scalar
        def _(act):
            act.wait_ge(s_w, 16 * 15)

            def body(p, like):
                rows, slots = sizes(like)
                for u in range(2 * WIN):
                    t = 2 * WIN * p + u
                    for c in range(CHAINS):
                        for g in range(5):
                            if g in (0, 2, 3):
                                act.wait_ge(s_gates[c], 3 * t + (1, 0, 2, 3)[g])
                            if g == 0 and not (like == 0 and u == 0):
                                act.wait_ge(s_cell[c], VC * t - 3)
                            nc.scalar.activation(gate[c][:, g, :, rows], banks[c][g][:, :, rows],
                                                 ACT.Tanh if g == 2 else ACT.Sigmoid, bias=bias[BI[g]][:, 0:1]).then_inc(s_act[c], 1)
                        act.wait_ge(s_cell[c], VC * t + 5)
                        nc.scalar.activation(tanhc[c][:, :, rows], cell[c][:, :, slots], ACT.Tanh).then_inc(s_act[c], 1)
            each_pair(act, body)

        @block.vector
        def _(dve):
            dve.wait_ge(s_init, 4 * CHAINS + 1)

            def body(p, like):
                rows, slots = sizes(like)
                for u in range(2 * WIN):
                    q, k = u // WIN, u % WIN
                    t = 2 * WIN * p + u
                    for c in range(CHAINS):
                        g = gate[c]
                        n = VC * t
                        up, left, mix, th = keep_up[c][:, :, rows], keep_left[c][:, :, rows], fresh[c][:, :, rows], tanhc[c][:, :, rows]
                        dve.wait_ge(s_act[c], 6 * t + 1)
                        if not (like == 0 and u == 0):
                            dve.wait_ge(s_cell[c], n)
                        nc.vector.tensor_tensor(up, g[:, 0, :, rows], cell[c][:, :, rows], ALU.mult).then_inc(s_cell[c], 1)
                        dve.wait_ge(s_act[c], 6 * t + 2)
                        nc.vector.tensor_tensor(left, g[:, 1, :, rows], cell[c][:, :, slots], ALU.mult).then_inc(s_cell[c], 1)
                        dve.wait_ge(s_cell[c], n + 2)
                        nc.vector.tensor_tensor(up, up, left, ALU.add).then_inc(s_cell[c], 1)
                        dve.wait_ge(s_act[c], 6 * t + 4)
                        nc.vector.tensor_tensor(mix, g[:, 3, :, rows], g[:, 2, :, rows], ALU.mult).then_inc(s_cell[c], 1)
                        dve.wait_ge(s_cell[c], n + 4)
                        nc.vector.tensor_tensor(cell[c][:, :, slots], up, mix, ALU.add).then_inc(s_cell[c], 1)
                        dve.wait_ge(s_act[c], 6 * t + 6)
                        if k == 0:
                            dve.wait_ge(s_st[c][q], 16 * p + 16)
                        h = hw[c][q][:, :, k, :]
                        nc.vector.tensor_tensor(h[:, :, slots], g[:, 4, :, rows], th, ALU.mult).then_inc(s_cell[c], 1)
                        dve.wait_ge(s_cell[c], n + 6)
                        if LO <= like < HI:
                            row = 2 * WIN * p + u - G + 1
                            hz, cz = h[:, :, bass.ds(row, 1)], cell[c][:, :, bass.ds(row, 1)]
                        elif cleared_row(2 * WIN * like + u) is not None and cleared_row(2 * WIN * like + u) < G:
                            row = cleared_row(2 * WIN * like + u) + 1
                            hz, cz = h[:, :, row:row + 1], cell[c][:, :, row:row + 1]
                        else:
                            hz, cz = h[:, :, 0:1], cell[c][:, :, 0:1]
                        z = zero[:, :].rearrange("p (l a) -> p l a", a=1)
                        nc.vector.tensor_copy(cz, z).then_inc(s_cell[c], 1)
                        nc.vector.tensor_copy(hz, z).then_inc(s_cell[c], 1)
                        nr, ns = sizes(like + 1) if (u == 2 * WIN - 1 and not LO <= like < HI - 0 and like + 1 < PAIRS) else (rows, slots)
                        dve.wait_ge(s_cell[c], n + 8)
                        nc.vector.tensor_tensor(hsum[c][:, :, nr], h[:, :, nr], h[:, :, ns], ALU.add).then_inc(s_cell[c], 1)
            each_pair(dve, body)


HEADS, DH, LM = 8, 16, 64
SEG = TOK // LM
PAIRS_H = HEADS // 2
GT = 4
NG = NT // GT
LSTM_RUN = (2 * G - 1) * SLOT
RMAX = bass.bass_isa.ReduceOp.max


class Resident:

    def __init__(self, m):
        self.attn2 = m.sb("r_attn2", [P, B, PAIRS_H, LM])
        self.k_lm = m.sb("r_k_lm", [C, B, LM])
        self.ctx = m.sb("r_ctx", [P, B, PAIRS_H, DH])
        self.ident = m.sb("r_ident", [P, P])
        self.head_mask = m.sb("r_head_mask", [C, HEADS, LM])


def fill_masks(pool, R, sem):
    make_identity(pool, R.ident, sem)
    mask = R.head_mask[:, :, :]
    pool.memset(mask, 1.0).then_inc(sem, 1)
    pool.wait_ge(sem, 3)
    pool.affine_select(out=mask, in_=mask, compare_op=ALU.is_ge, fill=0.0, base=0,
                       pattern=[[-DH, HEADS], [0, LM]], channel_multiplier=1).then_inc(sem, 1)
    pool.wait_ge(sem, 4)
    pool.affine_select(out=mask, in_=mask, compare_op=ALU.is_ge, fill=0.0, base=DH - 1,
                       pattern=[[DH, HEADS], [0, LM]], channel_multiplier=-1).then_inc(sem, 1)


def landmark_phase(nc, sems, R, x, hidden, wqkv, gamma, beta, b_out, xnt, base, vals):
    with ExitStack() as ctx:
        m = Memory(nc, ctx)
        hid = m.sb("a_hid", [C, LSTM_RUN])
        hrow = [m.sb(f"a_hrow{k}", [C, GT * P]) for k in range(2)]
        xin = m.sb("a_xin", [P, NT, C])
        t = m.sb("a_t", [P, NT, C])
        xn = [m.sb(f"a_xn{k}", [P, GT, C]) for k in range(2)]
        xnT = [m.sb(f"a_xnT{q}", [C, TOK]) for q in range(2)]
        xn_lp = m.sb("a_xn_lp", [C, TOK], BF16)
        v = m.sb("a_v", [P, NT, C])
        w = m.sb("a_w", [C, 3 * C])
        wkT = m.sb("a_wkT", [C, C])
        gam = m.sb("a_gamma", [C, 1])
        bet = m.sb("a_beta", [C, 1])
        bout = m.sb("a_bout", [P, C])
        st = m.sb("a_st", [P, GT, 6])
        mv = m.sb("a_mv", [P, NT, 2])
        half = m.sb("a_half", [P, GT])
        stat = {n: m.sb("a_" + n, [P, NT]) for n in ("v1", "v12", "r1", "r", "rb", "shb")}
        xm = m.sb("a_xm", [C, LM])
        ql = m.sb("a_ql", [C, LM])
        kl = m.sb("a_kl", [C, LM])
        qbd = m.sb("a_qbd", [C, HEADS * LM])
        ws = [m.sb(f"a_ws{q}", [C, HEADS * LM]) for q in range(2)]
        ws_lp = m.sb("a_ws_lp", [C, HEADS * LM], BF16)
        mx2 = m.sb("a_mx2", [P, PAIRS_H])
        sum2 = m.sb("a_sum2", [P, PAIRS_H])
        rec2 = m.sb("a_rec2", [P, PAIRS_H])
        e2 = m.sb("a_e2", [P, PAIRS_H, LM])
        e2x = m.sb("a_e2x", [P, PAIRS_H, LM])
        m3p = m.sb("a_m3p", [P, PAIRS_H, NG])
        m3 = m.sb("a_m3", [P, PAIRS_H])
        neg4 = m.sb("a_neg4", [PAIRS_H, PAIRS_H, P])
        m3row = [m.sb(f"a_m3row{q}", [PAIRS_H, PAIRS_H, P], BF16) for q in range(2)]
        ones4 = m.sb("a_ones4", [PAIRS_H, P], BF16)
        ones = m.sb("a_ones", [P, 1])
        p3 = [m.sb(f"a_p3{k}", [P, HEADS * LM]) for k in range(4)]
        acc = m.sb("a_acc", [P, HEADS * LM])
        pvs = m.sb("a_pvs", [C, P])
        den = m.sb("a_den", [P, PAIRS_H])
        turn_h = m.ps("a_turn_h", [P, GT, P])
        turn_n = m.ps("a_turn_n", [P, GT, P])
        S = [m.ps(f"a_s{k}", [P, 512]) for k in range(2)]
        L = [m.ps(f"a_l{k}", [P, 512]) for k in range(2)]
        pv = m.ps("a_pv", [C, 512])
        misc = m.ps("a_misc", [P, 512])

        s_w = sems.sem("a_w")
        s_const = sems.sem("a_const")
        s_ones = sems.sem("a_ones")
        s_wkT = sems.sem("a_wkT")
        s_hid = sems.sem("a_hid")
        s_xin = sems.sem("a_xin")
        s_hc = sems.sem("a_hc")
        s_ht = sems.sem("a_ht")
        s_add = sems.sem("a_add")
        s_ln = sems.sem("a_ln")
        s_pow = sems.sem("a_pow")
        s_rb = sems.sem("a_rb")
        s_xn = sems.sem("a_xn")
        s_sc = sems.sem("a_sc")
        s_base = sems.sem("a_base")
        s_xt = sems.sem("a_xt")
        s_xnT = sems.sem("a_xnT")
        s_xr = sems.sem("a_xr")
        s_xm = sems.sem("a_xm")
        s_stx = [sems.sem(f"a_store_xnt{q}") for q in range(2)]
        s_stb = sems.sem("a_store_base")
        s_stv = sems.sem("a_store_v")
        s_mset = sems.sem("a_mset")
        s_set = sems.sem("a_set")
        s_ws = sems.sem("a_ws")
        s_wsc = sems.sem("a_wsc")
        s_e2 = sems.sem("a_e2")
        s_lp = sems.sem("a_lp")
        s_mx = sems.sem("a_mx")
        s_val = sems.sem("a_val")
        s_valc = sems.sem("a_valc")
        s_s = sems.sem("a_s")
        s_exp = sems.sem("a_exp")
        s_pv = sems.sem("a_pv")
        s_acc = sems.sem("a_acc")
        s_mtail = sems.sem("a_mtail")
        s_tail = sems.sem("a_tail")
        MSET, SET, TAIL = 3, 12, 4
        NL = PAIRS_H * NG
        HIDDEN, NORMED, LANDMARKS, WEIGHTS_AT, MAXIMA = 2, 6, 23, 24, 25

        def every_other(n, start):
            return [(n - start) // 2] if n >= start and (n - start) % 2 == 0 and (n - start) // 2 < NG else []

        def maxima_due(n):
            k = NT - MAXIMA
            return range((n - MAXIMA) * NL // k, (n - MAXIMA + 1) * NL // k) if n >= MAXIMA else []

        def at_first(a, images=1):
            return isinstance(a, int) and a < images

        def pv_done(b, n):
            return 4 + NT * b + n + 1

        def acc_done(b, n):
            return 4 + (NT - 1) * b + max(n, 1)

        def each_image(eng, body):
            body(0, 0, True, False)
            with eng.Fori(0, B // 2 - 1) as i:
                body(2 * i + 1, 1, False, False)
                body(2 * i + 2, 0, False, False)
            body(B - 1, 1, False, True)

        block = ctx.enter_context(nc.Block())

        @block.sync
        def _(sp):
            sp.dma_start(w[:, :], wqkv).then_inc(s_w, 16)
            sp.dma_start(gam[:, :], gamma.rearrange("(p a) -> p a", a=1)).then_inc(s_w, 16)
            sp.dma_start(bet[:, :], beta.rearrange("(p a) -> p a", a=1)).then_inc(s_w, 16)
            sp.dma_start(bout[:, :], b_out.rearrange("(a c) -> a c", a=1).broadcast_to([P, C])).then_inc(s_w, 16)

            def load(a):
                if not at_first(a):
                    sp.wait_ge(s_hc, NG * a)
                    sp.wait_ge(s_add, NG * a)
                sp.dma_start(hid[:, :], hidden[a % LANES, :, bass.ds((a // LANES) * (PERIOD * SLOT), LSTM_RUN)]
                             ).then_inc(s_hid, 16)
                for g in range(NG):
                    sp.dma_start(xin[:, GT * g:GT * g + GT, :], x[a, 512 * g:512 * g + 512, :].rearrange("(n p) c -> p n c", p=P)
                                 ).then_inc(s_xin, 16)

            def store_normed(a, q):
                sp.wait_ge(s_base, NG * (a + 1))
                sp.dma_start(base[a].rearrange("(n p) c -> p n c", p=P), t[:, :, :]).then_inc(s_stb, 16)
                sp.wait_ge(s_xnT, NG * (a + 1))
                sp.dma_start(xnt[a], xnT[q][:, :]).then_inc(s_stx[q], 16)

            def body(b, q, first, last):
                if not isinstance(b, int) or b + 2 < B:
                    load(b + 2)
                if not last:
                    store_normed(b + 1, 1 - q)
                sp.wait_ge(s_valc, NG * (b + 1))
                sp.dma_start(vals[b].rearrange("(n p) c -> p n c", p=P), v[:, :, :]).then_inc(s_stv, 16)
            load(0)
            load(1)
            store_normed(0, 0)
            body(0, 0, True, False)
            with sp.Fori(0, B // 2 - 2) as i:
                body(2 * i + 1, 1, False, False)
                body(2 * i + 2, 0, False, False)
            for b in range(B - 3, B):
                body(b, b % 2, False, b == B - 1)
            for q in range(2):
                sp.wait_ge(s_stx[q], 16 * B // 2)
            sp.wait_ge(s_stb, 16 * B)
            sp.wait_ge(s_stv, 16 * B)

        @block.gpsimd
        def _(pool):
            fill_masks(pool, R, s_const)
            pool.memset(half[:, :], -0.5).then_inc(s_const, 1)
            pool.memset(ones4[:, :], 1.0).then_inc(s_ones, 1)
            pool.memset(ones[:, :], 1.0).then_inc(s_ones, 1)
            pool.memset(neg4[:, :, :], 0.0).then_inc(s_ones, 1)
            pool.wait_ge(s_ones, 3)
            pool.affine_select(out=neg4[:, :, :], in_=neg4[:, :, :], compare_op=ALU.not_equal, fill=-1.0, base=0,
                               pattern=[[-1, PAIRS_H], [0, P]], channel_multiplier=1).then_inc(s_ones, 1)
            pool.sem_inc(s_acc, 4)
            pool.wait_ge(s_const, 6)

            def powers(a, g):
                at = slice(GT * g, GT * g + GT)
                pool.wait_ge(s_ln, NG * a + g + 1)
                pool.tensor_tensor(stat["r"][:, at], stat["v12"][:, at], half[:, :], ALU.pow).then_inc(s_pow, 1)
                pool.tensor_tensor(stat["r1"][:, at], stat["v1"][:, at], half[:, :], ALU.pow).then_inc(s_pow, 1)

            def body(b, q, first, last):
                for n in range(NT):
                    if n == 1:
                        if not first:
                            pool.wait_ge(s_mtail, 2 * b - 1)
                        pool.wait_ge(s_exp, NT * b + 2)
                        pool.tensor_tensor(acc[:, :], p3[0][:, :], p3[1][:, :], ALU.add).then_inc(s_acc, 1)
                    elif n:
                        pool.wait_ge(s_exp, NT * b + n + 1)
                        pool.wait_ge(s_acc, acc_done(b, n - 1))
                        pool.tensor_tensor(acc[:, :], acc[:, :], p3[n % 4][:, :], ALU.add).then_inc(s_acc, 1)
                    if not last:
                        for g in every_other(n, HIDDEN + 1):
                            powers(b + 1, g)
            for g in range(NG):
                powers(0, g)
            each_image(pool, body)

        @block.tensor
        def _(pe):
            pe.sem_inc(s_pv, 4)
            pe.wait_ge(s_const, 6)
            pe.wait_ge(s_ones, 4)
            pe.wait_ge(s_w, 64)
            nc.tensor.transpose(misc[:, 0:C], w[:, C:2 * C], R.ident[:, :]).then_inc(s_wkT, 1)
            pe.wait_ge(s_wkT, 2)

            def turn_hidden(a, g):
                pe.wait_ge(s_hc, NG * a + g + 1)
                if g or not at_first(a):
                    pe.wait_ge(s_add, NG * a + g)
                for k in range(GT):
                    mt = nc.tensor.transpose(turn_h[:, k, :], hrow[g % 2][:, P * k:P * k + P], R.ident[:, :])
                mt.then_inc(s_ht, 1)

            def turn_normed(a, g):
                if g or not at_first(a):
                    pe.wait_ge(s_xnT, NG * a + g)
                pe.wait_ge(s_xn, NG * a + g + 1)
                for k in range(GT):
                    mt = nc.tensor.transpose(turn_n[:, k, :], xn[g % 2][:, k, :], R.ident[:, :])
                mt.then_inc(s_xt, 1)

            def landmarks(a):
                pe.wait_ge(s_xm, NG * (a + 1))
                if not at_first(a):
                    pe.wait_ge(s_set, SET * a - 3)
                if not at_first(a, 2):
                    pe.wait_ge(s_tail, TAIL * (a - 1))
                nc.tensor.matmul(misc[:, 0:LM], w[:, 0:C], xm[:, :], start=True, stop=True)
                nc.tensor.matmul(misc[:, LM:2 * LM], w[:, C:2 * C], xm[:, :], start=True, stop=True).then_inc(s_mset, 1)

            def scores_weights(a):
                pe.wait_ge(s_set, SET * a + 4)
                if not at_first(a):
                    pe.wait_ge(s_valc, NG * a - 1)
                nc.tensor.matmul(L[0][:, :], wkT[:, :], qbd[:, :], start=True, stop=True).then_inc(s_ws, 1)
                for g in range(PAIRS_H):
                    mt = nc.tensor.matmul(misc[:, P + LM * g:P + LM * g + LM], qbd[:, P * g:P * g + P], kl[:, :],
                                          start=True, stop=True)
                mt.then_inc(s_mset, 1)

            def rounded_scores(a, j):
                c, g = j // PAIRS_H, j % PAIRS_H
                if j == 0:
                    pe.wait_ge(s_set, SET * a + 5)
                    if not at_first(a):
                        pe.wait_ge(s_valc, NG * a)
                elif j == 1:
                    pe.wait_ge(s_wsc, a + 1)
                else:
                    pe.wait_ge(s_mx, NL * a + j - 1)
                nc.tensor.matmul(L[(j + 1) % 2][:, :], ws_lp[:, P * g:P * g + P], xn_lp[:, 512 * c:512 * c + 512],
                                 start=True, stop=True).then_inc(s_lp, 1)

            def turn_maxima(a):
                pe.wait_ge(s_set, SET * a + 8)
                nc.tensor.transpose(misc[0:PAIRS_H, 384:512], m3[:, :], R.ident[:, :]).then_inc(s_mset, 1)

            def make_ready(a, n):
                for g in every_other(n, HIDDEN):
                    turn_hidden(a, g)
                for g in every_other(n, NORMED):
                    turn_normed(a, g)
                if n == LANDMARKS:
                    landmarks(a)
                if n == WEIGHTS_AT:
                    scores_weights(a)
                for j in maxima_due(n):
                    rounded_scores(a, j)
                if n == NT - 1:
                    turn_maxima(a)

            def values(b, q, g):
                if g < 2:
                    pe.wait_ge(s_mx, NL * (b + 1) - g)
                else:
                    pe.wait_ge(s_valc, NG * b + g - 1)
                for k in range(GT):
                    n = GT * g + k
                    mt = nc.tensor.matmul(L[g % 2][:, P * k:P * k + P], xnT[q][:, P * n:P * n + P], w[:, 2 * C:3 * C],
                                          start=True, stop=True)
                mt.then_inc(s_val, 1)

            def weigh(b, n):
                pe.wait_ge(s_exp, NT * b + n + 1)
                if n % GT == 0:
                    pe.wait_ge(s_valc, NG * b + n // GT + 1)
                for g in range(PAIRS_H):
                    mt = nc.tensor.matmul(pv[32 * g:32 * g + 32, 0:P], v[:, n, 32 * g:32 * g + 32],
                                          p3[n % 4][:, P * g:P * g + P], start=n == 0, stop=n == NT - 1)
                mt.then_inc(s_pv, 1)

            def context(b):
                pe.wait_ge(s_acc, acc_done(b, NT - 1))
                for g in range(PAIRS_H):
                    mt = nc.tensor.matmul(misc[:, g:g + 1], acc[:, P * g:P * g + P], ones[:, :], start=True, stop=True)
                mt.then_inc(s_mtail, 1)
                pe.wait_ge(s_tail, TAIL * b + 1)
                nc.tensor.transpose(misc[:, P:2 * P], pvs[:, :], R.ident[:, :]).then_inc(s_mtail, 1)

            def body(b, q, first, last):
                for n in range(NT):
                    if n == 0:
                        pe.wait_ge(s_set, SET * b + 9)
                    if n >= 2 or not first:
                        pe.wait_ge(s_exp, NT * b + n - 1)
                    bank = S[n % 2]
                    nc.tensor.matmul(bank[:, :], xnT[q][:, P * n:P * n + P], ws[q][:, :], start=True, stop=False)
                    nc.tensor.matmul(bank[:, :], ones4[:, :], m3row[q][:, :, :].rearrange("p g c -> p (g c)"),
                                     start=False, stop=True).then_inc(s_s, 1)
                    if n % 3 == 0 and n // 3 < NG:
                        values(b, q, n // 3)
                    if n == 1 and not first:
                        context(b - 1)
                    if n >= 2:
                        weigh(b, n - 2)
                    if not last:
                        make_ready(b + 1, n)
                weigh(b, NT - 2)
                weigh(b, NT - 1)
            for n in range(NT):
                make_ready(0, n)
            each_image(pe, body)
            pe.wait_ge(s_tail, TAIL * (B - 1))
            context(B - 1)

        @block.scalar
        def _(act):
            act.wait_ge(s_w, 64)
            act.wait_ge(s_wkT, 1)
            nc.scalar.activation(wkT[:, :], misc[:, 0:C], ACT.Identity).then_inc(s_wkT, 1)

            def unskew(a, g):
                if g == 0:
                    act.wait_ge(s_hid, 16 * a + 16)
                if g >= 2 or not at_first(a):
                    act.wait_ge(s_ht, NG * a + g - 1)
                rows = GT * P // G
                start = (SLOT + 1) * rows * g + 1
                nc.scalar.activation(hrow[g % 2][:, :].rearrange("c (i j) -> c i j", j=G),
                                     strided(hid[:, start:start + 1], [[SLOT + 1, rows], [SLOT, G]]),
                                     ACT.Identity).then_inc(s_hc, 1)

            def norm_group(a, q, g):
                act.wait_ge(s_xt, NG * a + g + 1)
                if g == 0 and not at_first(a, 2):
                    act.wait_ge(s_stx[q], 8 * (a - q))
                nc.scalar.activation(xnT[q][:, 512 * g:512 * g + 512], turn_n[:, :, :].rearrange("c k t -> c (k t)"), ACT.Identity,
                                     bias=bet[:, 0:1], scale=gam[:, 0:1]).then_inc(s_xnT, 1)
                act.wait_ge(s_rb, NG * a + g + 1)
                act.wait_ge(s_xn, NG * a + g + 1)
                for k in range(GT):
                    n = GT * g + k
                    ma = nc.scalar.activation(t[:, n, :], t[:, n, :], ACT.Identity, bias=stat["shb"][:, n:n + 1],
                                              scale=stat["rb"][:, n:n + 1])
                ma.then_inc(s_sc, 1)

            def make_ready(a, q, n):
                for g in every_other(n, 0):
                    unskew(a, g)
                for g in every_other(n, NORMED + 1):
                    norm_group(a, q, g)
                if n == WEIGHTS_AT:
                    act.wait_ge(s_ws, a + 1)
                    nc.scalar.activation(ws[q][:, :], L[0][:, :], ACT.Identity).then_inc(s_wsc, 1)
                if n == MAXIMA:
                    act.wait_ge(s_set, SET * a + 7)
                    nc.scalar.activation(e2x[:, :, :], e2[:, :, :], ACT.Exp).then_inc(s_e2, 1)

            def body(b, q, first, last):
                for n in range(NT):
                    act.wait_ge(s_s, NT * b + n + 1)
                    act.wait_ge(s_pv, pv_done(b, n - 4))
                    act.wait_ge(s_acc, (acc_done(b, n - 4) if n >= 4 else 4 + (NT - 1) * b - 3 + n))
                    nc.scalar.activation(p3[n % 4][:, :], S[n % 2][:, :], ACT.Exp).then_inc(s_exp, 1)
                    if n % 3 == 0 and n // 3 < NG:
                        g = n // 3
                        act.wait_ge(s_val, NG * b + g + 1)
                        if g == 0 and not first:
                            act.wait_ge(s_stv, 16 * b)
                        nc.scalar.activation(v[:, GT * g:GT * g + GT, :].rearrange("p k c -> p (k c)"), L[g % 2][:, :],
                                             ACT.Identity).then_inc(s_valc, 1)
                    if not last:
                        make_ready(b + 1, 1 - q, n)
            for n in range(NT):
                make_ready(0, 0, n)
            each_image(act, body)

        @block.vector
        def _(dve):
            dve.wait_ge(s_const, 6)
            dve.wait_ge(s_ones, 4)
            dve.wait_ge(s_w, 64)

            def add_group(a, g):
                at = slice(GT * g, GT * g + GT)
                if g == 0:
                    dve.wait_ge(s_xin, 16 * NG * (a + 1))
                    if not at_first(a):
                        dve.wait_ge(s_stb, 16 * a)
                dve.wait_ge(s_ht, NG * a + g + 1)
                nc.vector.tensor_tensor(t[:, at, :], turn_h[:, :, :], xin[:, at, :], ALU.add).then_inc(s_add, 1)
                dve.wait_ge(s_add, NG * a + g + 1)
                for k in range(GT):
                    nc.vector.bn_stats(st[:, k, :], t[:, GT * g + k, :])
                dve.drain()
                for k in range(GT):
                    nc.vector.bn_aggr(mv[:, GT * g + k, :], st[:, k:k + 1, :])
                dve.drain()
                nc.vector.tensor_scalar(stat["v12"][:, at], mv[:, at, 1], 1.0 + EPS, EPS * EPS, ALU.mult, ALU.add)
                nc.vector.tensor_scalar(stat["v1"][:, at], mv[:, at, 1], EPS, None, ALU.add).then_inc(s_ln, 1)

            def norm_group(a, g):
                at = slice(GT * g, GT * g + GT)
                dve.wait_ge(s_pow, 2 * (NG * a + g) + 1)
                if g >= 2 or not at_first(a):
                    dve.wait_ge(s_xt, NG * a + g - 1)
                for k in range(GT):
                    n = GT * g + k
                    mn = nc.vector.tensor_scalar(xn[g % 2][:, k, :], t[:, n, :], mv[:, n, 0:1], stat["r"][:, n:n + 1],
                                                 ALU.subtract, ALU.mult)
                mn.then_inc(s_xn, 1)
                dve.wait_ge(s_pow, 2 * (NG * a + g) + 2)
                nc.vector.tensor_scalar(stat["rb"][:, at], stat["r1"][:, at], 1.0, None, ALU.add)
                nc.vector.scalar_tensor_tensor(out=stat["shb"][:, at], in0=mv[:, at, 0], scalar=-1.0, in1=stat["r1"][:, at],
                                               op0=ALU.mult, op1=ALU.mult).then_inc(s_rb, 1)

            def finish_group(a, q, g):
                dve.wait_ge(s_xnT, NG * a + g + 1)
                if g == 0 and not at_first(a):
                    dve.wait_ge(s_mset, MSET * a - 2)
                cols = slice(512 * g, 512 * g + 512)
                lms = slice(512 // SEG * g, 512 // SEG * (g + 1))
                nc.vector.tensor_reduce(xm[:, lms], xnT[q][:, cols].rearrange("c (l k) -> c l k", k=SEG), AX.X, ALU.add).then_inc(s_xm, 1)
                nc.vector.tensor_copy(xn_lp[:, cols], xnT[q][:, cols]).then_inc(s_xr, 1)
                dve.wait_ge(s_sc, NG * a + g + 1)
                tg = t[:, GT * g:GT * g + GT, :]
                nc.vector.tensor_tensor(tg, tg, bout[:, :].unsqueeze(1).broadcast_to([P, GT, C]), ALU.add).then_inc(s_base, 1)

            def make_ready(a, q):
                steps = 0

                def step(ins):
                    nonlocal steps
                    steps += 1
                    ins.then_inc(s_set, 1)

                def after(k):
                    dve.wait_ge(s_set, SET * a + k)

                for g in range(NG + 2):
                    if g < NG:
                        add_group(a, g)
                    if 1 <= g <= NG:
                        norm_group(a, g - 1)
                    if g >= 2:
                        finish_group(a, q, g - 2)
                dve.wait_ge(s_mset, MSET * a + 1)
                step(nc.vector.tensor_scalar(ql[:, :], misc[:, 0:LM], DH ** -0.5 / SEG, None, ALU.mult))
                step(nc.vector.tensor_scalar(kl[:, :], misc[:, LM:2 * LM], 1.0 / SEG, None, ALU.mult))
                after(2)
                step(nc.vector.tensor_scalar(R.k_lm[:, bass.ds(a, 1), :], kl[:, :].unsqueeze(1), 1.0, None, ALU.mult))
                step(nc.vector.tensor_tensor(qbd[:, :].rearrange("c (h l) -> c h l", l=LM), R.head_mask[:, :, :],
                                             ql[:, :].unsqueeze(1).broadcast_to([C, HEADS, LM]), ALU.mult))
                dve.wait_ge(s_wsc, a + 1)
                dve.wait_ge(s_xr, NG * (a + 1))
                step(nc.vector.tensor_copy(ws_lp[:, :], ws[q][:, :]))
                scores = misc[:, P:P + PAIRS_H * LM].rearrange("p (g l) -> p g l", l=LM)
                dve.wait_ge(s_mset, MSET * a + 2)
                step(nc.vector.tensor_reduce(mx2[:, :], scores, AX.X, ALU.max))
                after(6)
                step(nc.vector.tensor_tensor(e2[:, :, :], scores, mx2[:, :].unsqueeze(2).broadcast_to([P, PAIRS_H, LM]), ALU.subtract))
                for j in range(NL):
                    c, g = j // PAIRS_H, j % PAIRS_H
                    dve.wait_ge(s_lp, NL * a + j + 1)
                    nc.vector.tensor_reduce(m3p[:, g, c:c + 1], L[(j + 1) % 2][:, :], AX.X, ALU.max).then_inc(s_mx, 1)
                dve.wait_ge(s_mx, NL * (a + 1))
                step(nc.vector.tensor_reduce(m3[:, :], m3p[:, :, :], AX.X, ALU.max))
                dve.wait_ge(s_mset, MSET * a + 3)
                step(nc.vector.tensor_tensor(m3row[q][:, :, :], misc[0:PAIRS_H, 384:512].unsqueeze(1).broadcast_to([PAIRS_H, PAIRS_H, P]),
                                             neg4[:, :, :], ALU.mult))
                dve.wait_ge(s_e2, a + 1)
                step(nc.vector.tensor_reduce(sum2[:, :], e2x[:, :, :], AX.X, ALU.add))
                after(10)
                step(nc.vector.reciprocal(rec2[:, :], sum2[:, :]))
                after(11)
                step(nc.vector.tensor_tensor(R.attn2[:, bass.ds(a, 1), :, :].rearrange("p a g l -> p (a g) l"), e2x[:, :, :],
                                             rec2[:, :].unsqueeze(2).broadcast_to([P, PAIRS_H, LM]), ALU.mult))
                assert steps == SET

            def context(b):
                dve.wait_ge(s_pv, pv_done(b, NT - 1))
                nc.vector.tensor_copy(pvs[:, :], pv[:, 0:P]).then_inc(s_tail, 1)
                dve.wait_ge(s_mtail, 2 * b + 2)
                nc.vector.reciprocal(den[:, :], misc[:, 0:PAIRS_H]).then_inc(s_tail, 1)
                dve.wait_ge(s_tail, TAIL * b + 2)
                for h in range(2):
                    rows = slice(LM * h, LM * h + LM)
                    src = misc[rows, P:2 * P].rearrange("p (g h d) -> p g h d", g=PAIRS_H, h=2)[:, :, h, :]
                    nc.vector.tensor_tensor(R.ctx[rows, bass.ds(b, 1), :, :].rearrange("p a g d -> p (a g) d"), src,
                                            den[rows, :].unsqueeze(2).broadcast_to([LM, PAIRS_H, DH]), ALU.mult).then_inc(s_tail, 1)

            def body(b, q, first, last):
                if not first:
                    context(b - 1)
                if not last:
                    make_ready(b + 1, 1 - q)
            make_ready(0, 0)
            each_image(dve, body)
            context(B - 1)


PINV_ITERS = 6
NP = B * PAIRS_H
PCH = 8
NCH = NP // PCH


def pinv_phase(nc, sems, R):
    with ExitStack() as ctx:
        m = Memory(nc, ctx)
        xT = m.sb("i_xT", [P, NP, LM])
        pz = m.sb("i_pz", [P, NP, 2, LM])
        tm = m.sb("i_tm", [P, NP, LM])
        eye = {k: m.sb(f"i_eye{n}", [P, LM]) for n, k in enumerate((1.0, 7.0, 15.0, 3.25))}
        halves = m.sb("i_halves", [P, P])
        rsum = m.sb("i_rsum", [P, NP])
        cmax = m.sb("i_cmax", [P, NCH])
        top = m.sb("i_top", [P, 2])
        tops = m.sb("i_tops", [P, 2])
        prod = m.sb("i_prod", [P, 1])
        inv = m.sb("i_inv", [P, 1])
        bank = [m.ps(f"i_bank{k}", [P, PCH, LM]) for k in range(4)]
        wide = [[m.ps(f"i_wide{k}{h}", [P, PCH // 2, 2, LM]) for h in range(2)] for k in range(2)]

        s_const = sems.sem("i_const")
        s_norm = sems.sem("i_norm")
        s_col = sems.sem("i_col")
        s_all = sems.sem("i_all")
        s_x = sems.sem("i_x")
        s_xc = sems.sem("i_xc")
        s_q = sems.sem("i_q")
        s_t = sems.sem("i_t")
        s_pz = sems.sem("i_pz")
        s_new = sems.sem("i_new")
        s_pass = sems.sem("i_pass")
        s_z = sems.sem("i_z")

        block = ctx.enter_context(nc.Block())

        def flat(ap):
            return ap.rearrange("p a l -> p (a l)")

        x = R.attn2[:, :, :, :].rearrange("p b g l -> p (b g) l")
        c3 = R.ctx[:, :, :, :].rearrange("p b g d -> p (b g) d")
        chunk = [slice(PCH * c, PCH * c + PCH) for c in range(NCH)]
        HEAD = [slice(0, LM), slice(LM, 2 * LM)]

        @block.gpsimd
        def _(pool):
            pool.memset(halves[:, :], 0.0).then_inc(s_const, 1)
            pool.wait_ge(s_const, 1)
            for h in HEAD:
                pool.memset(halves[h, h], 1.0).then_inc(s_const, 1)
            pool.wait_ge(s_norm, 7)
            pool.partition_all_reduce(tops[:, :], top[:, :], P, RMAX).then_inc(s_all, 1)

        @block.tensor
        def _(pe):
            pe.wait_ge(s_const, 3)
            for c in range(NCH):
                if c >= 4:
                    pe.wait_ge(s_col, c - 3)
                nc.tensor.matmul(flat(bank[c % 4][:, :, :]), halves[:, :], flat(x[:, chunk[c], :]), start=True, stop=True).then_inc(s_x, 1)
            pe.wait_ge(s_norm, 4)
            for c in range(NCH):
                if c < 4:
                    pe.wait_ge(s_col, NCH + c - 3)
                else:
                    pe.wait_ge(s_xc, c - 3)
                for j in range(PCH):
                    for h in HEAD:
                        mt = nc.tensor.matmul(bank[c % 4][h, j, :], x[h, PCH * c + j, :], eye[1.0][h, :], start=True, stop=True)
                mt.then_inc(s_x, 1)
            for c in range(NCH):
                pe.wait_ge(s_xc, NCH + c - 3)
                pe.wait_ge(s_xc, c + 1)
                for j in range(PCH):
                    for h in HEAD:
                        xt = xT[h, PCH * c + j, :]
                        mt = nc.tensor.matmul(bank[c % 4][h, j, :], xt, xt, start=True, stop=True)
                mt.then_inc(s_x, 1)

            def iteration(k):
                for stage in range(2):
                    for c in range(NCH):
                        at = 3 * NCH * k + NCH * stage
                        pe.wait_ge(s_t, at + NCH + c - 3 if c >= 4 else at + c + 1 + 4 * stage)
                        pe.sem_inc(s_pass, 1)
                        for j in range(PCH):
                            for h in HEAD:
                                n = PCH * c + j
                                mt = nc.tensor.matmul(bank[c % 4][h, j, :], pz[h, n, 0, :], tm[h, n, :], start=True, stop=True)
                        mt.then_inc(s_q, 1)
                for c in range(NCH):
                    pe.wait_ge(s_t, 3 * NCH * k + 2 * NCH + c + 1)
                    pe.sem_inc(s_pass, 1)
                    pe.wait_ge(s_new, NCH * (k + 1) + c + 1)
                    pe.sem_inc(s_pass, 1)
                    for j in range(PCH):
                        for h in HEAD:
                            n = PCH * c + j
                            out = wide[c % 2][j // 4][h, j % 4, :, :].rearrange("p a l -> p (a l)")
                            mt = nc.tensor.matmul(out, tm[h, n, :], pz[h, n, :, :].rearrange("p a l -> p (a l)"),
                                                  start=True, stop=True)
                    mt.then_inc(s_pz, 1)
            pe.wait_ge(s_xc, 2 * NCH)
            with pe.Fori(0, PINV_ITERS) as k:
                iteration(k)
            pe.wait_ge(s_new, 2 + NCH * (PINV_ITERS + 1))
            for n in range(NP):
                for h in HEAD:
                    out = bank[n // 32][h, n % 32 // 4, DH * (n % 4):DH * (n % 4) + DH]
                    mt = nc.tensor.matmul(out, pz[h, n, 1, :], c3[h, n, :], start=True, stop=True)
            mt.then_inc(s_z, 1)

        @block.scalar
        def _(act):
            act.sem_inc(s_new, 2)
            for c in range(NCH):
                act.wait_ge(s_x, NCH + c + 1)
                nc.scalar.activation(xT[:, chunk[c], :], bank[c % 4][:, :, :], ACT.Identity).then_inc(s_xc, 1)
            act.wait_ge(s_norm, 9)
            for c in range(NCH):
                act.wait_ge(s_x, 2 * NCH + c + 1)
                nc.scalar.activation(pz[:, chunk[c], 0, :], bank[c % 4][:, :, :], ACT.Identity, scale=inv[:, 0:1]).then_inc(s_xc, 1)
                nc.scalar.activation(pz[:, chunk[c], 1, :], x[:, chunk[c], :], ACT.Identity, scale=inv[:, 0:1]).then_inc(s_new, 1)

            with act.Fori(0, PINV_ITERS) as k:
                for c in range(NCH):
                    act.wait_ge(s_pz, NCH * k + c + 1)
                    for h in range(2):
                        lo = PCH * c + 4 * h
                        mc = nc.scalar.activation(pz[:, lo:lo + 4, :, :], wide[c % 2][h][:, :, :, :], ACT.Identity)
                    mc.then_inc(s_new, 1)

        @block.vector
        def _(dve):
            steps = 0

            def step(ins):
                nonlocal steps
                steps += 1
                ins.then_inc(s_norm, 1)
                dve.wait_ge(s_norm, steps)
            step(nc.vector.tensor_tensor(eye[1.0][:, :], R.ident[:, 0:LM], R.ident[:, LM:2 * LM], ALU.add))
            for k in (7.0, 15.0, 3.25):
                step(nc.vector.tensor_scalar(eye[k][:, :], eye[1.0][:, :], k, None, ALU.mult))
            step(nc.vector.tensor_reduce(rsum[:, :], x, AX.X, ALU.add))
            step(nc.vector.tensor_reduce(top[:, 0:1], rsum[:, :], AX.X, ALU.max))
            for c in range(NCH):
                dve.wait_ge(s_x, c + 1)
                nc.vector.tensor_reduce(cmax[:, c:c + 1], flat(bank[c % 4][:, :, :]), AX.X, ALU.max).then_inc(s_col, 1)
            dve.wait_ge(s_col, NCH)
            step(nc.vector.tensor_reduce(top[:, 1:2], cmax[:, :], AX.X, ALU.max))
            dve.wait_ge(s_all, 1)
            step(nc.vector.tensor_tensor(prod[:, :], tops[:, 0:1], tops[:, 1:2], ALU.mult))
            step(nc.vector.reciprocal(inv[:, :], prod[:, :]))

            def both(k):
                return eye[k][:, :].unsqueeze(1).broadcast_to([P, PCH, LM])

            with dve.Fori(0, PINV_ITERS) as k:
                for c in range(NCH):
                    dve.wait_ge(s_new, 2 + NCH * k + c + 1)
                    nc.vector.tensor_tensor(tm[:, chunk[c], :], both(7.0), pz[:, chunk[c], 0, :], ALU.subtract).then_inc(s_t, 1)
                for c in range(NCH):
                    dve.wait_ge(s_q, 2 * NCH * k + c + 1)
                    nc.vector.tensor_tensor(tm[:, chunk[c], :], both(15.0), bank[c % 4][:, :, :], ALU.subtract).then_inc(s_t, 1)
                for c in range(NCH):
                    dve.wait_ge(s_q, 2 * NCH * k + NCH + c + 1)
                    nc.vector.scalar_tensor_tensor(out=tm[:, chunk[c], :], in0=bank[c % 4][:, :, :], scalar=-0.25,
                                                   in1=both(3.25), op0=ALU.mult, op1=ALU.add).then_inc(s_t, 1)
            dve.wait_ge(s_z, 1)
            for q in range(2):
                nc.vector.tensor_copy(c3[:, 32 * q:32 * q + 32, :].rearrange("p n d -> p (n d)"),
                                      flat(bank[q][:, :, :])).then_inc(s_z, 1)


TAPS = 33
EDGE = 32
BAND = P + 2 * EDGE


def output_phase(nc, sems, R, xnt, base, vals, band, taps, wqkv, w_out, ffn_wT, t2, wx, wx_stats):
    with ExitStack() as ctx:
        m = Memory(nc, ctx)
        w = m.sb("o_wq", [C, C])
        wT = m.sb("o_wqT", [C, C])
        wo = m.sb("o_wo", [C, C])
        fw = m.sb("o_fw", [C, C])
        bands = m.sb("o_bands", [P, HEADS, BAND])
        v = m.sb("o_v", [P, NT, C])
        res = m.sb("o_res", [P, NT, C])
        xnT = [m.sb(f"o_xnT{k}", [C, 512]) for k in range(4)]
        bs = [m.sb(f"o_base{k}", [P, GT, C]) for k in range(4)]
        kbd = m.sb("o_kbd", [C, HEADS * LM])
        wk = m.sb("o_wk", [C, HEADS * LM])
        wk_lp = m.sb("o_wk_lp", [C, HEADS * LM], BF16)
        zb = m.sb("o_zb", [P, PAIRS_H, 2 * DH])
        onesb = m.sb("o_onesb", [P, 2 * DH])
        ind = m.sb("o_ind", [HEADS, HEADS, LM], BF16)
        xn_lp = m.sb("o_xn_lp", [C, 512], BF16)
        m1 = m.sb("o_m1", [P, GT, HEADS])
        negm = [m.sb(f"o_negm{k}", [HEADS, 512], BF16) for k in range(2)]
        p1 = [m.sb(f"o_p1{k}", [P, 512]) for k in range(4)]
        rden = m.sb("o_rden", [C, 512])
        att = m.sb("o_att", [C, 512])
        oT = m.sb("o_oT", [C, 512])
        t2s = [m.sb(f"o_t2{k}", [P, GT, C]) for k in range(2)]
        z = m.sb("o_z", [P, GT, C])
        zT = m.sb("o_zT", [C, 512])
        wxs = [m.sb(f"o_wx{k}", [C, 512]) for k in range(2)]
        st = m.sb("o_st", [P, GT, 6])
        fst = m.sb("o_fst", [C, NG, 6])
        half = m.sb("o_half", [P, GT])
        eps = m.sb("o_eps", [P, GT])
        mv = m.sb("o_mv", [P, GT, 2])
        vare = m.sb("o_vare", [P, GT])
        r = m.sb("o_r", [P, GT])
        bank_q = m.ps("o_bank_q", [C, 512])
        bank_l = [m.ps(f"o_bank_l{k}", [P, 512]) for k in range(2)]
        bank_s = [m.ps(f"o_bank_s{k}", [P, 512]) for k in range(2)]
        bank_pv = m.ps("o_bank_pv", [C, 512])
        bank_den = m.ps("o_bank_den", [C, 512])
        bank_m = m.ps("o_bank_m", [P, GT, P])

        names = """w const ones v conv convc setup turnw copyw wkm wk xr lp max mt neg s1 exp pv ct rec add wo res
                   z bn pow zt ztc wxm wxc fst stats""".split()
        s = {n: sems.sem("o_" + n) for n in names}
        credit = dict(convc=0, neg=1, max=2, exp=4, pv=4, rec=2, wo=1, s1=8, lp=1, mt=1, zt=1, wxm=1, fst=2,
                      ct=1, ztc=1, wxc=2, add=1, bn=1)
        s_band = sems.sem("o_band")
        s_xl = [sems.sem(f"o_xl{k}") for k in range(4)]
        s_bl = [sems.sem(f"o_bl{k}") for k in range(4)]
        s_t2 = [sems.sem(f"o_t2st{k}") for k in range(2)]
        s_wx = [sems.sem(f"o_wxst{k}") for k in range(2)]
        SETUP = 4

        def nth(b, c):
            return NG * b + c + 1

        def start_counts(eng, *names):
            for n in names:
                eng.sem_inc(s[n], credit[n])

        def wait(eng, name, count):
            eng.wait_ge(s[name], credit.get(name, 0) + count)

        block = ctx.enter_context(nc.Block())

        @block.sync
        def _(sp):
            for q in range(2):
                sp.sem_inc(s_t2[q], 16)
                sp.sem_inc(s_wx[q], 16)
            for dst, src in ((w[:, :], wqkv[:, 0:C]), (wo[:, :], w_out), (fw[:, :], ffn_wT)):
                sp.dma_start(dst, src).then_inc(s["w"], 16)
            sp.wait_ge(s["const"], 1)
            sp.dma_start(band.rearrange("h p c -> p h c"), bands[:, :, :]).then_inc(s_band, 16)
            sp.wait_ge(s_band, 16)
            for h in range(HEADS):
                diagonals = bass.AP(tensor=band.tensor, offset=band.offset + h * P * BAND + EDGE - TAPS // 2,
                                    ap=[[BAND + 1, P], [1, TAPS]])
                sp.dma_start(diagonals, taps[h:h + 1, :].broadcast_to([P, TAPS])).then_inc(s_band, 16)
            sp.wait_ge(s_band, 16 * (HEADS + 1))
            sp.dma_start(bands[:, :, :], band.rearrange("h p c -> p h c")).then_inc(s_band, 16)

            def load_v(b):
                for g in range(NG):
                    sp.dma_start(v[:, GT * g:GT * g + GT, :], vals[b, 512 * g:512 * g + 512, :].rearrange("(n p) c -> p n c", p=P)
                                 ).then_inc(s["v"], 16)

            def load_chunk(b, c):
                sp.dma_start(xnT[c % 4][:, :], xnt[b, :, 512 * c:512 * c + 512]).then_inc(s_xl[c % 4], 16)
                sp.dma_start(bs[c % 4][:, :, :], base[b, 512 * c:512 * c + 512, :].rearrange("(n p) c -> p n c", p=P)
                             ).then_inc(s_bl[c % 4], 16)

            def stores(b, c):
                sp.wait_ge(s["res"], nth(b, c))
                sp.dma_start(t2[b, 512 * c:512 * c + 512, :].rearrange("(n p) c -> p n c", p=P), t2s[c % 2][:, :, :]
                             ).then_inc(s_t2[c % 2], 16)
                wait(sp, "wxc", nth(b, c))
                sp.dma_start(wx[b, :, 512 * c:512 * c + 512], wxs[c % 2][:, :]).then_inc(s_wx[c % 2], 16)

            def image(b, more):
                for c in range(NG):
                    if c == 1 and more:
                        sp.wait_ge(s["conv"], HEADS * (b + 1))
                        load_v(b + 1)
                    stores(b, c)
                    if c < NG - 4:
                        load_chunk(b, c + 4)
                    elif more:
                        load_chunk(b + 1, c - 4)
            load_v(0)
            for c in range(4):
                load_chunk(0, c)
            with sp.Fori(0, B - 1) as b:
                image(b, True)
            image(B - 1, False)
            for q in range(2):
                sp.wait_ge(s_t2[q], 16 * (1 + B * NG // 2))
                sp.wait_ge(s_wx[q], 16 * (1 + B * NG // 2))

        @block.gpsimd
        def _(pool):
            pool.memset(bands[:, :, :], 0.0).then_inc(s["const"], 1)
            pool.memset(zb[:, :, :], 0.0).then_inc(s["ones"], 1)
            pool.memset(onesb[:, :], 0.0).then_inc(s["ones"], 1)
            pool.memset(half[:, :], -0.5).then_inc(s["ones"], 1)
            pool.memset(eps[:, :], EPS).then_inc(s["ones"], 1)
            pool.memset(ind[:, :, :], 0.0).then_inc(s["ones"], 1)
            pool.wait_ge(s["ones"], 5)
            for h in range(2):
                pool.memset(onesb[LM * h:LM * h + LM, DH * h:DH * h + DH], 1.0).then_inc(s["ones"], 1)
            pool.affine_select(out=ind[:, :, :], in_=ind[:, :, :], compare_op=ALU.not_equal, fill=1.0, base=0,
                               pattern=[[-1, HEADS], [0, LM]], channel_multiplier=1).then_inc(s["ones"], 1)

            def image(b):
                for c in range(NG):
                    wait(pool, "bn", nth(b, c))
                    pool.tensor_tensor(vare[:, :], mv[:, :, 1], eps[:, :], ALU.add).then_inc(s["pow"], 1)
                    pool.wait_ge(s["pow"], 2 * nth(b, c) - 1)
                    pool.tensor_tensor(r[:, :], vare[:, :], half[:, :], ALU.pow).then_inc(s["pow"], 1)
            with pool.Fori(0, B) as b:
                image(b)

        @block.tensor
        def _(pe):
            start_counts(pe, "pv", "wo", "s1", "lp", "mt", "zt", "wxm", "ct")
            pe.wait_ge(s["w"], 48)
            pe.wait_ge(s["ones"], 8)
            pe.wait_ge(s_band, 16 * (HEADS + 2))
            nc.tensor.transpose(bank_q[:, 0:C], w[:, :], R.ident[:, :]).then_inc(s["turnw"], 1)
            pe.wait_ge(s["copyw"], 1)

            def weights(b):
                pe.wait_ge(s["setup"], SETUP * b + 1)
                wait(pe, "wxc", NG * b - 1)
                nc.tensor.matmul(bank_q[:, :], wT[:, :], kbd[:, :], start=True, stop=True).then_inc(s["wkm"], 1)

            def convolve(b, first):
                pe.wait_ge(s["v"], 16 * NG * (b + 1))
                for h in range(HEADS):
                    ch = slice(DH * h, DH * h + DH)
                    out = bank_l[h % 2]
                    if h < 2:
                        wait(pe, ("neg", "max")[h], (NG * b, NT * b)[h])
                    else:
                        wait(pe, "convc", HEADS * b + h - 1)
                    nc.tensor.matmul(out[:, :], bands[:, h, EDGE:EDGE + P], v[:, :, ch], start=True, stop=False,
                                     skip_group_check=True)
                    nc.tensor.matmul(out[P - EDGE:P, 0:(NT - 1) * DH], bands[:, h, 0:EDGE], v[:, 1:NT, ch],
                                     start=False, stop=False, skip_group_check=True)
                    nc.tensor.matmul(out[0:EDGE, DH:NT * DH], bands[:, h, EDGE + P:BAND], v[:, 0:NT - 1, ch],
                                     start=False, stop=True, skip_group_check=True).then_inc(s["conv"], 1)
                    if h == 1 and not first:
                        project(b, -1)
                    if h == 2:
                        weights(b)
                    if h == 5 and not first:
                        turn_normed(b, -1)
                if not first:
                    ffn(b, -1)

            def row_maxima(b, c, k):
                if k == 0:
                    wait(pe, "xr", nth(b, c))
                    wait(pe, "neg", nth(b, c) - 1)
                wait(pe, "max", GT * (NG * b + c) + k - 1)
                nc.tensor.matmul(bank_l[k % 2][:, :], xn_lp[:, P * k:P * k + P], wk_lp[:, :], start=True, stop=True
                                 ).then_inc(s["lp"], 1)

            def turn_maxima(b, c):
                wait(pe, "max", GT * nth(b, c))
                for k in range(GT):
                    mt = nc.tensor.transpose(bank_l[0][0:HEADS, P * k:P * k + P], m1[:, k, :], R.ident[:, :])
                mt.then_inc(s["mt"], 1)

            def attend(b, c):
                wait(pe, "neg", nth(b, c))
                for g in range(PAIRS_H + 1):
                    i = PAIRS_H * (NG * b + c) + g
                    if g < PAIRS_H:
                        wait(pe, "exp", i - 1)
                        nc.tensor.matmul(bank_s[g % 2][:, :], wk[:, P * g:P * g + P], xnT[c % 4][:, :], start=True, stop=False)
                        nc.tensor.matmul(bank_s[g % 2][:, :], ind[:, 2 * g:2 * g + 2, :].rearrange("h a l -> h (a l)"),
                                         negm[c % 2][:, :], start=False, stop=True).then_inc(s["s1"], 1)
                    if g == 1 and c:
                        project(b, c - 1)
                    if g:
                        h = g - 1
                        wait(pe, "exp", i)
                        if h == 0:
                            wait(pe, "rec", 2 * (NG * b + c))
                        rows = slice(2 * DH * h, 2 * DH * h + 2 * DH)
                        nc.tensor.matmul(bank_pv[rows, :], zb[:, h, :], p1[h][:, :], start=True, stop=True)
                        nc.tensor.matmul(bank_den[rows, :], onesb[:, :], p1[h][:, :], start=True, stop=True).then_inc(s["pv"], 1)
                    if c + 1 < NG and g >= 2:
                        row_maxima(b, c + 1, g - 2)
                if c + 1 < NG:
                    row_maxima(b, c + 1, GT - 1)

            def turn_normed(b, c):
                wait(pe, "z", nth(b, c))
                for k in range(GT):
                    mt = nc.tensor.transpose(bank_m[:, k, :], z[:, k, :], R.ident[:, :])
                mt.then_inc(s["zt"], 1)

            def turn_convolved(b, c):
                wait(pe, "convc", HEADS * (b + 1))
                wait(pe, "ztc", NG * b + c)
                for k in range(GT):
                    mt = nc.tensor.transpose(bank_m[:, k, :], res[:, GT * c + k, :], R.ident[:, :])
                mt.then_inc(s["ct"], 1)

            def project(b, c):
                wait(pe, "add", nth(b, c))
                for k in range(GT):
                    mt = nc.tensor.matmul(bank_m[:, k, :], oT[:, P * k:P * k + P], wo[:, :], start=True, stop=True)
                mt.then_inc(s["wo"], 1)

            def ffn(b, c):
                wait(pe, "ztc", nth(b, c))
                if c == -1:
                    pe.wait_ge(s["wk"], b + 1)
                else:
                    wait(pe, "wxc", nth(b, c) - 1)
                nc.tensor.matmul(bank_q[:, :], fw[:, :], zT[:, :], start=True, stop=True).then_inc(s["wxm"], 1)

            def image(b, first):
                convolve(b, first)
                pe.wait_ge(s["setup"], SETUP * (b + 1))
                wait(pe, "convc", HEADS * (b + 1))
                for k in range(GT):
                    row_maxima(b, 0, k)
                turn_maxima(b, 0)
                for c in range(NG):
                    attend(b, c)
                    if c:
                        turn_normed(b, c - 1)
                    turn_convolved(b, c)
                    if c + 1 < NG:
                        turn_maxima(b, c + 1)
                    if c:
                        ffn(b, c - 1)
            image(0, True)
            with pe.Fori(1, B) as b:
                image(b, False)
            project(B - 1, NG - 1)
            turn_normed(B - 1, NG - 1)
            ffn(B - 1, NG - 1)

        @block.scalar
        def _(act):
            start_counts(act, "neg", "exp", "ztc", "wxc")

            act.wait_ge(s["turnw"], 1)
            nc.scalar.activation(wT[:, :], bank_q[:, 0:C], ACT.Copy).then_inc(s["copyw"], 1)

            def negate(b, c):
                wait(act, "mt", nth(b, c))
                nc.scalar.activation(negm[c % 2][:, :], bank_l[0][0:HEADS, :], ACT.Copy, scale=-1.0).then_inc(s["neg"], 1)

            def copy_normed(b, c):
                wait(act, "zt", nth(b, c))
                wait(act, "wxm", nth(b, c) - 1)
                nc.scalar.activation(zT[:, :], bank_m[:, :, :].rearrange("c k t -> c (k t)"), ACT.Copy).then_inc(s["ztc"], 1)

            def copy_wx(b, c):
                q = c % 2
                wait(act, "wxm", nth(b, c))
                wait(act, "fst", nth(b, c) - 2)
                act.wait_ge(s_wx[q], 16 + 16 * (NG // 2 * b + c // 2))
                nc.scalar.activation(wxs[q][:, :], bank_q[:, :], ACT.Copy).then_inc(s["wxc"], 1)

            def image(b, first):
                wait(act, "ct", NG * b)
                for h in range(HEADS):
                    wait(act, "conv", HEADS * b + h + 1)
                    nc.scalar.activation(res[:, :, DH * h:DH * h + DH], bank_l[h % 2][:, :].rearrange("p (n d) -> p n d", d=DH),
                                         ACT.Copy).then_inc(s["convc"], 1)
                    if h == 2:
                        act.wait_ge(s["wkm"], b + 1)
                        nc.scalar.activation(wk[:, :], bank_q[:, :], ACT.Copy, scale=DH ** -0.5).then_inc(s["wk"], 1)
                    if h == 5 and not first:
                        copy_normed(b, -1)
                if not first:
                    copy_wx(b, -1)
                negate(b, 0)
                for c in range(NG):
                    for g in range(PAIRS_H):
                        i = PAIRS_H * (NG * b + c) + g
                        wait(act, "s1", i + 1)
                        wait(act, "pv", i - 3)
                        nc.scalar.activation(p1[g][:, :], bank_s[g % 2][:, :], ACT.Exp).then_inc(s["exp"], 1)
                    if c:
                        copy_normed(b, c - 1)
                    if c + 1 < NG:
                        negate(b, c + 1)
                    if c:
                        copy_wx(b, c - 1)
            image(0, True)
            with act.Fori(1, B) as b:
                image(b, False)
            copy_normed(B - 1, NG - 1)
            copy_wx(B - 1, NG - 1)

        @block.vector
        def _(dve):
            start_counts(dve, "max", "rec", "fst", "add", "bn")
            dve.wait_ge(s["ones"], 8)

            def set_up(b, first):
                wait(dve, "pv", NT * b)
                nc.vector.tensor_tensor(kbd[:, :].rearrange("c (h l) -> c h l", l=LM), R.head_mask[:, :, :],
                                        R.k_lm[:, bass.ds(b, 1), :].broadcast_to([C, HEADS, LM]), ALU.mult).then_inc(s["setup"], 1)
                for h in range(2):
                    rows = slice(LM * h, LM * h + LM)
                    nc.vector.tensor_scalar(zb[rows, :, DH * h:DH * h + DH], R.ctx[rows, bass.ds(b, 1), :, :].rearrange("p a g d -> p (a g) d"),
                                            1.0, None, ALU.mult).then_inc(s["setup"], 1)
                if not first:
                    residual(b, -1)
                dve.wait_ge(s["wk"], b + 1)
                nc.vector.tensor_copy(wk_lp[:, :], wk[:, :]).then_inc(s["setup"], 1)

            def round_tokens(b, c):
                dve.wait_ge(s_xl[c % 4], 16 * (2 * b + c // 4 + 1))
                wait(dve, "lp", GT * (NG * b + c))
                nc.vector.tensor_copy(xn_lp[:, :], xnT[c % 4][:, :]).then_inc(s["xr"], 1)

            def maxima(b, c, tiles):
                wait(dve, "mt", NG * b + c)
                for k in tiles:
                    wait(dve, "lp", GT * (NG * b + c) + k + 1)
                    nc.vector.tensor_reduce(m1[:, k, :], bank_l[k % 2][:, :].rearrange("p (h l) -> p h l", l=LM), AX.X, ALU.max
                                            ).then_inc(s["max"], 1)

            def residual(b, c):
                out = t2s[c % 2]
                wait(dve, "wo", nth(b, c))
                dve.wait_ge(s_bl[c % 4], 16 * (2 * b + c // 4 + 1))
                dve.wait_ge(s_t2[c % 2], 16 + 16 * (NG // 2 * b + c // 2))
                nc.vector.tensor_tensor(out[:, :, :], bank_m[:, :, :], bs[c % 4][:, :, :], ALU.add).then_inc(s["res"], 1)
                wait(dve, "res", nth(b, c))
                for k in range(GT):
                    nc.vector.bn_stats(st[:, k, :], out[:, k, :])
                dve.drain()
                for k in range(GT):
                    ms = nc.vector.bn_aggr(mv[:, k, :], st[:, k:k + 1, :])
                ms.then_inc(s["bn"], 1)

            def norm(b, c):
                out = t2s[c % 2]
                wait(dve, "bn", nth(b, c))
                wait(dve, "pow", 2 * nth(b, c))
                wait(dve, "zt", nth(b, c) - 1)
                for k in range(GT):
                    mz = nc.vector.tensor_scalar(z[:, k, :], out[:, k, :], mv[:, k, 0:1], r[:, k:k + 1], ALU.subtract, ALU.mult)
                mz.then_inc(s["z"], 1)

            def statistics(b, c):
                wait(dve, "wxc", nth(b, c))
                nc.vector.bn_stats(fst[:, c % NG, :], wxs[c % 2][:, :]).then_inc(s["fst"], 1)
                if c % NG == NG - 1:
                    wait(dve, "fst", nth(b, c))
                    at = b - 1 if c < 0 else b
                    nc.vector.tensor_scalar(wx_stats[:, bass.ds(at, 1), :], fst[:, :, :].rearrange("c k s -> c (k s)").unsqueeze(1),
                                            1.0, None, ALU.mult).then_inc(s["stats"], 1)

            def image(b, first):
                set_up(b, first)
                round_tokens(b, 0)
                if not first:
                    norm(b, -1)
                    statistics(b, -1)
                maxima(b, 0, range(GT))
                for c in range(NG):
                    if c + 1 < NG:
                        round_tokens(b, c + 1)
                    if c:
                        residual(b, c - 1)
                    if c + 1 < NG:
                        maxima(b, c + 1, range(2))
                    if c:
                        norm(b, c - 1)
                    if c + 1 < NG:
                        maxima(b, c + 1, range(2, GT))
                    wait(dve, "pv", PAIRS_H * nth(b, c))
                    nc.vector.reciprocal(rden[:, :], bank_den[:, :]).then_inc(s["rec"], 1)
                    wait(dve, "rec", 2 * (NG * b + c) + 1)
                    wait(dve, "add", nth(b, c) - 1)
                    nc.vector.tensor_tensor(att[:, :], bank_pv[:, :], rden[:, :], ALU.mult).then_inc(s["rec"], 1)
                    wait(dve, "rec", 2 * nth(b, c))
                    wait(dve, "ct", nth(b, c))
                    wait(dve, "wo", nth(b, c) - 1)
                    nc.vector.tensor_tensor(oT[:, :], att[:, :], bank_m[:, :, :].rearrange("c k t -> c (k t)"), ALU.add
                                            ).then_inc(s["add"], 1)
                    if c:
                        if c == 1 and not first:
                            dve.wait_ge(s["stats"], b)
                        statistics(b, c - 1)
            image(0, True)
            with dve.Fori(1, B) as b:
                image(b, False)
            residual(B - 1, NG - 1)
            norm(B - 1, NG - 1)
            statistics(B - 1, NG - 1)


RT = P
RC = 32
CHUNKS = RT // RC
BLOCKS = TOK // RT
PIECES = 4
PT = RC // PIECES
FILL = 256


def recurrence_phase(nc, sems, t2, wx, wx_stats, ffn_v_t, gamma, beta, out):
    with ExitStack() as ctx:
        m = Memory(nc, ctx)
        vT = m.sb("f_vT", [C, C])
        gam = m.sb("f_gamma", [C, 1])
        bet = m.sb("f_beta", [C, 1])
        ident = m.sb("f_ident", [P, P])
        mv = m.sb("f_mv", [C, 2])
        vare = m.sb("f_vare", [C, 1])
        half = m.sb("f_half", [C, 1])
        rstd = m.sb("f_rstd", [C, 1])
        scale = m.sb("f_scale", [C, 1])
        moved = m.sb("f_moved", [C, 1])
        shift = m.sb("f_shift", [C, 1])
        wxb = [m.sb(f"f_wx{q}", [C, B, RT]) for q in range(2)]
        t2b = [m.sb(f"f_t2{q}", [P, B, C]) for q in range(2)]
        y = [m.sb(f"f_y{q}", [C, RT, B]) for q in range(2)]
        sums = [m.sb(f"f_sum{q}", [P, B, C]) for q in range(2)]
        idle = m.sb("f_idle", [C, FILL], BF16)
        acc = [m.ps(f"f_acc{k}", [C, RC, B]) for k in range(2)]
        turned = [m.ps(f"f_turned{k}", [P, 4, C]) for k in range(2)]
        junk = m.ps("f_junk", [C, FILL])

        s_w = sems.sem("f_weights")
        s_const = sems.sem("f_const")
        s_bn = sems.sem("f_bn")
        s_rstd = sems.sem("f_rstd")
        s_wx = [sems.sem(f"f_wx{q}") for q in range(2)]
        s_t2 = [sems.sem(f"f_t2{q}") for q in range(2)]
        s_norm = sems.sem("f_norm")
        s_pre = sems.sem("f_pre")
        s_mm = sems.sem("f_mm")
        s_y = sems.sem("f_y")
        s_turn = sems.sem("f_turn")
        s_sum = sems.sem("f_sum")
        s_out = [sems.sem(f"f_out{q}") for q in range(2)]
        GR = B // 4
        TURN0, SUM0 = 2 * GR, 2

        block = ctx.enter_context(nc.Block())

        def each_pair(eng, body):
            for q in range(2):
                body(q, q, q == 0, False)
            with eng.Fori(1, BLOCKS // 2 - 1) as i:
                for q in range(2):
                    body(2 * i + q, q, False, False)
            for q in range(2):
                body(BLOCKS - 2 + q, q, False, q == 1)

        @block.sync
        def _(sp):
            for dst, src in ((vT[:, :], ffn_v_t), (gam[:, :], gamma.rearrange("(p a) -> p a", a=1)),
                             (bet[:, :], beta.rearrange("(p a) -> p a", a=1))):
                sp.dma_start(dst, src).then_inc(s_w, 16)
            for q in range(2):
                sp.sem_inc(s_out[q], 16 * GR)

            def load_wx(T, q):
                for g in range(GR):
                    sp.dma_start(wxb[q][:, 4 * g:4 * g + 4, :], wx[4 * g:4 * g + 4, :, bass.ds(T * RT, RT)].rearrange("b c t -> c b t")
                                 ).then_inc(s_wx[q], 16)

            def load_t2(T, q):
                for g in range(GR):
                    sp.dma_start(t2b[q][:, 4 * g:4 * g + 4, :], t2[4 * g:4 * g + 4, bass.ds(T * RT, RT), :].rearrange("b p c -> p b c")
                                 ).then_inc(s_t2[q], 16)

            def store(T, q):
                for g in range(GR):
                    sp.wait_ge(s_sum, SUM0 + GR * T + g + 1)
                    sp.dma_start(out[4 * g:4 * g + 4, bass.ds(T * RT, RT), :].rearrange("b p c -> p b c"), sums[q][:, 4 * g:4 * g + 4, :]
                                 ).then_inc(s_out[q], 16)

            def body(T, q, first, last):
                if not first:
                    store(T - 1, 1 - q)
                if not last:
                    load_t2(T + 1, 1 - q)
                if not isinstance(T, int) or T + 2 < BLOCKS:
                    sp.wait_ge(s_pre, CHUNKS * (T + 1))
                    load_wx(T + 2, q)
            load_wx(0, 0)
            load_wx(1, 1)
            load_t2(0, 0)
            each_pair(sp, body)
            store(BLOCKS - 1, 1)
            for q in range(2):
                sp.wait_ge(s_out[q], 16 * GR * (1 + BLOCKS // 2))

        @block.gpsimd
        def _(pool):
            make_identity(pool, ident, s_const)
            pool.memset(half[:, :], -0.5).then_inc(s_const, 1)
            pool.memset(idle[:, :], 0.0).then_inc(s_const, 1)
            pool.wait_ge(s_const, 4)
            pool.wait_ge(s_bn, 2)
            pool.tensor_tensor(rstd[:, :], vare[:, :], half[:, :], ALU.pow).then_inc(s_rstd, 1)

        @block.vector
        def _(dve):
            dve.sem_inc(s_sum, SUM0)
            nc.vector.memset(y[1][:, RT - 1, :], 0.0).then_inc(s_y, 1)
            nc.vector.bn_aggr(mv[:, :], wx_stats[:, :, :].rearrange("c b (k s) -> c (b k) s", s=6)).then_inc(s_bn, 1)
            dve.wait_ge(s_bn, 1)
            nc.vector.tensor_scalar(vare[:, :], mv[:, 1:2], EPS, None, ALU.add).then_inc(s_bn, 1)
            dve.wait_ge(s_w, 48)
            dve.wait_ge(s_rstd, 1)
            nc.vector.tensor_tensor(scale[:, :], rstd[:, :], gam[:, :], ALU.mult).then_inc(s_bn, 1)
            dve.wait_ge(s_bn, 3)
            nc.vector.tensor_tensor(moved[:, :], mv[:, 0:1], scale[:, :], ALU.mult).then_inc(s_bn, 1)
            dve.wait_ge(s_bn, 4)
            nc.vector.tensor_tensor(shift[:, :], bet[:, :], moved[:, :], ALU.subtract).then_inc(s_bn, 1)
            dve.wait_ge(s_bn, 5)

            def normalise(T, q):
                dve.wait_ge(s_wx[q], 16 * GR * (T // 2 + 1) if isinstance(T, int) else 8 * GR * (T - q) + 16 * GR)
                nc.vector.tensor_scalar(wxb[q][:, :, :], wxb[q][:, :, :], scale[:, 0:1], shift[:, 0:1], ALU.mult, ALU.add
                                        ).then_inc(s_norm, 1)

            def add(T, q):
                pair = 8 * GR * (T - q) + 16 * GR
                dve.wait_ge(s_t2[q], pair)
                dve.wait_ge(s_out[q], pair)
                for g in range(GR):
                    dve.wait_ge(s_turn, TURN0 + GR * T + g + 1)
                    at = slice(4 * g, 4 * g + 4)
                    nc.vector.tensor_tensor(sums[q][:, at, :], turned[g % 2][:, :, :], t2b[q][:, at, :], ALU.add).then_inc(s_sum, 1)

            def body(T, q, first, last):
                if not last:
                    normalise(T + 1, 1 - q)
                if not first:
                    add(T - 1, 1 - q)
            normalise(0, 0)
            each_pair(dve, body)
            add(BLOCKS - 1, 1)

        @block.tensor
        def _(pe):
            pe.sem_inc(s_turn, TURN0)
            pe.wait_ge(s_w, 48)
            pe.wait_ge(s_const, 4)

            def lay(T, q, k, piece):
                if piece == 0 and k == 0:
                    pe.wait_ge(s_norm, T + 1)
                at = slice(RC * k + PT * piece, RC * k + PT * piece + PT)
                mm = nc.tensor.matmul(acc[k % 2][:, PT * piece:PT * piece + PT, :], ident[:, :],
                                      wxb[q][:, :, at].rearrange("c b t -> c t b"), start=piece == 0, stop=False,
                                      skip_group_check=True)
                if piece == PIECES - 1:
                    mm.then_inc(s_pre, 1)

            def turn(T, q, b):
                g = b // 4
                if b % 4 == 0:
                    pe.wait_ge(s_sum, GR * T + g + 1)
                mt = nc.tensor.transpose(turned[g % 2][:, b % 4, :], y[q][:, :, b], ident[:, :])
                if b % 4 == 3:
                    mt.then_inc(s_turn, 1)

            def body(T, q, first, last):
                for u in range(RT):
                    k, t = u // RC, u % RC
                    pe.wait_ge(s_y, RT * T + u + 1)
                    before = y[q][:, u - 1, :] if u else y[1 - q][:, RT - 1, :]
                    for g in range(4):
                        rows = slice(32 * g, 32 * g + 32)
                        mm = nc.tensor.matmul(acc[k % 2][rows, t, :], vT[:, rows], before, start=False, stop=True,
                                              skip_group_check=True)
                    mm.then_inc(s_mm, 1)
                    work = 0
                    if t % 2 == 0 and t // 2 < PIECES and not (last and k == CHUNKS - 1):
                        work = 1
                        if k < CHUNKS - 1:
                            lay(T, q, k + 1, t // 2)
                        else:
                            lay(T + 1, 1 - q, 0, t // 2)
                    b = 4 * k + (t - 2 * PIECES) // 4
                    if not first and 2 * PIECES <= t < 2 * PIECES + 16 and t % 4 == 0:
                        work = 1
                        turn(T - 1, 1 - q, b)
                    for _ in range(3 - work):
                        nc.tensor.matmul(junk[:, :], idle[:, 0:P], idle[:, :], start=True, stop=True)

            for piece in range(PIECES):
                lay(0, 0, 0, piece)
            each_pair(pe, body)
            pe.wait_ge(s_y, TOK + 1)
            for b in range(B):
                turn(BLOCKS - 1, 1, b)

        @block.scalar
        def _(act):
            def body(T, q, first, last):
                act.wait_ge(s_turn, GR * T + GR)
                for u in range(RT):
                    act.wait_ge(s_mm, RT * T + u + 1)
                    nc.scalar.activation(y[q][:, u, :], acc[u // RC % 2][:, u % RC, :], ACT.Sigmoid).then_inc(s_y, 1)
            each_pair(act, body)


WEIGHTS = ["wf0", "uf0", "bf0", "wf1", "uf1", "bf1", "wi", "ui", "bi", "wo", "uo", "bo", "wc", "uc", "bc"]


def program(nc, args, out):
    def scratch(name, shape):
        return nc.dram_tensor(name, shape, F32, kind="Internal").ap()

    skew = scratch("skew", (LANES, C, STEPS * G))
    hidden = scratch("hidden", (LANES, C, STEPS * SLOT))
    xnt = scratch("xnt", (B, C, TOK))
    base = scratch("base", (B, TOK, C))
    vals = scratch("vals", (B, TOK, C))
    band = scratch("band", (HEADS, P, BAND))
    t2 = scratch("t2", (B, TOK, C))
    wx = scratch("wx", (B, C, TOK))
    lstm = {n: args["L0_conv_" + n] for n in WEIGHTS}
    attn = {n: args["L1_attn_" + n] for n in ("gamma", "beta", "w_qkv", "w_out", "b_out", "conv_w")}
    with ExitStack() as ctx:
        sems = Memory(nc, ctx)
        group_norm_phase(nc, sems, args["x"], skew)
        lstm_phase(nc, sems, skew, hidden, lstm, lstm)
        wx_stats = sems.sb("wx_stats", [C, B, NG * 6])
        with ExitStack() as attention:
            R = Resident(Memory(nc, attention))
            landmark_phase(nc, sems, R, args["x"], hidden, attn["w_qkv"], attn["gamma"], attn["beta"], attn["b_out"],
                           xnt, base, vals)
            pinv_phase(nc, sems, R)
            output_phase(nc, sems, R, xnt, base, vals, band, attn["conv_w"], attn["w_qkv"], attn["w_out"],
                         args["L1_ffn_W"], t2, wx, wx_stats)
        recurrence_phase(nc, sems, t2, wx, wx_stats, args["L1_ffn_V"], args["L1_ffn_gamma"], args["L1_ffn_beta"], out)


def kernel(**inputs):
    import numpy as np
    import concourse.bacc as bacc
    from concourse.bass_utils import run_bass_kernel_spmd

    nc = bacc.Bacc("TRN2", target_bir_lowering=False, num_devices=1)
    arrays, args = {}, {}
    for name, value in inputs.items():
        a = np.asarray(value)
        if name == "x":
            a = a.reshape(B, TOK, C)
        elif name == "L1_attn_conv_w":
            a = a[:, 0, ::-1, 0]
        elif name in ("L1_ffn_W", "L1_ffn_V"):
            a = a.T
        arrays[f"in_{name}"] = np.ascontiguousarray(a)
        args[name] = nc.dram_tensor(f"in_{name}", a.shape, mybir.dt.from_np(a.dtype), kind="ExternalInput").ap()
    out = nc.dram_tensor("out", (B, TOK, C), F32, kind="ExternalOutput").ap()
    program(nc, args, out)
    r = run_bass_kernel_spmd(nc, [arrays], core_ids=[0])
    return np.asarray(r.results[0]["out"]).reshape(B, G, G, C)
```
